# Optimizing a Trainium2 kernel written in Bass

```python
import numpy as np
import jax
import jax.numpy as jnp

def _softmax(x, axis=-1):
    return jax.nn.softmax(x, axis=axis)

def _gelu(x):
    return jax.nn.gelu(x, approximate=True)

def _silu(x):
    return jax.nn.silu(x)

def _sigmoid(x):
    return jax.nn.sigmoid(x)

def _layernorm(x, axis=-1, eps=1e-05):
    m = jnp.mean(x, axis=axis, keepdims=True)
    v = jnp.var(x, axis=axis, keepdims=True)
    return (x - m) / jnp.sqrt(v + eps)

def _scatter_add(tgt, idx, src, axis=0):
    return tgt.at[idx].add(src)

def _segment_sum(src, seg, n):
    return jax.ops.segment_sum(src, seg, n)
kernel_name = 'mk_gnn_resnorm_d4_gnn_r32_6ed13c'

def setup_inputs(seed: int=0):
    np.random.seed(seed)
    _w = jnp.asarray

    def _rec_inputs():
        import jax
        import jax.numpy as jnp
        _gk = jax.random.key(seed)
        x = -0.0008691 + 1 * jax.random.normal(jax.random.fold_in(_gk, 1), (3125, 128), jnp.float32)
        _s = jax.random.randint(jax.random.fold_in(_gk, 2), (50000,), 0, 3125, jnp.int32)
        _d = jax.random.randint(jax.random.fold_in(_gk, 3), (50000,), 0, 3125, jnp.int32)
        _loop = jnp.arange(3125, dtype=jnp.int32)
        src = jnp.concatenate([_s, _d, _loop])
        dst = jnp.concatenate([_d, _s, _loop])
        _o = jnp.argsort(dst, stable=True)
        src = src[_o]
        dst = dst[_o]
        edge_attr_16 = 0.000196303 + 1.00016 * jax.random.normal(jax.random.fold_in(_gk, 12), (103125, 16), jnp.float32)
        return (x, src, dst, edge_attr_16)
    x, src, dst, edge_attr_16 = _rec_inputs()

    def _L0_gnn_setup():
        import jax, jax.numpy as jnp
        import numpy as np
        N_NODES = 10000
        N_EDGES = 20000
        D_FEAT = 128
        D_OUT = 128
        key = jax.random.key(seed)
        ks = jax.random.split(key, 7)
        feat = jax.random.normal(ks[0], (N_NODES, D_FEAT), dtype=jnp.float32)
        W_src = jax.random.normal(ks[1], (D_FEAT, D_FEAT), dtype=jnp.float32) * (1.0 / np.sqrt(D_FEAT))
        b_src = jax.random.normal(ks[2], (D_FEAT,), dtype=jnp.float32) * 0.01
        W_fc = jax.random.normal(ks[3], (D_OUT, 2 * D_FEAT), dtype=jnp.float32) * (1.0 / np.sqrt(2 * D_FEAT))
        b_fc = jax.random.normal(ks[4], (D_OUT,), dtype=jnp.float32) * 0.01
        src = jax.random.randint(ks[5], (N_EDGES,), 0, N_NODES, dtype=jnp.int32)
        dst = jax.random.randint(ks[6], (N_EDGES,), 0, N_NODES, dtype=jnp.int32)
        return {'feat': feat, 'W_src': W_src, 'b_src': b_src, 'W_fc': W_fc, 'b_fc': b_fc, 'src': src, 'dst': dst}
    _L0_gnn_all = _L0_gnn_setup()
    _L0_gnn_in = {k: v for k, v in _L0_gnn_all.items() if k in ('W_src', 'b_src', 'W_fc', 'b_fc')}
    del _L0_gnn_all

    def _L1_gnn_setup():
        import jax, jax.numpy as jnp
        import numpy as np
        NUM_STEPS = 1

        def _seg_mean(vals, idx, num_nodes):
            s = jax.ops.segment_sum(vals, idx, num_segments=num_nodes)
            cnt = jax.ops.segment_sum(jnp.ones((vals.shape[0],), vals.dtype), idx, num_segments=num_nodes)
            return s / jnp.maximum(cnt, 1.0)[:, None]

        def _gru_cell(a, h, w_ih, w_hh, b_ih, b_hh):
            gi = a @ w_ih.T + b_ih
            gh = h @ w_hh.T + b_hh
            H = h.shape[1]
            i_r, i_z, i_n = (gi[:, :H], gi[:, H:2 * H], gi[:, 2 * H:])
            h_r, h_z, h_n = (gh[:, :H], gh[:, H:2 * H], gh[:, 2 * H:])
            r = jax.nn.sigmoid(i_r + h_r)
            z = jax.nn.sigmoid(i_z + h_z)
            n = jnp.tanh(i_n + r * h_n)
            return (1.0 - z) * n + z * h
        key = jax.random.key(seed)
        ks = jax.random.split(key, 8)
        N, E, H = (3125, 20000, 128)
        sc = 1.0 / np.sqrt(H)
        feat = jax.random.normal(ks[0], (N, H), jnp.float32)
        src = jax.random.randint(ks[1], (E,), 0, N, jnp.int32)
        dst = jax.random.randint(ks[2], (E,), 0, N, jnp.int32)
        W_in = jax.random.normal(ks[3], (H, H), jnp.float32) * sc
        W_out = jax.random.normal(ks[4], (H, H), jnp.float32) * sc
        w_ih = jax.random.normal(ks[5], (3 * H, 2 * H), jnp.float32) * sc
        w_hh = jax.random.normal(ks[6], (3 * H, H), jnp.float32) * sc
        return {'feat': feat, 'src': src, 'dst': dst, 'W_in': W_in, 'b_in': jnp.zeros((H,), jnp.float32), 'W_out': W_out, 'b_out': jnp.zeros((H,), jnp.float32), 'w_ih': w_ih, 'w_hh': w_hh, 'b_ih': jnp.zeros((3 * H,), jnp.float32), 'b_hh': jnp.zeros((3 * H,), jnp.float32)}
    _L1_gnn_all = _L1_gnn_setup()
    _L1_gnn_in = {k: v for k, v in _L1_gnn_all.items() if k in ('W_in', 'b_in', 'W_out', 'b_out', 'w_ih', 'w_hh', 'b_ih', 'b_hh')}
    del _L1_gnn_all

    def _L2_gnn_setup():
        import jax, jax.numpy as jnp
        import numpy as np
        N_NODES = 50000
        N_EDGES = 25000
        C_IN = 128
        C_OUT = 128
        key = jax.random.key(seed)
        k1, k2, k3 = jax.random.split(key, 3)
        x = jax.random.normal(k1, (N_NODES, C_IN), dtype=jnp.float32)
        edge_index = jax.random.randint(k2, (2, N_EDGES), 0, N_NODES, dtype=jnp.int64)
        scale = jnp.sqrt(2.0 / (C_IN + C_OUT)).astype(jnp.float32)
        weight = jax.random.normal(k3, (C_IN, C_OUT), dtype=jnp.float32) * scale
        bias = jnp.zeros((C_OUT,), dtype=jnp.float32)
        return {'x': x, 'edge_index': edge_index, 'weight': weight, 'bias': bias}
    _L2_gnn_all = _L2_gnn_setup()
    _L2_gnn_in = {k: v for k, v in _L2_gnn_all.items() if k in ('weight', 'bias')}
    del _L2_gnn_all

    def _L3_gnn_setup():
        import jax, jax.numpy as jnp
        import numpy as np
        N_NODES = 3125
        N_EDGES = 50000
        HID = 128
        WIDTH = 80
        EDIM = 16
        NEG_SLOPE = 0.2

        def _param(key, shape):
            fan_in = shape[0]
            return (jax.random.normal(key, shape, jnp.float32) / np.sqrt(fan_in)).astype(jnp.float32)

        def _gat_conv(h_in, src, dst, eattr, W, a_src, a_dst, We, a_e, b, n_nodes):
            h = h_in @ W
            alpha_src = h @ a_src
            alpha_dst = h @ a_dst
            alpha_e = eattr @ We @ a_e
            alpha = alpha_src[src] + alpha_dst[dst] + alpha_e
            alpha = jax.nn.leaky_relu(alpha, NEG_SLOPE)
            m = jax.ops.segment_max(alpha, dst, num_segments=n_nodes)
            ea = jnp.exp(alpha - m[dst])
            denom = jax.ops.segment_sum(ea, dst, num_segments=n_nodes)
            coef = ea / denom[dst]
            out = jax.ops.segment_sum(h[src] * coef[:, None], dst, num_segments=n_nodes)
            return out + b
        key = jax.random.key(seed)
        ks = jax.random.split(key, 24)
        inp = {'x': jax.random.normal(ks[0], (N_NODES, HID), jnp.float32), 'edge_index': jax.random.randint(ks[1], (2, N_EDGES), 0, N_NODES, jnp.int64), 'edge_attr': jax.random.normal(ks[2], (N_EDGES, EDIM), jnp.float32)}
        dims = [(HID, WIDTH), (WIDTH, WIDTH), (WIDTH, HID)]
        k = 3
        for li, (din, dout) in enumerate(dims, start=1):
            inp[f'W{li}'] = _param(ks[k], (din, dout))
            k += 1
            inp[f'as{li}'] = _param(ks[k], (dout,))
            k += 1
            inp[f'ad{li}'] = _param(ks[k], (dout,))
            k += 1
            inp[f'We{li}'] = _param(ks[k], (EDIM, dout))
            k += 1
            inp[f'ae{li}'] = _param(ks[k], (dout,))
            k += 1
            inp[f'b{li}'] = jnp.zeros((dout,), jnp.float32)
            k += 1
        return inp
    _L3_gnn_all = _L3_gnn_setup()
    _L3_gnn_in = {k: v for k, v in _L3_gnn_all.items() if k in ('W1', 'as1', 'ad1', 'We1', 'ae1', 'b1', 'W2', 'as2', 'ad2', 'We2', 'ae2', 'b2', 'W3', 'as3', 'ad3', 'We3', 'ae3', 'b3')}
    del _L3_gnn_all
    return {'x': x, 'src': src, 'dst': dst, 'edge_attr_16': edge_attr_16, 'L0_gnn_W_src': _L0_gnn_in['W_src'], 'L0_gnn_b_src': _L0_gnn_in['b_src'], 'L0_gnn_W_fc': _L0_gnn_in['W_fc'], 'L0_gnn_b_fc': _L0_gnn_in['b_fc'], 'L1_gnn_W_in': _L1_gnn_in['W_in'], 'L1_gnn_b_in': _L1_gnn_in['b_in'], 'L1_gnn_W_out': _L1_gnn_in['W_out'], 'L1_gnn_b_out': _L1_gnn_in['b_out'], 'L1_gnn_w_ih': _L1_gnn_in['w_ih'], 'L1_gnn_w_hh': _L1_gnn_in['w_hh'], 'L1_gnn_b_ih': _L1_gnn_in['b_ih'], 'L1_gnn_b_hh': _L1_gnn_in['b_hh'], 'L2_gnn_weight': _L2_gnn_in['weight'], 'L2_gnn_bias': _L2_gnn_in['bias'], 'L3_gnn_W1': _L3_gnn_in['W1'], 'L3_gnn_as1': _L3_gnn_in['as1'], 'L3_gnn_ad1': _L3_gnn_in['ad1'], 'L3_gnn_We1': _L3_gnn_in['We1'], 'L3_gnn_ae1': _L3_gnn_in['ae1'], 'L3_gnn_b1': _L3_gnn_in['b1'], 'L3_gnn_W2': _L3_gnn_in['W2'], 'L3_gnn_as2': _L3_gnn_in['as2'], 'L3_gnn_ad2': _L3_gnn_in['ad2'], 'L3_gnn_We2': _L3_gnn_in['We2'], 'L3_gnn_ae2': _L3_gnn_in['ae2'], 'L3_gnn_b2': _L3_gnn_in['b2'], 'L3_gnn_W3': _L3_gnn_in['W3'], 'L3_gnn_as3': _L3_gnn_in['as3'], 'L3_gnn_ad3': _L3_gnn_in['ad3'], 'L3_gnn_We3': _L3_gnn_in['We3'], 'L3_gnn_ae3': _L3_gnn_in['ae3'], 'L3_gnn_b3': _L3_gnn_in['b3']}

def reference(x, src, dst, edge_attr_16, L0_gnn_W_src, L0_gnn_b_src, L0_gnn_W_fc, L0_gnn_b_fc, L1_gnn_W_in, L1_gnn_b_in, L1_gnn_W_out, L1_gnn_b_out, L1_gnn_w_ih, L1_gnn_w_hh, L1_gnn_b_ih, L1_gnn_b_hh, L2_gnn_weight, L2_gnn_bias, L3_gnn_W1, L3_gnn_as1, L3_gnn_ad1, L3_gnn_We1, L3_gnn_ae1, L3_gnn_b1, L3_gnn_W2, L3_gnn_as2, L3_gnn_ad2, L3_gnn_We2, L3_gnn_ae2, L3_gnn_b2, L3_gnn_W3, L3_gnn_as3, L3_gnn_ad3, L3_gnn_We3, L3_gnn_ae3, L3_gnn_b3):
    import jax
    import jax.numpy as jnp

    def _L0_gnn_ref(feat, W_src, b_src, W_fc, b_fc, src, dst):
        import jax, jax.numpy as jnp
        import numpy as np
        N_NODES = 10000
        N_EDGES = 20000
        D_FEAT = 128
        D_OUT = 128
        'SAGEConv forward (eval mode: dropout = identity, activation = identity).\n\n            message: m_e = src_fc(feat[src_e])                 # [E, D]\n            reduce:  neigh_v = mean_{e: dst_e = v} m_e         # [N, D]\n            apply:   h_v = fc(concat(feat_v, neigh_v))         # [N, D_out]\n            '
        n = feat.shape[0]
        m = feat[src] @ W_src.T + b_src
        agg = jax.ops.segment_sum(m, dst, num_segments=n)
        deg = jax.ops.segment_sum(jnp.ones(dst.shape, feat.dtype), dst, num_segments=n)
        neigh = agg / jnp.maximum(deg, 1.0)[:, None]
        h = jnp.concatenate([feat, neigh], axis=-1) @ W_fc.T + b_fc
        return h

    def _L1_gnn_ref(feat, src, dst, W_in, b_in, W_out, b_out, w_ih, w_hh, b_ih, b_hh):
        import jax, jax.numpy as jnp
        import numpy as np
        NUM_STEPS = 1

        def _seg_mean(vals, idx, num_nodes):
            s = jax.ops.segment_sum(vals, idx, num_segments=num_nodes)
            cnt = jax.ops.segment_sum(jnp.ones((vals.shape[0],), vals.dtype), idx, num_segments=num_nodes)
            return s / jnp.maximum(cnt, 1.0)[:, None]

        def _gru_cell(a, h, w_ih, w_hh, b_ih, b_hh):
            gi = a @ w_ih.T + b_ih
            gh = h @ w_hh.T + b_hh
            H = h.shape[1]
            i_r, i_z, i_n = (gi[:, :H], gi[:, H:2 * H], gi[:, 2 * H:])
            h_r, h_z, h_n = (gh[:, :H], gh[:, H:2 * H], gh[:, 2 * H:])
            r = jax.nn.sigmoid(i_r + h_r)
            z = jax.nn.sigmoid(i_z + h_z)
            n = jnp.tanh(i_n + r * h_n)
            return (1.0 - z) * n + z * h
        N = feat.shape[0]
        h = feat
        for _ in range(NUM_STEPS):
            feat_in = h @ W_in.T + b_in
            feat_out = h @ W_out.T + b_out
            a_in = _seg_mean(feat_in[src], dst, N)
            a_out = _seg_mean(feat_out[dst], src, N)
            a = jnp.concatenate((a_in, a_out), axis=1)
            h = _gru_cell(a, h, w_ih, w_hh, b_ih, b_hh)
        return h

    def _L2_gnn_ref(x, edge_index, weight, bias):
        import jax, jax.numpy as jnp
        import numpy as np
        N_NODES = 50000
        N_EDGES = 25000
        C_IN = 128
        C_OUT = 128
        n = x.shape[0]
        loops = jnp.arange(n, dtype=edge_index.dtype)
        src = jnp.concatenate([edge_index[0], loops])
        dst = jnp.concatenate([edge_index[1], loops])
        ew = jnp.ones(src.shape[0], dtype=x.dtype)
        deg = jax.ops.segment_sum(ew, dst, num_segments=n)
        deg_inv_sqrt = jnp.where(deg > 0, jax.lax.rsqrt(jnp.maximum(deg, 1.0)), 0.0)
        norm = deg_inv_sqrt[src] * deg_inv_sqrt[dst]
        h = x @ weight
        msg = h[src] * norm[:, None]
        agg = jax.ops.segment_sum(msg, dst, num_segments=n)
        return jax.nn.relu(agg + bias)

    def _L3_gnn_ref(x, edge_index, edge_attr, W1, as1, ad1, We1, ae1, b1, W2, as2, ad2, We2, ae2, b2, W3, as3, ad3, We3, ae3, b3):
        import jax, jax.numpy as jnp
        import numpy as np
        N_NODES = 3125
        N_EDGES = 50000
        HID = 128
        WIDTH = 80
        EDIM = 16
        NEG_SLOPE = 0.2

        def _param(key, shape):
            fan_in = shape[0]
            return (jax.random.normal(key, shape, jnp.float32) / np.sqrt(fan_in)).astype(jnp.float32)

        def _gat_conv(h_in, src, dst, eattr, W, a_src, a_dst, We, a_e, b, n_nodes):
            h = h_in @ W
            alpha_src = h @ a_src
            alpha_dst = h @ a_dst
            alpha_e = eattr @ We @ a_e
            alpha = alpha_src[src] + alpha_dst[dst] + alpha_e
            alpha = jax.nn.leaky_relu(alpha, NEG_SLOPE)
            m = jax.ops.segment_max(alpha, dst, num_segments=n_nodes)
            ea = jnp.exp(alpha - m[dst])
            denom = jax.ops.segment_sum(ea, dst, num_segments=n_nodes)
            coef = ea / denom[dst]
            out = jax.ops.segment_sum(h[src] * coef[:, None], dst, num_segments=n_nodes)
            return out + b
        n = x.shape[0]
        loop = jnp.arange(n, dtype=edge_index.dtype)
        src = jnp.concatenate([edge_index[0], loop])
        dst = jnp.concatenate([edge_index[1], loop])
        mean_ea = jnp.mean(edge_attr, axis=0)
        eattr = jnp.concatenate([edge_attr, jnp.broadcast_to(mean_ea, (n, edge_attr.shape[1]))], axis=0)
        skip = x
        h = _gat_conv(x, src, dst, eattr, W1, as1, ad1, We1, ae1, b1, n)
        h = jax.nn.relu(h)
        h = _gat_conv(h, src, dst, eattr, W2, as2, ad2, We2, ae2, b2, n)
        h = jax.nn.relu(h)
        h = _gat_conv(h, src, dst, eattr, W3, as3, ad3, We3, ae3, b3, n)
        return h + skip
    edge_index = jnp.stack([src, dst])
    x = _layernorm(x + _L0_gnn_ref(x, L0_gnn_W_src, L0_gnn_b_src, L0_gnn_W_fc, L0_gnn_b_fc, src, dst), axis=-1)
    x = _layernorm(x + _L1_gnn_ref(x, src, dst, L1_gnn_W_in, L1_gnn_b_in, L1_gnn_W_out, L1_gnn_b_out, L1_gnn_w_ih, L1_gnn_w_hh, L1_gnn_b_ih, L1_gnn_b_hh), axis=-1)
    x = _layernorm(x + _L2_gnn_ref(x, edge_index, L2_gnn_weight, L2_gnn_bias), axis=-1)
    x = _layernorm(x + _L3_gnn_ref(x, edge_index, edge_attr_16, L3_gnn_W1, L3_gnn_as1, L3_gnn_ad1, L3_gnn_We1, L3_gnn_ae1, L3_gnn_b1, L3_gnn_W2, L3_gnn_as2, L3_gnn_ad2, L3_gnn_We2, L3_gnn_ae2, L3_gnn_b2, L3_gnn_W3, L3_gnn_as3, L3_gnn_ad3, L3_gnn_We3, L3_gnn_ae3, L3_gnn_b3), axis=-1)
    return x

_drawn_inputs = setup_inputs


def setup_inputs(seed=0):
    import zlib

    import numpy as np

    out = dict(_drawn_inputs(seed))
    spreads = {'L1_gnn_b_in': (0.0, 0.277),
     'L1_gnn_b_out': (0.0, 0.1),
     'L1_gnn_b_ih': (0.0, 0.1),
     'L1_gnn_b_hh': (0.0, 0.377),
     'L2_gnn_bias': (0.0, 0.1),
     'L3_gnn_b1': (0.0, 0.606),
     'L3_gnn_b2': (0.0, 0.272),
     'L3_gnn_b3': (0.0, 0.1)}
    factors = {'edge_attr_16': 8.0,
     'L0_gnn_b_src': 7.436,
     'L0_gnn_b_fc': 4.753,
     'L3_gnn_W1': 3.369,
     'L3_gnn_as1': 4.031,
     'L3_gnn_ad1': 8.0,
     'L3_gnn_We1': 8.0,
     'L3_gnn_ae1': 8.0,
     'L3_gnn_as2': 8.0,
     'L3_gnn_ad2': 8.0,
     'L3_gnn_We2': 8.0,
     'L3_gnn_ae2': 8.0,
     'L3_gnn_as3': 8.0,
     'L3_gnn_ad3': 8.0,
     'L3_gnn_We3': 8.0,
     'L3_gnn_ae3': 8.0}
    for name, (base, spread) in spreads.items():
        noise = np.random.default_rng([zlib.crc32(name.encode()), seed]).standard_normal(out[name].shape)
        drawn = base * np.exp(spread * noise) if base else spread * noise
        out[name] = jnp.asarray(drawn.astype(out[name].dtype))
    for name, factor in factors.items():
        out[name] = (out[name] * factor).astype(out[name].dtype)
    return out
```

```python
from contextlib import ExitStack

import concourse.bass as bass
from concourse import mybir

P = 128
N = 3125
NT = -(-N // P)
NP = NT * P
E = 103125
HALF = 12
BODY = 2 * HALF
CH = -(-E // (P * BODY)) * BODY
EP = CH * P
ITERS = CH // BODY
ACCW = NP + P
BLOCKS = [(b, min(512, NP - b)) for b in range(0, NP, 512)]
NB = len(BLOCKS)
D = 128
EDIM = 16
LAYERS = [(128, 80), (80, 80), (80, 128)]
SLOPE = 0.2
EPS = 1e-5
QUADS = CH // 4
RING = BODY // 4
WIN = 20
KEYS = NT * WIN
AW = N + WIN + 1
ADJ_BLOCKS = [(b, min(n, 64)) if b + 512 > NP else (b, n) for b, n in BLOCKS]
ADJ_END = sum(ADJ_BLOCKS[-1])
GAT_WEIGHTS = ("w_gat", "b_gat", "w_a", "w_eT")
BIG = 1e30
GROUP = 4
TURNS = 17
SLOTS = [204, 204, 136]
BANKS = [3, 3, 2]
AHEAD_PICK = 108
AHEAD_SOFT = 164
assert KEYS <= 512 and N <= ADJ_END <= AW and RING % 2 == 0
assert CH == ITERS * BODY
assert all(CH % s == 0 and s % (GROUP * TURNS) == 0 and s // GROUP % b == 0 for s, b in zip(SLOTS, BANKS))

F32 = mybir.dt.float32
I32 = mybir.dt.int32
BF16 = mybir.dt.bfloat16
U8 = mybir.dt.uint8
F16 = mybir.dt.float16
ALU = mybir.AluOpType
ACT = mybir.ActivationFunctionType
AX = mybir.AxisListType.X


def ev(step, block):
    return NB * step + block + 1


class Chain:

    def __init__(self, engine, sem):
        self.engine, self.sem, self.n = engine, sem, 0

    def link(self, ins):
        self.n += 1
        ins.then_inc(self.sem, 1)
        self.engine.wait_ge(self.sem, self.n)


def gnn_kernel(nc, t, out):
    def sb(name, shape, dt=F32):
        return nc.alloc_sbuf_tensor(name, shape, dt)

    phase_own = []

    def sem(name, kept=False):
        made = nc.alloc_semaphore(name)
        if not kept:
            phase_own.append(made)
        return made

    def end_phase():
        nc.clear_and_free_semaphores(list(phase_own))
        phase_own.clear()
        nc.all_engine_barrier()

    def dram(name, shape, dt=F32):
        return nc.dram_tensor(name, shape, dt, kind="Internal").ap()

    h_tab = [dram(f"h_tab{l}", [NP, dout]) for l, (_, dout) in enumerate(LAYERS)]
    e_first = dram("e_first", [EP + P, 2])
    e_as = dram("e_as", [EP])
    e_coef = dram("e_coef", [EP])
    e_self = dram("e_self", [EP + P, 1])
    e_lo = dram("e_lo", [EP], BF16)

    xT = sb("xT", [P, NP])
    ident = sb("ident", [P, P])
    ident_bf = sb("ident_bf", [P, P], BF16)
    iota_row = sb("iota_row", [P, P])
    part_id = sb("part_id", [P, 1])
    ones = sb("ones", [P, P])
    ones_bf = sb("ones_bf", [P, 1], BF16)
    mean_m = sb("mean_m", [P, P])
    eps_col = sb("eps_col", [P, 1])
    one_col = sb("one_col", [P, 1])
    first_pos = sb("first_pos", [P, NT], I32)
    rdeg = sb("rdeg", [P, NT])
    dinv = sb("dinv", [P, NT])
    psum = nc.alloc_psum_tensor("psum", [P, 8, 512], F32)

    consts = sem("consts")
    with nc.Block() as block:

        @block.gpsimd
        def _(pool):
            nc.gpsimd.memset(ident[:], 0.0).then_inc(consts, 1)
            pool.wait_ge(consts, 1)
            nc.gpsimd.affine_select(out=ident[:], in_=ident[:], compare_op=ALU.not_equal, fill=1.0,
                                    base=0, pattern=[[-1, P]], channel_multiplier=1)
            nc.gpsimd.memset(ident_bf[:], 0.0).then_inc(consts, 1)
            pool.wait_ge(consts, 2)
            nc.gpsimd.affine_select(out=ident_bf[:], in_=ident_bf[:], compare_op=ALU.not_equal, fill=1.0,
                                    base=0, pattern=[[-1, P]], channel_multiplier=1)
            nc.gpsimd.iota(iota_row[:], [[1, P]], base=0, channel_multiplier=0,
                           allow_small_or_imprecise_dtypes=True)
            nc.gpsimd.iota(part_id[:], [[0, 1]], base=0, channel_multiplier=1,
                           allow_small_or_imprecise_dtypes=True)
            nc.gpsimd.memset(ones[:], 1.0)
            nc.gpsimd.memset(mean_m[:], 1.0 / D)
            nc.gpsimd.memset(eps_col[:], EPS)
            nc.gpsimd.memset(one_col[:], 1.0)
            nc.gpsimd.memset(ones_bf[:], 1.0)

    early = ExitStack()

    def eb(name, shape, dt=F32):
        return early.enter_context(nc.sbuf_tensor(name, shape, dt))

    adj = eb("adj", [P, NT, AW], BF16)

    end_phase()
    with ExitStack() as stack:
        def bb(name, shape, dt=F32):
            return stack.enter_context(nc.sbuf_tensor(name, shape, dt))

        src_i = bb("src_i", [P, CH], I32)
        dst_i = bb("dst_i", [P, CH], I32)
        base_i = bb("base_i", [P, QUADS], I32)
        lo_f = bb("lo_f", [P, CH + 4])
        hi_f = bb("adj_hi", [P, CH], BF16)
        valid = bb("valid", [P, CH], BF16)
        place = bb("place", [P, CH])
        key = bb("key", [P, CH + 4])
        q_base = bb("q_base", [1, QUADS], I32)
        q_last = bb("q_last", [1, QUADS], I32)
        span = bb("span", [1, QUADS])
        steps = bb("steps", [1, N // WIN])
        passes_f = bb("passes_f", [1, 1])
        passes_i = bb("passes_i", [1, 1], I32)
        iota_key = bb("iota_key", [P, KEYS], F16)
        lo_hot = bb("adj_lo_hot", [P, 8, P], BF16)
        key_hot = bb("adj_key_hot", [P, 8, KEYS], BF16)

        loaded = sem("adj_loaded")
        iotas = sem("adj_iotas")
        ready = sem("adj_ready")
        pass_ready = sem("adj_pass_ready")
        hots_made = sem("adj_hots_made")
        counted = sem("adj_counted")
        added = sem("adj_added")
        ch = sem("adj_chain")

        with nc.Block() as block:

            @block.sync
            def _(sp):
                for to, of in ((src_i[:], t["src_cl"]), (dst_i[:], t["dst_cl"]),
                               (base_i[:], t["quad_base"].partition_broadcast(P)),
                               (q_base[:], t["quad_base"].rearrange("(a n) -> a n", a=1)),
                               (q_last[:], t["quad_last"].rearrange("(a n) -> a n", a=1))):
                    sp.dma_start(to, of).then_inc(loaded, 16)

            @block.gpsimd
            def _(pool):
                nc.gpsimd.iota(iota_key[:], [[1, KEYS]], base=0, channel_multiplier=0,
                               allow_small_or_imprecise_dtypes=True).then_inc(iotas, 1)
                nc.gpsimd.iota(steps[:], [[WIN, N // WIN]], base=WIN, channel_multiplier=0,
                               allow_small_or_imprecise_dtypes=True).then_inc(iotas, 1)
                nc.gpsimd.memset(adj[:, 0:NT // 2, :].rearrange("p h n -> p (h n)").bitcast(I32), 0
                                 ).then_inc(iotas, 1)

            @block.vector
            def _(dve):
                chain = Chain(dve, ch)
                half = NT // 2
                nc.vector.memset(adj[:, half:NT, :].rearrange("p h n -> p (h n)").bitcast(I32), 0)
                nc.vector.memset(key[:, CH:CH + 4], -1.0)
                nc.vector.memset(lo_f[:, CH:CH + 4], 0.0)
                dve.wait_ge(loaded, 16 * 5)
                chain.link(nc.vector.tensor_tensor(
                    place[:].rearrange("p (q k) -> p q k", k=4), dst_i[:].rearrange("p (q k) -> p q k", k=4),
                    base_i[:, :, None].to_broadcast([P, QUADS, 4]), ALU.subtract))
                chain.link(nc.vector.tensor_single_scalar(dst_i[:], src_i[:], P - 1, ALU.bitwise_and))
                chain.link(nc.vector.tensor_copy(lo_f[:, 0:CH], dst_i[:]))
                chain.link(nc.vector.tensor_single_scalar(dst_i[:], src_i[:], 7, ALU.arith_shift_right))
                chain.link(nc.vector.tensor_copy(hi_f[:], dst_i[:]))
                chain.link(nc.vector.tensor_scalar(span[:], q_last[:], float(N - 1), None, ALU.min))
                chain.link(nc.vector.tensor_tensor(span[:], span[:], q_base[:], ALU.subtract))
                chain.link(nc.vector.tensor_reduce(passes_f[:], span[:], AX, ALU.max))
                dve.wait_ge(iotas, 3)
                chain.link(nc.vector.tensor_scalar(steps[:], steps[:], passes_f[:], None, ALU.is_le))
                chain.link(nc.vector.tensor_reduce(passes_f[:], steps[:], AX, ALU.add))
                chain.link(nc.vector.tensor_scalar(passes_i[:], passes_f[:], 1.0, None, ALU.add))
                dve.sem_inc(ready, 1)
                passes = dve.value_load(passes_i[0:1, 0:1], min_val=1, max_val=N // WIN + 1)

                def hots_of(c, k):
                    nc.vector.tensor_scalar(lo_hot[:, k % 8, :], iota_key[:, 0:P], lo_f[:, bass.ds(c, 1)], None,
                                            ALU.is_equal).then_inc(hots_made, 1)
                    nc.vector.tensor_scalar(key_hot[:, k % 8, :], iota_key[:], key[:, bass.ds(c, 1)], None,
                                            ALU.is_equal).then_inc(hots_made, 1)

                dve.sem_inc(added, RING)
                dve.sem_inc(pass_ready, 1)
                with dve.Fori(0, passes) as s:
                    def after(ins, n):
                        ins.then_inc(pass_ready, 1)
                        dve.wait_ge(pass_ready, s * 7 + (n + 2))
                    after(nc.vector.tensor_scalar(valid[:], place[:], 0.0, None, ALU.is_ge), 0)
                    after(nc.vector.scalar_tensor_tensor(valid[:], place[:], float(WIN), valid[:],
                                                         ALU.is_lt, ALU.mult), 1)
                    after(nc.vector.scalar_tensor_tensor(key[:, 0:CH], hi_f[:], float(WIN), place[:],
                                                         ALU.mult, ALU.add), 2)
                    after(nc.vector.scalar_tensor_tensor(key[:, 0:CH], key[:, 0:CH], 1.0, valid[:],
                                                         ALU.add, ALU.mult), 3)
                    after(nc.vector.tensor_scalar(key[:, 0:CH], key[:, 0:CH], -1.0, None, ALU.add), 4)
                    for c in range(4):
                        hots_of(c, c)
                    with dve.Fori(0, ITERS) as i:
                        for q in range(RING):
                            for k in range(4):
                                hots_of(i * BODY + (4 * q + k + 4), 4 * q + k + 4)
                            j = i * RING + q
                            base = dve.value_load(q_base[0:1, bass.ds(j, 1)], min_val=0, max_val=AW - WIN)
                            dve.wait_ge(counted, s * QUADS + i * RING + (q + 1 + RING))
                            dve.wait_ge(added, s * QUADS + i * RING + (q + RING))
                            window = adj[:, :, bass.ds(base, WIN)]
                            nc.vector.tensor_tensor(window, window, psum[:, q, 0:KEYS].rearrange(
                                "p (h w) -> p h w", w=WIN), ALU.add).then_inc(added, 1)
                    after(nc.vector.tensor_scalar(place[:], place[:], -float(WIN), None, ALU.add), 5)
                    after(nc.vector.tensor_scalar(q_base[:], q_base[:], float(WIN), float(AW - WIN),
                                                  ALU.add, ALU.min), 6)

            @block.tensor
            def _(pe):
                pe.wait_ge(ready, 1)
                passes = pe.value_load(passes_i[0:1, 0:1], min_val=1, max_val=N // WIN + 1)
                pe.sem_inc(counted, RING)
                with pe.Fori(0, passes) as s:
                    with pe.Fori(0, ITERS) as i:
                        for q in range(RING):
                            pe.wait_ge(added, s * QUADS + i * RING + (q + 1))
                            for k in range(4):
                                pe.wait_ge(hots_made, s * (2 * CH + 8) + i * (2 * BODY) + (8 * q + 2 * k + 2))
                                last = nc.tensor.matmul(psum[:, q, 0:KEYS], lhsT=lo_hot[:, (4 * q + k) % 8, :],
                                                        rhs=key_hot[:, (4 * q + k) % 8, :],
                                                        start=k == 0, stop=k == 3)
                            last.then_inc(counted, 1)

    end_phase()
    mm, dv, ch = sem("first_mm"), sem("first_dv"), sem("first_chain")
    with ExitStack() as stack, nc.Block() as block:
        deg_row = stack.enter_context(nc.sbuf_tensor("deg_row", [1, NP], F32))
        first_row = stack.enter_context(nc.sbuf_tensor("first_row", [1, NP], F32))
        dump = stack.enter_context(nc.sbuf_tensor("dump", [1, P], F32))
        dumped = sem("dumped")
        rooted = sem("rooted")

        @block.gpsimd
        def _(pool):
            nc.gpsimd.iota(dump[:], [[1, P]], base=EP, channel_multiplier=0,
                           allow_small_or_imprecise_dtypes=True).then_inc(dumped, 1)

        @block.tensor
        def _(pe):
            for b, (lo, n) in enumerate(ADJ_BLOCKS):
                for h in range(NT):
                    last = nc.tensor.matmul(psum[0:1, b, 0:n], lhsT=ones_bf[:, 0:1],
                                            rhs=adj[:, h, lo:lo + n], start=h == 0, stop=h == NT - 1)
                last.then_inc(mm, 1)
            pe.wait_ge(dv, NB + 1)
            for k in range(NT):
                nc.tensor.matmul(psum[:, 7, k:k + 1], lhsT=deg_row[0:1, k * P:(k + 1) * P],
                                 rhs=one_col[0:1, :], start=True, stop=True)
                last = nc.tensor.matmul(psum[:, 7, NT + k:NT + k + 1], lhsT=first_row[0:1, k * P:(k + 1) * P],
                                        rhs=one_col[0:1, :], start=True, stop=True)
            last.then_inc(mm, 1)

        @block.vector
        def _(dve):
            chain = Chain(dve, ch)
            chain.link(nc.vector.memset(deg_row[:, ADJ_END:NP], 0.0))
            chain.link(nc.vector.memset(first_row[:], 1.0))
            for b, (lo, n) in enumerate(ADJ_BLOCKS):
                dve.wait_ge(mm, b + 1)
                nc.vector.tensor_copy(deg_row[:, lo:lo + n], psum[0:1, b, 0:n]).then_inc(dv, 1)
            dve.wait_ge(dv, NB)
            chain.link(nc.vector.tensor_tensor_scan(first_row[:], first_row[:], deg_row[:], 0.0,
                                                    ALU.mult, ALU.add))
            chain.link(nc.vector.tensor_tensor(first_row[:], first_row[:], deg_row[:], ALU.subtract))
            dve.wait_ge(dumped, 1)
            nc.vector.tensor_copy(first_row[:, N:NP], dump[:, 0:NP - N]).then_inc(dv, 1)
            dve.wait_ge(mm, NB + 1)
            nc.vector.tensor_copy(first_pos[:], psum[:, 7, NT:2 * NT])
            chain.link(nc.vector.tensor_scalar_max(rdeg[:], psum[:, 7, 0:NT], 1.0))
            chain.link(nc.vector.reciprocal(rdeg[:], rdeg[:]))
            nc.vector.tensor_scalar(dinv[:], psum[:, 7, 0:NT], 1.0, None, ALU.add).then_inc(dv, 1)
            dve.wait_ge(rooted, 1)
            nc.vector.reciprocal(dinv[:], dinv[:]).then_inc(dv, 1)

        @block.scalar
        def _(act):
            act.wait_ge(dv, NB + 2)
            nc.scalar.activation(dinv[:], dinv[:], ACT.Sqrt).then_inc(rooted, 1)

    ew = {k: eb("sb_" + k, list(t[k].shape)) for k in t
          if k.startswith(("w_", "b_")) and not k.startswith(GAT_WEIGHTS)}
    gate_b = eb("gate_b", [P, 3])
    parts = eb("parts", [P, 3, NT, D], BF16)
    temp = eb("temp", [P, 5, 512])
    diag = eb("adj_diag", [P, 4, P])
    SLICES = 6
    products = [(h, s) for h in range(NT) for s in range(3)]

    def neighbour_slice(b, k):
        lo, n = ADJ_BLOCKS[b]
        size = -(-len(products) // SLICES)
        for j, (h, s) in list(enumerate(products))[k * size:(k + 1) * size]:
            last = nc.tensor.matmul(psum[:, b % 2, 0:n], lhsT=parts[:, s, h, :], rhs=adj[:, h, lo:lo + n],
                                    start=j == 0, stop=j == len(products) - 1)
        return last

    def spread(b):
        lo, n = ADJ_BLOCKS[b]
        for k in range(0, n, P):
            m = min(P, n - k)
            last = nc.tensor.matmul(psum[:, 2, k:k + m], lhsT=ones[:], rhs=diag[:, k // P, 0:m],
                                    start=True, stop=True)
        return last

    def diagonals(b, value):
        lo, n = ADJ_BLOCKS[b]
        for k in range(0, n, P):
            last = nc.vector.tensor_scalar(diag[:, k // P, :], ident[:],
                                           value[:, lo // P + k // P:lo // P + k // P + 1], None, ALU.mult)
        return last

    def split_dve(dve, b, source, spare, chain):
        lo, n = BLOCKS[b]
        s = slice(lo // P, (lo + n) // P)
        first, second, third = (parts[:, k, s, :].rearrange("p t d -> p (t d)") for k in range(3))
        chain.link(nc.vector.tensor_tensor(spare, source, first, ALU.subtract))
        chain.link(nc.vector.tensor_copy(second, spare))
        return nc.vector.tensor_tensor(third, spare, second, ALU.subtract)

    def norm(name, after):
        end_phase()
        mean_done, var_done, node_done = sem(name + "_mean"), sem(name + "_var"), sem(name + "_node")
        centred, normed, split = sem(name + "_centred"), sem(name + "_normed"), sem(name + "_split")
        squared, rooted, first_part, ch = (sem(f"{name}_{k}") for k in ("squared", "rooted", "first", "chain"))
        with nc.Block() as block:

            @block.tensor
            def _(pe):
                for b, (lo, n) in enumerate(BLOCKS):
                    nc.tensor.matmul(psum[:, b, 0:n], lhsT=mean_m[:], rhs=xT[:, lo:lo + n],
                                     start=True, stop=True).then_inc(mean_done, 1)
                for b, (lo, n) in enumerate(BLOCKS):
                    pe.wait_ge(squared, b + 1)
                    nc.tensor.matmul(psum[:, b, 0:n], lhsT=mean_m[:], rhs=temp[:, b % 2, 0:n],
                                     start=True, stop=True).then_inc(var_done, 1)
                for b, (lo, n) in enumerate(BLOCKS):
                    if after is None:
                        break
                    pe.wait_ge(normed, b + 1)
                    for k in range(n // P):
                        to, of = psum[:, b, k * P:(k + 1) * P], xT[:, lo + k * P:lo + (k + 1) * P]
                        if after == "transpose":
                            last = nc.tensor.transpose(to, of, ident[:])
                        else:
                            last = nc.tensor.matmul(to, lhsT=of, rhs=ew["w_gcn"][:], start=True, stop=True)
                    last.then_inc(node_done, 1)

            @block.gpsimd
            def _(pool):
                for h in range(NT if after == "project" else 0):
                    own = adj[:, h, h * P:min(h * P + P, N)]
                    nc.gpsimd.tensor_tensor(own, own, ident_bf[:, 0:own.shape[-1]], ALU.add)

            @block.scalar
            def _(act):
                for b, (lo, n) in enumerate(BLOCKS):
                    act.wait_ge(centred, b + 1)
                    if b >= 2:
                        act.wait_ge(var_done, b - 1)
                    nc.scalar.activation(temp[:, b % 2, 0:n], xT[:, lo:lo + n], ACT.Square).then_inc(squared, 1)
                for b, (lo, n) in enumerate(BLOCKS):
                    act.wait_ge(var_done, b + 1)
                    if b >= 2:
                        act.wait_ge(normed, b - 1)
                    nc.scalar.activation(temp[:, 2 + b % 2, 0:n], psum[:, b, 0:n], ACT.Sqrt,
                                         bias=eps_col[:]).then_inc(rooted, 1)
                for b, (lo, n) in enumerate(BLOCKS):
                    if after is None:
                        break
                    act.wait_ge(node_done, b + 1)
                    if after == "project":
                        if b >= 2:
                            act.wait_ge(split, b - 1)
                        for k in range(n // P):
                            last = nc.scalar.activation(temp[:, b % 2, k * P:(k + 1) * P],
                                                        psum[:, b, k * P:(k + 1) * P], ACT.Copy,
                                                        scale=dinv[:, lo // P + k:lo // P + k + 1])
                        last.then_inc(squared, 1)
                        act.wait_ge(squared, NB + b + 1)
                        source = temp[:, b % 2, 0:n]
                    else:
                        source = psum[:, b, 0:n]
                    nc.scalar.copy(parts[:, 0, lo // P:(lo + n) // P, :].rearrange("p t d -> p (t d)"),
                                   source).then_inc(first_part, 1)

            @block.vector
            def _(dve):
                chain = Chain(dve, ch)
                for b, (lo, n) in enumerate(BLOCKS):
                    dve.wait_ge(mean_done, b + 1)
                    nc.vector.tensor_tensor(xT[:, lo:lo + n], xT[:, lo:lo + n], psum[:, b, 0:n], ALU.subtract
                                            ).then_inc(centred, 1)
                for b, (lo, n) in enumerate(BLOCKS):
                    std = temp[:, 2 + b % 2, 0:n]
                    dve.wait_ge(rooted, b + 1)
                    chain.link(nc.vector.reciprocal(std, std))
                    nc.vector.tensor_tensor(xT[:, lo:lo + n], xT[:, lo:lo + n], std, ALU.mult
                                            ).then_inc(normed, 1)
                for b, (lo, n) in enumerate(BLOCKS):
                    if after is None:
                        break
                    dve.wait_ge(first_part, b + 1)
                    source = psum[:, b, 0:n] if after == "transpose" else temp[:, b % 2, 0:n]
                    split_dve(dve, b, source, temp[:, 4, 0:n], chain).then_inc(split, 1)
                    dve.wait_ge(split, b + 1)

    end_phase()
    landed, weights_landed = sem("x_zeroed"), sem("weights_landed")
    first_part, split, ch = sem("x_first"), sem("x_split"), sem("x_chain")
    x_rows = [sem(f"x_rows{k}") for k in range(2)]
    with nc.Block() as block:
        full = N // P

        @block.sync
        def _(sp):
            for b, (lo, n) in enumerate(BLOCKS):
                if b >= 2:
                    sp.wait_ge(split, b - 1)
                to = temp[:, b % 2, 0:n].rearrange("p (t d) -> p t d", d=D)
                if b < NB - 1:
                    sp.dma_start(to, t["x"][lo:lo + n, :].rearrange("(t p) d -> p t d", p=P)
                                 ).then_inc(x_rows[b % 2], 16)
                else:
                    sp.wait_ge(landed, 1)
                    sp.dma_start(to[0:N - lo, 0, :], t["x"][lo:N, :]).then_inc(x_rows[b % 2], 16)

        @block.scalar
        def _(act):
            for k, w in ew.items():
                act.dma_start(w[:], t[k]).then_inc(weights_landed, 16)
            act.dma_start(xT[:, 0:N], t["xT"]).then_inc(weights_landed, 16)
            for b, (lo, n) in enumerate(BLOCKS):
                act.wait_ge(x_rows[b % 2], 16 * (b // 2 + 1))
                nc.scalar.copy(parts[:, 0, lo // P:(lo + n) // P, :].rearrange("p t d -> p (t d)"),
                               temp[:, b % 2, 0:n]).then_inc(first_part, 1)
            act.wait_ge(weights_landed, 16 * (len(ew) + 1))

        @block.gpsimd
        def _(pool):
            nc.gpsimd.memset(xT[:, N:NP], 0.0)

        @block.vector
        def _(dve):
            chain = Chain(dve, ch)
            for b, (lo, n) in enumerate(BLOCKS):
                if b == NB - 1:
                    dve.wait_ge(split, b - 1)
                    nc.vector.memset(temp[:, b % 2, 0:n], 0.0).then_inc(landed, 1)
                dve.wait_ge(first_part, b + 1)
                split_dve(dve, b, temp[:, b % 2, 0:n], temp[:, 4, 0:n], chain).then_inc(split, 1)
                dve.wait_ge(split, b + 1)

    class Layer:

        def __init__(self, name, pe, dve, act):
            self.pe, self.dve, self.act = pe, dve, act
            self.sums, self.spread, self.diags, self.chain = (
                sem(f"{name}_{k}") for k in ("sums", "spread", "diagonals", "chain"))
            self.pe_done, self.dve_done, self.act_done = (sem(f"{name}_{k}_done") for k in ("pe", "dve", "act"))

    def blocks_pe(pe, y, step):
        pe.wait_ge(y.diags, 1)
        spread(0).then_inc(y.spread, 1)
        for k in range(SLICES):
            last = neighbour_slice(0, k)
        last.then_inc(y.sums, 1)
        for b in range(NB):
            more = b + 1 < NB
            if more:
                pe.wait_ge(y.diags, b + 2)
                pe.wait_ge(y.act_done, b * y.act + 1)
                spread(b + 1).then_inc(y.spread, 1)
                if b >= 1:
                    pe.wait_ge(y.dve_done, (b - 1) * y.dve + 1)
            for k in range(SLICES):
                if k < y.pe:
                    step(b, k).then_inc(y.pe_done, 1)
                if more:
                    last = neighbour_slice(b + 1, k)
            if more:
                last.then_inc(y.sums, 1)

    def spread_act(act, y, b, behind):
        lo, n = ADJ_BLOCKS[b]
        act.wait_ge(y.spread, b + 1)
        if b >= 1:
            act.wait_ge(y.dve_done, (b - 1) * y.dve + behind + 1)
        nc.scalar.copy(temp[:, 4, 0:n], psum[:, 2, 0:n]).then_inc(y.act_done, 1)

    def scaled_dve(dve, y, b, value):
        lo, n = ADJ_BLOCKS[b]
        dve.wait_ge(y.sums, b + 1)
        dve.wait_ge(y.act_done, b * y.act + 1)
        if b >= 1:
            dve.wait_ge(y.dve_done, b * y.dve)
        nc.vector.tensor_tensor(temp[:, 0, 0:n], psum[:, b % 2, 0:n], temp[:, 4, 0:n], ALU.mult
                                ).then_inc(y.dve_done, 1)
        if b + 1 < NB:
            diagonals(b + 1, value).then_inc(y.diags, 1)

    end_phase()
    y = Layer("sage", 2, 2, 2)
    with nc.Block() as block:

        @block.tensor
        def _(pe):
            def step(b, k):
                lo, n = ADJ_BLOCKS[b]
                if k == 0:
                    pe.wait_ge(y.dve_done, b * y.dve + 1)
                    return nc.tensor.matmul(psum[:, 3, 0:n], lhsT=ew["w_src"][:], rhs=temp[:, 0, 0:n],
                                            start=True, stop=True)
                if b >= 1:
                    pe.wait_ge(y.dve_done, b * y.dve)
                pe.wait_ge(y.act_done, b * y.act + 2)
                nc.tensor.matmul(psum[:, 4, 0:n], lhsT=ew["w_fc"][:, 0:D], rhs=xT[:, lo:lo + n],
                                 start=True, stop=False)
                return nc.tensor.matmul(psum[:, 4, 0:n], lhsT=ew["w_fc"][:, D:2 * D], rhs=temp[:, 1, 0:n],
                                        start=False, stop=True)

            blocks_pe(pe, y, step)

        @block.scalar
        def _(act):
            for b, (lo, n) in enumerate(ADJ_BLOCKS):
                spread_act(act, y, b, 0)
                act.wait_ge(y.pe_done, b * y.pe + 1)
                nc.scalar.activation(temp[:, 1, 0:n], psum[:, 3, 0:n], ACT.Identity, bias=ew["b_src"][:]
                                     ).then_inc(y.act_done, 1)

        @block.vector
        def _(dve):
            diagonals(0, rdeg).then_inc(y.diags, 1)
            for b, (lo, n) in enumerate(ADJ_BLOCKS):
                scaled_dve(dve, y, b, rdeg)
                dve.wait_ge(y.pe_done, b * y.pe + 2)
                nc.vector.scalar_tensor_tensor(xT[:, lo:lo + n], psum[:, 4, 0:n], ew["b_fc"][:],
                                               xT[:, lo:lo + n], ALU.add, ALU.add).then_inc(y.dve_done, 1)

    norm("norm0", "transpose")

    end_phase()
    y = Layer("gru", 6, 4, 6)
    with nc.Block() as block:

        @block.tensor
        def _(pe):
            def step(b, k):
                lo, n = ADJ_BLOCKS[b]
                x_b, t0, t1, t2 = xT[:, lo:lo + n], temp[:, 0, 0:n], temp[:, 1, 0:n], temp[:, 2, 0:n]
                wi, wh = ew["w_ih"], ew["w_hh"]
                if k == 0:
                    pe.wait_ge(y.dve_done, b * y.dve + 1)
                if k < 2:
                    w = ew["w_in"] if k == 0 else ew["w_out"]
                    return nc.tensor.matmul(psum[:, 3 + k, 0:n], lhsT=w[:], rhs=t0, start=True, stop=True)
                if k == 2:
                    pe.wait_ge(y.act_done, b * y.act + 3)
                gate = {2: 0, 3: 1, 4: 2, 5: 2}[k]
                g = slice(gate * D, (gate + 1) * D)
                bank = {2: 5, 3: 6, 4: 7, 5: 3}[k]
                if k != 4:
                    nc.tensor.matmul(psum[:, bank, 0:n], lhsT=wi[:, 0, g], rhs=t1, start=True, stop=False)
                    last = nc.tensor.matmul(psum[:, bank, 0:n], lhsT=wi[:, 1, g], rhs=t2,
                                            start=False, stop=k == 5)
                if k != 5:
                    last = nc.tensor.matmul(psum[:, bank, 0:n], lhsT=wh[:, g], rhs=x_b,
                                            start=k == 4, stop=True)
                return last

            blocks_pe(pe, y, step)

        @block.scalar
        def _(act):
            act.wait_ge(y.chain, 1)
            for b, (lo, n) in enumerate(ADJ_BLOCKS):
                spread_act(act, y, b, 3)
                for k, bias in enumerate(("b_in", "b_out")):
                    act.wait_ge(y.pe_done, b * y.pe + k + 1)
                    nc.scalar.activation(temp[:, 1 + k, 0:n], psum[:, 3 + k, 0:n], ACT.Identity,
                                         bias=ew[bias][:]).then_inc(y.act_done, 1)
                for k in range(2):
                    act.wait_ge(y.pe_done, b * y.pe + 3 + k)
                    nc.scalar.activation(temp[:, 3 + k, 0:n], psum[:, 5 + k, 0:n], ACT.Sigmoid,
                                         bias=gate_b[:, k:k + 1]).then_inc(y.act_done, 1)
                act.wait_ge(y.dve_done, b * y.dve + 3)
                nc.scalar.activation(temp[:, 3, 0:n], temp[:, 3, 0:n], ACT.Tanh).then_inc(y.act_done, 1)

        @block.vector
        def _(dve):
            chain = Chain(dve, y.chain)
            chain.link(nc.vector.tensor_tensor(gate_b[:], ew["b_ih"][:], ew["b_hh"][:], ALU.add))
            diagonals(0, rdeg).then_inc(y.diags, 1)
            for b, (lo, n) in enumerate(ADJ_BLOCKS):
                t0, t3, t4, x_b = temp[:, 0, 0:n], temp[:, 3, 0:n], temp[:, 4, 0:n], xT[:, lo:lo + n]
                scaled_dve(dve, y, b, rdeg)
                dve.wait_ge(y.pe_done, b * y.pe + 5)
                dve.wait_ge(y.act_done, b * y.act + 5)
                nc.vector.scalar_tensor_tensor(t3, psum[:, 7, 0:n], ew["b_hh"][:, 2:3], t3,
                                               ALU.add, ALU.mult).then_inc(y.dve_done, 1)
                dve.wait_ge(y.pe_done, b * y.pe + 6)
                dve.wait_ge(y.dve_done, b * y.dve + 2)
                nc.vector.scalar_tensor_tensor(t3, psum[:, 3, 0:n], ew["b_ih"][:, 2:3], t3,
                                               ALU.add, ALU.add).then_inc(y.dve_done, 1)
                dve.wait_ge(y.act_done, b * y.act + 6)
                chain.link(nc.vector.tensor_tensor(t0, x_b, t3, ALU.subtract))
                chain.link(nc.vector.tensor_tensor(t0, t0, t4, ALU.mult))
                chain.link(nc.vector.tensor_tensor(t0, t0, t3, ALU.add))
                nc.vector.tensor_tensor(x_b, x_b, t0, ALU.add).then_inc(y.dve_done, 1)

    norm("norm1", "project")

    end_phase()
    y = Layer("gcn", 0, 2, 1)
    with nc.Block() as block:

        @block.tensor
        def _(pe):
            blocks_pe(pe, y, None)

        @block.scalar
        def _(act):
            for b in range(NB):
                spread_act(act, y, b, 0)

        @block.vector
        def _(dve):
            chain = Chain(dve, y.chain)
            diagonals(0, dinv).then_inc(y.diags, 1)
            for b, (lo, n) in enumerate(ADJ_BLOCKS):
                t0, x_b = temp[:, 0, 0:n], xT[:, lo:lo + n]
                scaled_dve(dve, y, b, dinv)
                dve.wait_ge(y.dve_done, b * y.dve + 1)
                chain.link(nc.vector.tensor_scalar(t0, t0, ew["b_gcn"][:], 0.0, ALU.add, ALU.max))
                nc.vector.tensor_tensor(x_b, x_b, t0, ALU.add).then_inc(y.dve_done, 1)

    norm("norm2", None)
    early.close()

    nodes = sb("nodes", [P, NT, D])
    weights = {k: sb("sb_" + k, list(t[k].shape)) for k in t if k.startswith(GAT_WEIGHTS)}
    src_cl = sb("src_cl", [P, CH], I32)
    dloc = sb("dloc", [P, CH + GROUP])
    scale = sb("scale", [P, CH + GROUP])
    wxx = [sb(f"wxx{l}", [din, dout + 2]) for l, (din, dout) in enumerate(LAYERS)]
    ae = [sb(f"ae{l}", [P, CH]) for l in range(len(LAYERS))]
    ae_mean = sb("ae_mean", [P, len(LAYERS)])
    base_row = sb("base_row", [1, CH], I32)
    ring = sb("ring", [P, max(s * dout for s, (_, dout) in zip(SLOTS, LAYERS))])
    idx = sb("idx", [P, max(SLOTS)], I32)
    hot = sb("hot", [P, max(BANKS) * GROUP, P])

    rows_landed = [sem(f"rows_landed{k}", True) for k in range(max(SLOTS) // GROUP)]
    idx_copied = sem("idx_copied", True)
    idx_seen = sem("idx_seen", True)
    hot_ready = sem("hot_ready", True)
    sum_ready = sem("sum_ready", True)
    sum_added = sem("sum_added", True)

    def gather(l, slot, index):
        width = LAYERS[l][1]
        nc.gpsimd.indirect_dma_start(
            out=ring[:, slot * width:(slot + 1) * width], out_offset=None, in_=h_tab[l],
            in_offset=bass.IndirectOffsetOnAxis(ap=index, axis=0)).then_inc(rows_landed[slot // GROUP], 16)

    def gather_ahead(l, first, last):
        for c in range(first, last):
            gather(l, c, src_cl[:, c:c + 1])

    def neighbour_sums(l, acc):
        width, slots, banks = LAYERS[l][1], SLOTS[l], BANKS[l]
        groups = slots // GROUP
        turn = slots // TURNS
        landed_before = sum(CH // s * 16 * GROUP for s in SLOTS[:l])
        copied_before = sum((CH // s - 1) * TURNS for s in SLOTS[:l])
        sums_before = l * (CH // GROUP)
        hots_before = l * (CH + GROUP)
        added_before = l * CH + sum(BANKS[:l]) * GROUP

        with nc.Block() as block:

            @block.gpsimd
            def _(pool):
                gather_ahead(l, min(AHEAD_SOFT, slots), slots)
                with pool.Fori(0, CH // slots - 1) as i:
                    for k in range(TURNS):
                        pool.wait_ge(sum_ready, i * groups + (sums_before + (k + 1) * turn // GROUP))
                        nc.gpsimd.tensor_copy(
                            idx[:, k * turn:(k + 1) * turn], src_cl[:, bass.ds(i * slots + (slots + k * turn), turn)]
                        ).then_inc(idx_copied, 1)
                        pool.wait_ge(idx_copied, i * TURNS + (copied_before + k + 1))
                        pool.sem_inc(idx_seen, 1)
                        for c in range(k * turn, (k + 1) * turn):
                            gather(l, c, idx[:, c:c + 1])

            @block.tensor
            def _(pe):
                with pe.Fori(0, CH // slots) as i:
                    for g in range(groups):
                        pe.wait_ge(rows_landed[g], i * (16 * GROUP) + (landed_before + 16 * GROUP))
                        pe.wait_ge(hot_ready, i * slots + (hots_before + (g + 1) * GROUP))
                        pe.wait_ge(sum_added, i * slots + (added_before + (g + 1) * GROUP))
                        for k in range(GROUP):
                            c = g * GROUP + k
                            last = nc.tensor.matmul(psum[0:width, g % banks, k * P:(k + 1) * P],
                                                    lhsT=ring[:, c * width:(c + 1) * width],
                                                    rhs=hot[:, g % banks * GROUP + k, :], start=True, stop=True)
                        last.then_inc(sum_ready, 1)

            @block.vector
            def _(dve):
                dve.sem_inc(sum_added, banks * GROUP)

                def one_hot(c, place):
                    nc.vector.tensor_scalar(hot[:, place, :], iota_row[:], dloc[:, bass.ds(c, 1)],
                                            scale[:, bass.ds(c, 1)], ALU.is_equal, ALU.mult
                                            ).then_inc(hot_ready, 1)

                for c in range(GROUP):
                    one_hot(c, c)
                with dve.Fori(0, CH // (banks * GROUP)) as i:
                    for g in range(banks):
                        c = i * (banks * GROUP) + g * GROUP
                        _, bases = nc.values_load_multi_w_load_instructions(
                            base_row[0:1, bass.ds(c, GROUP)], engines=(mybir.EngineType.DVE,),
                            min_val=0, max_val=N)
                        for k, base in enumerate(bases):
                            one_hot(c + (GROUP + k), (g + 1) % banks * GROUP + k)
                            if k == 0:
                                dve.wait_ge(sum_ready, i * banks + (sums_before + g + 1))
                            dve.wait_ge(sum_added, c + (added_before + banks * GROUP + k))
                            window = acc[0:width, 0, bass.ds(base, P)]
                            nc.vector.tensor_tensor(window, window, psum[0:width, g, k * P:(k + 1) * P],
                                                    ALU.add).then_inc(sum_added, 1)

    end_phase()
    loaded = sem("gat_loaded")
    v0 = sem("v0")
    with ExitStack() as stack:
        dst_cl = stack.enter_context(nc.sbuf_tensor("gat_dst_cl", [P, CH], I32))
        base_cl = stack.enter_context(nc.sbuf_tensor("base_cl", [P, CH], I32))
        src_sl = stack.enter_context(nc.sbuf_tensor("gat_src_sl", [P, CH], I32))
        lo_sl = stack.enter_context(nc.sbuf_tensor("lo_sl", [P, CH], I32))
        lo_bf = stack.enter_context(nc.sbuf_tensor("lo_bf", [P, CH], BF16))
        with nc.Block() as block:
            loads = len(weights) + 5
            lo_ready = sem("lo_ready")
            lo_stored = sem("lo_stored")

            @block.sync
            def _(sp):
                for dst, src in ((src_cl[:], t["src_cl"]), (dst_cl[:], t["dst_cl"]),
                                 (base_cl[:], t["base"].partition_broadcast(P)),
                                 (src_sl[:], t["src_sl"]), (base_row[:], t["base"].rearrange("(a n) -> a n", a=1))):
                    sp.dma_start(dst, src).then_inc(loaded, 16)
                for k, w in weights.items():
                    sp.dma_start(w[:], t[k]).then_inc(loaded, 16)
                sp.wait_ge(lo_ready, 1)
                sp.dma_start(e_lo.rearrange("(p n) -> p n", p=P), lo_bf[:]).then_inc(lo_stored, 16)
                sp.wait_ge(lo_stored, 16)

            @block.vector
            def _(dve):
                nc.vector.memset(scale[:], 1.0)
                nc.vector.memset(dloc[:, CH:CH + GROUP], -1.0)
                dve.wait_ge(loaded, 16 * loads)
                nc.vector.tensor_tensor(dloc[:, 0:CH], dst_cl[:], base_cl[:], ALU.subtract)
                chain = Chain(dve, v0)
                chain.link(nc.vector.tensor_single_scalar(lo_sl[:], src_sl[:], P - 1, ALU.bitwise_and))
                nc.vector.tensor_copy(lo_bf[:], lo_sl[:]).then_inc(lo_ready, 1)


    end_phase()
    mm, dv, ch = sem("edge_mm"), sem("edge_dv"), sem("edge_chain")
    PART = CH // ITERS * 2
    with ExitStack() as stack:
        attr = stack.enter_context(nc.sbuf_tensor("attr", [P, 2, PART, EDIM], F32))
        prod = stack.enter_context(nc.sbuf_tensor("prod", [P, PART, EDIM], F32))
        we_ae = stack.enter_context(nc.sbuf_tensor("we_ae", [P, len(LAYERS), EDIM], F32))
        ae_rep = stack.enter_context(nc.sbuf_tensor("ae_rep", [P, len(LAYERS), P], F32))
        sums = stack.enter_context(nc.sbuf_tensor("sums", [P, len(LAYERS)], F32))
        blocks = [(a, min(PART, CH - a)) for a in range(0, CH, PART)]
        with nc.Block() as block:
            attr_landed = [sem(f"attr_landed{k}") for k in range(2)]
            attr_used = sem("attr_used")

            @block.sync
            def _(sp):
                for j, (a, n) in enumerate(blocks):
                    if j >= 2:
                        sp.wait_ge(attr_used, j - 1)
                    sp.dma_start(attr[:, j % 2, 0:n, :], t["attr"][:, a:a + n, :]).then_inc(attr_landed[j % 2], 16)

            @block.tensor
            def _(pe):
                pe.wait_ge(dv, 1)
                for l, (din, dout) in enumerate(LAYERS):
                    nc.tensor.matmul(psum[0:din, l, 0:2], lhsT=weights[f"w_gatT{l}"][:],
                                     rhs=weights[f"w_a{l}"][:], start=True, stop=True)
                    nc.tensor.matmul(psum[:, 3 + l, 0:EDIM], lhsT=ae_rep[0:dout, l, :],
                                     rhs=weights[f"w_eT{l}"][:], start=True, stop=True).then_inc(mm, 1)
                pe.wait_ge(dv, 2)
                nc.tensor.matmul(psum[:, 7, 0:len(LAYERS)], lhsT=ones[:], rhs=sums[:], start=True, stop=True
                                 ).then_inc(mm, 1)

            @block.vector
            def _(dve):
                chain = Chain(dve, ch)
                for l, (din, dout) in enumerate(LAYERS):
                    last = nc.vector.tensor_scalar(ae_rep[0:dout, l, :], ones[0:dout, :],
                                                   weights[f"w_ae{l}"][:], None, ALU.mult)
                last.then_inc(dv, 1)
                for l, (din, dout) in enumerate(LAYERS):
                    dve.wait_ge(mm, l + 1)
                    nc.vector.tensor_copy(wxx[l][:, 0:dout], weights[f"w_gat{l}"][:])
                    nc.vector.tensor_copy(wxx[l][:, dout:dout + 2], psum[0:din, l, 0:2])
                    chain.link(nc.vector.tensor_copy(we_ae[:, l, :], psum[:, 3 + l, 0:EDIM]))
                for j, (a, n) in enumerate(blocks):
                    dve.wait_ge(attr_landed[j % 2], 16 * (j // 2 + 1))
                    for l in range(len(LAYERS)):
                        chain.link(nc.vector.tensor_tensor(
                            prod[:, 0:n, :], attr[:, j % 2, 0:n, :],
                            we_ae[:, l, None, :].to_broadcast([P, n, EDIM]), ALU.mult))
                        chain.link(nc.vector.tensor_reduce(ae[l][:, a:a + n], prod[:, 0:n, :], AX, ALU.add))
                    nc.vector.sem_inc(attr_used, 1)
                for l in range(len(LAYERS)):
                    chain.link(nc.vector.tensor_reduce(sums[:, l:l + 1], ae[l][:], AX, ALU.add))
                nc.vector.sem_inc(dv, 1)
                dve.wait_ge(mm, len(LAYERS) + 1)
                nc.vector.tensor_scalar(ae_mean[:], psum[:, 7, 0:len(LAYERS)], 1.0 / E, None,
                                        ALU.mult).then_inc(dv, 1)

    def norm_pe(pe, mm, dv, ac, m, d, w2, w3):
        for b, (lo, n) in enumerate(BLOCKS):
            pe.wait_ge(dv, ev(d, b))
            nc.tensor.matmul(psum[:, b, 0:n], lhsT=mean_m[:], rhs=w2[:, lo:lo + n],
                             start=True, stop=True).then_inc(mm, 1)
        for b, (lo, n) in enumerate(BLOCKS):
            pe.wait_ge(ac["sq"], b + 1)
            nc.tensor.matmul(psum[:, b, 0:n], lhsT=mean_m[:], rhs=w3[:, lo:lo + n],
                             start=True, stop=True).then_inc(mm, 1)
        for b, (lo, n) in enumerate(BLOCKS):
            pe.wait_ge(dv, ev(d + 2, b))
            for k in range(n // P):
                last = nc.tensor.transpose(psum[:, b, k * P:(k + 1) * P], xT[:, lo + k * P:lo + (k + 1) * P],
                                           ident[:])
            last.then_inc(mm, 1)

    def norm_dve(dve, mm, dv, ac, m, chain, w2, w3):
        for b, (lo, n) in enumerate(BLOCKS):
            s = slice(lo, lo + n)
            dve.wait_ge(mm, ev(m, b))
            nc.vector.tensor_tensor(w1[:, s], w2[:, s], psum[:, b, 0:n], ALU.subtract).then_inc(dv, 1)
        for b, (lo, n) in enumerate(BLOCKS):
            s = slice(lo, lo + n)
            dve.wait_ge(ac["std"], b + 1)
            chain.link(nc.vector.reciprocal(w3[:, s], w3[:, s]))
            nc.vector.tensor_tensor(xT[:, s], w1[:, s], w3[:, s], ALU.mult).then_inc(dv, 1)

    def norm_act(act, mm, dv, ac, m, d, w3):
        for b, (lo, n) in enumerate(BLOCKS):
            act.wait_ge(dv, ev(d + 1, b))
            nc.scalar.activation(w3[:, lo:lo + n], w1[:, lo:lo + n], ACT.Square).then_inc(ac["sq"], 1)
        for b, (lo, n) in enumerate(BLOCKS):
            act.wait_ge(mm, ev(m + 1, b))
            nc.scalar.activation(w3[:, lo:lo + n], psum[:, b, 0:n], ACT.Sqrt,
                                 bias=eps_col[:]).then_inc(ac["std"], 1)
        take_nodes(act, mm, ac, m + 2)

    def take_nodes(act, mm, ac, m):
        for b, (lo, n) in enumerate(BLOCKS):
            act.wait_ge(mm, ev(m, b))
            nc.scalar.copy(nodes[:, lo // P:(lo + n) // P, :].rearrange("p t d -> p (t d)"),
                           psum[:, b, 0:n]).then_inc(ac["nodes"], 1)

    def phase_sems(name):
        return (sem(name + "_mm"), sem(name + "_dv"), sem(name + "_chain"), sem(name + "_stored"),
                {k: sem(f"{name}_{k}") for k in ("gate", "sq", "std", "nodes")})

    GROUPS = [(g, min(P, CH - g)) for g in range(0, CH, P)]

    def prefix_pe(pe, s, number):
        col, crow = s["col"], s["crow"]
        pe.wait_ge(s["state"], number + 1)
        nc.tensor.matmul(psum[0:1, 7, 0:P], lhsT=col[:], rhs=ident[:], start=True, stop=True
                         ).then_inc(s["row"], 1)
        pe.wait_ge(s["starts_row"], number + 1)
        at = s["at"][number]
        nc.tensor.matmul(psum[:, 7, P:P + 1], lhsT=crow[0:1, at:at + P], rhs=one_col[0:1, :],
                         start=True, stop=True).then_inc(s["starts"], 1)

    def prefix_dve(dve, s, number, chain, out_, link, data, back=False, largest=False):
        op0, op1 = (ALU.add, ALU.max) if largest else (ALU.mult, ALU.add)
        first = -BIG if largest else 0.0
        links_row = {(False, False): 0, (False, True): 1, (True, False): 2, (True, True): 3}[back, largest]
        crow, link_rows, col, start_col = s["crow"], s["link_rows"], s["col"], s["start_col"]
        turn = slice(None, None, -1) if back else slice(None)
        chain.link(nc.vector.tensor_tensor_scan(out_[:, turn], link[:, turn], data[:, turn], first, op0, op1))
        end = 0 if back else CH - 1
        chain.link(nc.vector.memset(crow[:], first))
        nc.vector.tensor_copy(col[:], out_[:, end:end + 1]).then_inc(s["state"], 1)
        dve.wait_ge(s["row"], number + 1)
        nc.vector.tensor_tensor_scan(crow[0:1, 1:P + 1][:, turn], link_rows[0:1, links_row, :][:, turn],
                                     psum[0:1, 7, 0:P][:, turn], first, op0, op1).then_inc(s["starts_row"], 1)
        dve.wait_ge(s["starts"], number + 1)
        chain.link(nc.vector.tensor_copy(start_col[:], psum[:, 7, P:P + 1]))
        chain.link(nc.vector.tensor_tensor_scan(out_[:, turn], link[:, turn], data[:, turn],
                                                start_col[:], op0, op1))

    acc = sb("gat_acc", [P, 1, ACCW])
    gat = ExitStack()

    def gb(name, shape, dt=F32):
        return gat.enter_context(nc.sbuf_tensor(name, shape, dt))

    same = gb("same", [P, CH], BF16)
    same_next = gb("same_next", [P, CH], BF16)
    pen = gb("pen", [P, CH], BF16)
    pen_next = gb("pen_next", [P, CH], BF16)
    last_of = gb("last_of", [P, CH], BF16)
    hi_hot = gb("hi_hot", [P, CH, NT], U8)
    link_rows = gb("link_rows", [1, 4, P])
    crow = gb("crow", [1, P + 2])
    col = gb("col", [P, 1])
    start_col = gb("start_col", [P, 1])
    ends = gb("ends", [P, 4])
    scan_sems = {k: sem("prefix_" + k, True) for k in ("state", "row", "starts_row", "starts")}
    scan_sems |= {"crow": crow, "link_rows": link_rows, "col": col, "start_col": start_col}
    scan_sems["at"] = [0, 0, 0, 2, 0, 2] * len(LAYERS)

    end_phase()
    mm, dv, ch, stored, ac = phase_sems("gat_setup")
    with ExitStack() as stack, nc.Block() as block:
        dst_sl = stack.enter_context(nc.sbuf_tensor("dst_sl", [P, CH], I32))
        before_sl = stack.enter_context(nc.sbuf_tensor("before_sl", [P, CH], I32))
        after_sl = stack.enter_context(nc.sbuf_tensor("after_sl", [P, CH], I32))
        hi_cl = stack.enter_context(nc.sbuf_tensor("hi_cl", [P, CH], I32))
        hi_f = stack.enter_context(nc.sbuf_tensor("hi_f", [P, CH], F32))
        zero2 = stack.enter_context(nc.sbuf_tensor("zero2", [P, 2 * (CH + 1)], F32))
        landed = sem("gat_edges_landed")
        zeroed = sem("gat_zeroed")
        cleared = sem("gat_cleared")

        @block.sync
        def _(sp):
            for to, of in ((dst_sl, "dst_sl"), (before_sl, "dst_before"), (after_sl, "dst_after")):
                sp.dma_start(to[:], t[of]).then_inc(landed, 16)
            sp.wait_ge(zeroed, 1)
            sp.dma_start(e_first.rearrange("(p n) two -> p (n two)", p=P), zero2[:]).then_inc(cleared, 16)
            sp.dma_start(e_self.rearrange("(p n) one -> p (n one)", p=P), zero2[:, 0:CH + 1]).then_inc(cleared, 16)
            sp.wait_ge(cleared, 32)

        @block.vector
        def _(dve):
            chain = Chain(dve, ch)
            nc.vector.memset(zero2[:], 0.0).then_inc(zeroed, 1)
            dve.wait_ge(landed, 48)
            for links, pens, other in ((same, pen, before_sl), (same_next, pen_next, after_sl)):
                chain.link(nc.vector.tensor_tensor(links[:], dst_sl[:], other[:], ALU.is_equal))
                chain.link(nc.vector.tensor_scalar(pens[:], links[:], -1.0, BIG, ALU.add, ALU.mult))
            chain.link(nc.vector.tensor_scalar(last_of[:], same_next[:], -1.0, -1.0, ALU.add, ALU.mult))
            for n, links in enumerate((same, pen, same_next, pen_next)):
                chain.link(nc.vector.tensor_reduce(ends[:, n:n + 1], links[:], AX, ALU.min))
            nc.vector.tensor_copy(col[:], ends[:, 0:1]).then_inc(dv, 1)
            for n in range(4):
                dve.wait_ge(mm, n + 1)
                chain.link(nc.vector.tensor_copy(link_rows[0:1, n, :], psum[0:1, n + 1, 0:P]))
            chain.link(nc.vector.tensor_single_scalar(hi_cl[:], src_cl[:], 7, ALU.arith_shift_right))
            chain.link(nc.vector.tensor_copy(hi_f[:], hi_cl[:]))
            nc.vector.tensor_tensor(hi_hot[:], iota_row[:, None, 0:NT].to_broadcast([P, CH, NT]),
                                    hi_f[:, :, None].to_broadcast([P, CH, NT]), ALU.is_equal).then_inc(dv, 1)

        @block.tensor
        def _(pe):
            pe.wait_ge(dv, 1)
            for n in range(4):
                nc.tensor.matmul(psum[0:1, n + 1, 0:P], lhsT=ends[:, n:n + 1], rhs=ident[:],
                                 start=True, stop=True).then_inc(mm, 1)

    as_cl = gb("as_cl", [P, CH])
    score = gb("score", [P, CH])
    self_e = gb("self_e", [P, CH])
    top = gb("top", [P, CH])
    den = gb("den", [P, CH])
    asad = gb("asad", [P, NT, 2])
    node_vals = gb("node_vals", [P, NT, 2])
    self_n = gb("self_n", [P, NT])
    as_parts = gb("as_parts", [P, 3, NT], BF16)
    as_rest = gb("as_rest", [P, NT])

    for l, (din, dout) in enumerate(LAYERS):
        inp = xT if l == 0 else acc[:, 0, :]
        wx, b_l = weights[f"w_gat{l}"], weights[f"b_gat{l}"]

        end_phase()
        mm, dv, ch, stored, ac = phase_sems(f"gat{l}_rows")
        with nc.Block() as block:
            scattered = sem(f"gat{l}_scattered")

            @block.tensor
            def _(pe):
                for k in range(NT):
                    if k >= 7:
                        pe.wait_ge(ac["nodes"], k - 6)
                        pe.wait_ge(dv, k - 6)
                    nc.tensor.matmul(psum[:, k % 7, 0:dout + 2], lhsT=inp[0:din, k * P:(k + 1) * P],
                                     rhs=wxx[l][:], start=True, stop=True).then_inc(mm, 1)

            @block.scalar
            def _(act):
                for k in range(NT):
                    act.wait_ge(dv, k + 1)
                    nc.scalar.copy(nodes[:, k, 0:dout], psum[:, k % 7, 0:dout]).then_inc(ac["nodes"], 1)

            @block.vector
            def _(dve):
                chain = Chain(dve, ch)
                for k in range(NT):
                    dve.wait_ge(mm, k + 1)
                    nc.vector.tensor_copy(asad[:, k, :], psum[:, k % 7, dout:dout + 2]).then_inc(dv, 1)
                dve.wait_ge(dv, NT)
                chain.link(nc.vector.tensor_copy(node_vals[:, :, 0], asad[:, :, 1]))
                chain.link(nc.vector.scalar_tensor_tensor(self_n[:], asad[:, :, 0], ae_mean[:, l:l + 1],
                                                          asad[:, :, 1], ALU.add, ALU.add))
                nc.vector.scalar_tensor_tensor(node_vals[:, :, 1], self_n[:], SLOPE, self_n[:],
                                               ALU.mult, ALU.max).then_inc(dv, 1)
                chain.link(nc.vector.tensor_copy(as_parts[:, 0, :], asad[:, :, 0]))
                chain.link(nc.vector.tensor_tensor(as_rest[:], asad[:, :, 0], as_parts[:, 0, :], ALU.subtract))
                chain.link(nc.vector.tensor_copy(as_parts[:, 1, :], as_rest[:]))
                chain.link(nc.vector.tensor_tensor(as_parts[:, 2, :], as_rest[:], as_parts[:, 1, :], ALU.subtract))

            @block.sync
            def _(sp):
                sp.wait_ge(ac["nodes"], NT)
                sp.dma_start(h_tab[l].rearrange("(t p) d -> p t d", p=P), nodes[:, :, 0:dout]
                             ).then_inc(stored, 16)
                sp.wait_ge(stored, 16)

            @block.gpsimd
            def _(pool):
                pool.wait_ge(dv, NT + 1)
                for k in range(NT):
                    nc.gpsimd.indirect_dma_start(
                        out=e_first, out_offset=bass.IndirectOffsetOnAxis(ap=first_pos[:, k:k + 1], axis=0),
                        in_=node_vals[:, k, :], in_offset=None).then_inc(scattered, 16)
                pool.wait_ge(scattered, 16 * NT)

        end_phase()
        with ExitStack() as stack, nc.Block() as block:
            lo_rep = stack.enter_context(nc.sbuf_tensor(f"lo_rep{l}", [P, 4, HALF * P], BF16))
            lo_hot = stack.enter_context(nc.sbuf_tensor(f"lo_hot{l}", [P, 2, HALF * P], BF16))
            picked = top[:, 0:HALF * NT].rearrange("p (c h) -> p c h", c=HALF)
            lo_landed = [sem(f"gat{l}_lo_landed{k}") for k in range(4)]
            lo_used = sem(f"gat{l}_lo_used")
            table_rows = sem(f"gat{l}_table_rows")
            rows_used = sem(f"gat{l}_rows_used")
            summed = sem(f"gat{l}_summed")
            TIMES = CH // (4 * HALF)

            @block.sync
            def _(sp):
                with sp.Fori(0, TIMES) as i:
                    for k in range(4):
                        sp.wait_ge(lo_used, i * 4 + (k + 1))
                        sp.dma_start(lo_rep[:, k, :], e_lo[bass.ds(i * (4 * HALF * P) + k * HALF * P, HALF * P)]
                                     .partition_broadcast(P)).then_inc(lo_landed[k], 16)

            @block.gpsimd
            def _(pool):
                gather_ahead(l, 0, AHEAD_PICK)

            @block.vector
            def _(dve):
                dve.sem_inc(lo_used, 4)
                dve.sem_inc(summed, 1)

                def one_hot(k):
                    nc.vector.tensor_scalar(lo_hot[:, k % 2, :], lo_rep[:, k % 4, :], part_id[:], None,
                                            ALU.is_equal).then_inc(lo_used, 1)

                def pick(n, k):
                    dve.wait_ge(table_rows, n * 4 + (k + 1))
                    dve.wait_ge(summed, n * 4 + (k + 1))
                    c = n * (4 * HALF) + k * HALF
                    nc.vector.tensor_tensor(
                        picked, psum[:, k % 2, 0:HALF * NT].rearrange("p (c h) -> p c h", c=HALF),
                        hi_hot[:, bass.ds(c, HALF), :], ALU.mult).then_inc(rows_used, 1)
                    dve.wait_ge(rows_used, n * 4 + (k + 3))
                    nc.vector.tensor_reduce(as_cl[:, bass.ds(c, HALF)], picked, AX, ALU.add
                                            ).then_inc(summed, 1)

                dve.wait_ge(lo_landed[0], 16)
                one_hot(0)
                with dve.Fori(0, TIMES - 1) as i:
                    for k in range(4):
                        dve.wait_ge(lo_landed[(k + 1) % 4], i * 16 + (32 if k == 3 else 16))
                        one_hot(k + 1)
                        pick(i, k)
                for k in range(4):
                    if k < 3:
                        dve.wait_ge(lo_landed[k + 1], 16 * TIMES)
                        one_hot(k + 1)
                    pick(TIMES - 1, k)

            @block.tensor
            def _(pe):
                pe.sem_inc(rows_used, 2)
                with pe.Fori(0, TIMES) as i:
                    for k in range(4):
                        pe.wait_ge(lo_used, i * 4 + (k + 5))
                        pe.wait_ge(rows_used, i * 4 + (k + 1))
                        for c in range(HALF):
                            for part in range(3):
                                last = nc.tensor.matmul(psum[:, k % 2, c * NT:(c + 1) * NT],
                                                        lhsT=lo_hot[:, k % 2, c * P:(c + 1) * P],
                                                        rhs=as_parts[:, part, :],
                                                        start=part == 0, stop=part == 2)
                        last.then_inc(table_rows, 1)

        end_phase()
        mm, dv, ch, stored, ac = phase_sems(f"gat{l}_soft")
        with ExitStack() as stack, nc.Block() as block:
            efirst = stack.enter_context(nc.sbuf_tensor(f"efirst{l}", [P, CH, 2], F32))
            by_chunk = stack.enter_context(nc.sbuf_tensor(f"by_chunk{l}", [P, len(GROUPS), P], F32))
            diag = stack.enter_context(nc.sbuf_tensor(f"diag{l}", [P, 4, P], F32))
            as_landed = sem(f"gat{l}_as_landed")
            first_landed = sem(f"gat{l}_first_landed")
            coef_landed = sem(f"gat{l}_coef_landed")
            exped = sem(f"gat{l}_exped")
            self_got = sem(f"gat{l}_self_got")

            def chunk_rows(array):
                return [(g // P, n, array[g * P:(g + n) * P].rearrange("(c e) -> c e", e=P))
                        for g, n in GROUPS]

            @block.tensor
            def _(pe):
                for g, n in GROUPS:
                    nc.tensor.transpose(psum[0:n, g // P, 0:P], as_cl[:, g:g + n], ident[:]).then_inc(mm, 1)
                for s in range(6):
                    prefix_pe(pe, scan_sems, 6 * l + s)
                pe.wait_ge(coef_landed, 16 * len(GROUPS))
                for g, n in GROUPS:
                    nc.tensor.transpose(psum[:, g // P, 0:n], by_chunk[0:n, g // P, :], ident[0:n, 0:n]
                                        ).then_inc(mm, 1)
                for k in range(NT):
                    pe.wait_ge(dv, 4 + 2 * len(GROUPS) + k)
                    nc.tensor.matmul(psum[0:dout, k % 4, 0:P], lhsT=nodes[:, k, 0:dout], rhs=diag[:, k % 4, :],
                                     start=True, stop=True).then_inc(ac["gate"], 1)

            @block.sync
            def _(sp):
                sp.dma_start(efirst[:].rearrange("p n two -> p (n two)"),
                             e_first[0:EP, :].rearrange("(p n) two -> p (n two)", p=P)
                             ).then_inc(first_landed, 16)
                sp.wait_ge(dv, len(GROUPS))
                for g, n, rows_ in chunk_rows(e_as):
                    sp.dma_start(rows_, by_chunk[0:n, g, :]).then_inc(stored, 16)
                sp.wait_ge(stored, 16 * len(GROUPS))
                sp.dma_start(score[:], e_as.rearrange("(p n) -> p n", p=P)).then_inc(as_landed, 16)
                sp.wait_ge(dv, len(GROUPS) + 2)
                sp.dma_start(e_coef.rearrange("(p n) -> p n", p=P), score[:]).then_inc(stored, 16)
                sp.wait_ge(dv, len(GROUPS) + 3)
                sp.dma_start(e_self[0:EP, :].rearrange("(p n) one -> p (n one)", p=P), self_e[:]
                             ).then_inc(stored, 16)
                sp.wait_ge(stored, 16 * (len(GROUPS) + 2))
                for g, n, rows_ in chunk_rows(e_coef):
                    sp.dma_start(by_chunk[0:n, g, :], rows_).then_inc(coef_landed, 16)

            @block.gpsimd
            def _(pool):
                gather_ahead(l, AHEAD_PICK, min(AHEAD_SOFT, SLOTS[l]))
                pool.wait_ge(stored, 16 * (len(GROUPS) + 2))
                for k in range(NT):
                    nc.gpsimd.indirect_dma_start(
                        out=self_n[:, k:k + 1], out_offset=None, in_=e_self,
                        in_offset=bass.IndirectOffsetOnAxis(ap=first_pos[:, k:k + 1], axis=0)
                    ).then_inc(self_got, 16)

            @block.scalar
            def _(act):
                act.wait_ge(dv, len(GROUPS) + 1)
                nc.scalar.activation(score[:], score[:], ACT.Exp).then_inc(exped, 1)
                nc.scalar.activation(self_e[:], self_e[:], ACT.Exp).then_inc(exped, 1)

            @block.vector
            def _(dve):
                chain = Chain(dve, ch)
                for g, n in GROUPS:
                    dve.wait_ge(mm, g // P + 1)
                    nc.vector.tensor_copy(by_chunk[0:n, g // P, :], psum[0:n, g // P, 0:P]).then_inc(dv, 1)
                dve.wait_ge(first_landed, 16)
                prefix_dve(dve, scan_sems, 6 * l, chain, den, same, efirst[:, :, 0])
                prefix_dve(dve, scan_sems, 6 * l + 1, chain, self_e, same, efirst[:, :, 1])
                dve.wait_ge(as_landed, 16)
                chain.link(nc.vector.tensor_tensor(den[:], den[:], ae[l][:], ALU.add))
                chain.link(nc.vector.tensor_tensor(score[:], score[:], den[:], ALU.add))
                chain.link(nc.vector.scalar_tensor_tensor(score[:], score[:], SLOPE, score[:],
                                                          ALU.mult, ALU.max))
                chain.link(nc.vector.tensor_tensor(den[:], score[:], self_e[:], ALU.max))
                prefix_dve(dve, scan_sems, 6 * l + 2, chain, top, pen, den, largest=True)
                prefix_dve(dve, scan_sems, 6 * l + 3, chain, den, pen_next, top, back=True, largest=True)
                chain.link(nc.vector.tensor_tensor(score[:], score[:], den[:], ALU.subtract))
                nc.vector.tensor_tensor(self_e[:], self_e[:], den[:], ALU.subtract).then_inc(dv, 1)
                dve.wait_ge(exped, 2)
                prefix_dve(dve, scan_sems, 6 * l + 4, chain, top, same, score)
                chain.link(nc.vector.tensor_tensor(top[:], top[:], last_of[:], ALU.mult))
                prefix_dve(dve, scan_sems, 6 * l + 5, chain, den, same_next, top, back=True)
                chain.link(nc.vector.tensor_tensor(den[:], den[:], self_e[:], ALU.add))
                chain.link(nc.vector.reciprocal(den[:], den[:]))
                nc.vector.tensor_tensor(score[:], score[:], den[:], ALU.mult).then_inc(dv, 1)
                nc.vector.tensor_tensor(self_e[:], self_e[:], den[:], ALU.mult).then_inc(dv, 1)
                for g, n in GROUPS:
                    dve.wait_ge(mm, len(GROUPS) + g // P + 1)
                    nc.vector.tensor_copy(scale[:, g:g + n], psum[:, g // P, 0:n]).then_inc(dv, 1)
                dve.wait_ge(self_got, 16 * NT)
                nc.vector.memset(acc[:, 0, NP:ACCW], 0.0)
                for k in range(NT + 2):
                    if k < NT:
                        nc.vector.tensor_scalar(diag[:, k % 4, :], ident[:], self_n[:, k:k + 1], None,
                                                ALU.mult).then_inc(dv, 1)
                    if k >= 2:
                        dve.wait_ge(ac["gate"], k - 1)
                        nc.vector.tensor_copy(acc[0:dout, 0, (k - 2) * P:(k - 1) * P],
                                              psum[0:dout, (k - 2) % 4, 0:P]).then_inc(ch, 1)

        neighbour_sums(l, acc)

        if l < len(LAYERS) - 1:
            relu_done = sem(f"gat{l}_relu")
            with nc.Block() as block:

                @block.vector
                def _(dve):
                    nc.vector.tensor_scalar(acc[0:dout, 0, 0:NP], acc[0:dout, 0, 0:NP], b_l[:], 0.0,
                                            ALU.add, ALU.max).then_inc(relu_done, 1)


    gat.close()
    w1, w2, w3 = (sb(f"last_w{k}", [P, NP]) for k in (1, 2, 3))
    end_phase()
    mm, dv, ch, stored, ac = phase_sems("last")
    with nc.Block() as block:

        @block.tensor
        def _(pe):
            norm_pe(pe, mm, dv, ac, 0, 0, w2, w3)

        @block.vector
        def _(dve):
            chain = Chain(dve, ch)
            for b, (lo, n) in enumerate(BLOCKS):
                s = slice(lo, lo + n)
                chain.link(nc.vector.scalar_tensor_tensor(w2[:, s], acc[:, 0, s], b_l[:], xT[:, s],
                                                          ALU.add, ALU.add))
                nc.vector.tensor_tensor(w2[:, s], w2[:, s], xT[:, s], ALU.add).then_inc(dv, 1)
            norm_dve(dve, mm, dv, ac, 0, chain, w2, w3)

        @block.scalar
        def _(act):
            norm_act(act, mm, dv, ac, 0, 0, w3)

        @block.sync
        def _(sp):
            sp.wait_ge(ac["nodes"], NB)
            full = N // P
            sp.dma_start(out[0:full * P, :].rearrange("(t p) d -> p t d", p=P), nodes[:, 0:full, :]
                         ).then_inc(stored, 16)
            sp.dma_start(out[full * P:N, :], nodes[0:N - full * P, full, :]).then_inc(stored, 16)
            sp.wait_ge(stored, 32)


def kernel(**inputs):
    import numpy as np
    import concourse.bacc as bacc
    from concourse.bass_utils import run_bass_kernel_spmd

    i = {k: np.asarray(v) for k, v in inputs.items()}
    src = np.concatenate([i["src"], np.zeros(EP - E, np.int32)])
    pad = np.full(EP - E, N, np.int32)
    dst = np.concatenate([i["dst"], pad])
    arrays = {
        "x": i["x"], "xT": i["x"].T,
        "src_cl": src.reshape(CH, P).T, "dst_cl": dst.reshape(CH, P).T, "base": dst[::P], "quad_base": dst[::4 * P], "quad_last": dst[4 * P - 1::4 * P],
        "src_sl": src.reshape(P, CH), "dst_sl": dst.reshape(P, CH),
        "dst_before": np.concatenate([np.full(1, -1, np.int32), dst[:-1]]).reshape(P, CH),
        "dst_after": np.concatenate([dst[1:], np.full(1, -1, np.int32)]).reshape(P, CH),
        "attr": np.concatenate([i["edge_attr_16"], np.zeros((EP - E, EDIM), np.float32)]).reshape(P, CH, EDIM),
        "w_src": i["L0_gnn_W_src"].T, "b_src": i["L0_gnn_b_src"][:, None],
        "w_fc": i["L0_gnn_W_fc"].T.reshape(2, D, D).transpose(1, 0, 2).reshape(D, 2 * D),
        "b_fc": i["L0_gnn_b_fc"][:, None],
        "w_in": i["L1_gnn_W_in"].T, "b_in": i["L1_gnn_b_in"][:, None],
        "w_out": i["L1_gnn_W_out"].T, "b_out": i["L1_gnn_b_out"][:, None],
        "w_ih": i["L1_gnn_w_ih"].T.reshape(2, D, 3 * D).transpose(1, 0, 2),
        "w_hh": i["L1_gnn_w_hh"].T,
        "b_ih": i["L1_gnn_b_ih"].reshape(3, D).T, "b_hh": i["L1_gnn_b_hh"].reshape(3, D).T,
        "w_gcn": i["L2_gnn_weight"], "b_gcn": i["L2_gnn_bias"][:, None],
    }
    for l in range(len(LAYERS)):
        arrays[f"w_gat{l}"] = i[f"L3_gnn_W{l + 1}"]
        arrays[f"w_gatT{l}"] = i[f"L3_gnn_W{l + 1}"].T
        arrays[f"w_a{l}"] = np.stack([i[f"L3_gnn_as{l + 1}"], i[f"L3_gnn_ad{l + 1}"]], 1)
        arrays[f"w_eT{l}"] = i[f"L3_gnn_We{l + 1}"].T
        arrays[f"w_ae{l}"] = i[f"L3_gnn_ae{l + 1}"][:, None]
        arrays[f"b_gat{l}"] = i[f"L3_gnn_b{l + 1}"][:, None]
    arrays = {k: np.ascontiguousarray(v) for k, v in arrays.items()}

    nc = bacc.Bacc("TRN2", target_bir_lowering=False, num_devices=1)
    aps = {k: nc.dram_tensor("in_" + k, v.shape, mybir.dt.from_np(v.dtype), kind="ExternalInput").ap()
           for k, v in arrays.items()}
    out = nc.dram_tensor("out", (N, D), F32, kind="ExternalOutput").ap()
    gnn_kernel(nc, aps, out)
    r = run_bass_kernel_spmd(nc, [{"in_" + k: v for k, v in arrays.items()}], core_ids=[0])
    return r.results[0]["out"]
```

```python
from contextlib import ExitStack

import concourse.bass as bass
from concourse import mybir

P = 128
N = 3125
NT = -(-N // P)
NP = NT * P
E = 103125
HALF = 12
BODY = 2 * HALF
CH = -(-E // (P * BODY)) * BODY
EP = CH * P
ITERS = CH // BODY
ACCW = NP + P
BLOCKS = [(b, min(512, NP - b)) for b in range(0, NP, 512)]
NB = len(BLOCKS)
D = 128
EDIM = 16
LAYERS = [(128, 80), (80, 80), (80, 128)]
WIDE = 80
SLOPE = 0.2
EPS = 1e-5
QUADS = CH // 4
RING = BODY // 4
WIN = 20
KEYS = NT * WIN
AW = N + WIN + 1
ADJ_BLOCKS = [(b, min(n, 64)) if b + 512 > NP else (b, n) for b, n in BLOCKS]
ADJ_END = sum(ADJ_BLOCKS[-1])
GAT_WEIGHTS = ("w_gat", "b_gat", "w_a", "w_eT")
BIG = 1e30
LEAD = 8
GROUP = 4
TURNS = 17
SLOTS = 204
BANKS = 3
AHEAD_PICK = 84
AHEAD_SOFT = 140
assert KEYS <= 512 and N <= ADJ_END <= AW and RING % 2 == 0
assert CH == ITERS * BODY
assert CH % SLOTS == 0 and SLOTS % (GROUP * TURNS) == 0 and SLOTS // GROUP % BANKS == 0

F32 = mybir.dt.float32
I32 = mybir.dt.int32
BF16 = mybir.dt.bfloat16
U8 = mybir.dt.uint8
F16 = mybir.dt.float16
ALU = mybir.AluOpType
ACT = mybir.ActivationFunctionType
AX = mybir.AxisListType.X


def ev(step, block):
    return NB * step + block + 1


class Chain:

    def __init__(self, engine, sem):
        self.engine, self.sem, self.n = engine, sem, 0

    def link(self, ins):
        self.n += 1
        ins.then_inc(self.sem, 1)
        self.engine.wait_ge(self.sem, self.n)


def gnn_kernel(nc, t, out):
    def sb(name, shape, dt=F32):
        return nc.alloc_sbuf_tensor(name, shape, dt)

    phase_own = []

    def sem(name, kept=False):
        made = nc.alloc_semaphore(name)
        if not kept:
            phase_own.append(made)
        return made

    def end_phase():
        nc.clear_and_free_semaphores(list(phase_own))
        phase_own.clear()
        nc.all_engine_barrier()

    def dram(name, shape, dt=F32):
        return nc.dram_tensor(name, shape, dt, kind="Internal").ap()

    h_tab = [dram(f"h_tab{l}", [NP, WIDE]) for l in range(len(LAYERS))]
    e_first = dram("e_first", [EP + P, 2])
    e_as = dram("e_as", [EP])
    e_coef = dram("e_coef", [EP])
    e_self = dram("e_self", [EP + P, 1])
    e_lo = dram("e_lo", [EP], BF16)

    xT = sb("xT", [P, NP])
    ident = sb("ident", [P, P])
    ident_bf = sb("ident_bf", [P, P], BF16)
    iota_row = sb("iota_row", [P, P])
    part_id = sb("part_id", [P, 1])
    ones = sb("ones", [P, P])
    ones_bf = sb("ones_bf", [P, 1], BF16)
    mean_m = sb("mean_m", [P, P])
    eps_col = sb("eps_col", [P, 1])
    one_col = sb("one_col", [P, 1])
    first_pos = sb("first_pos", [P, NT], I32)
    rdeg = sb("rdeg", [P, NT])
    dinv = sb("dinv", [P, NT])
    psum = nc.alloc_psum_tensor("psum", [P, 8, 512], F32)

    consts = sem("consts")
    with nc.Block() as block:

        @block.gpsimd
        def _(pool):
            nc.gpsimd.memset(ident[:], 0.0).then_inc(consts, 1)
            pool.wait_ge(consts, 1)
            nc.gpsimd.affine_select(out=ident[:], in_=ident[:], compare_op=ALU.not_equal, fill=1.0,
                                    base=0, pattern=[[-1, P]], channel_multiplier=1)
            nc.gpsimd.memset(ident_bf[:], 0.0).then_inc(consts, 1)
            pool.wait_ge(consts, 2)
            nc.gpsimd.affine_select(out=ident_bf[:], in_=ident_bf[:], compare_op=ALU.not_equal, fill=1.0,
                                    base=0, pattern=[[-1, P]], channel_multiplier=1)
            nc.gpsimd.iota(iota_row[:], [[1, P]], base=0, channel_multiplier=0,
                           allow_small_or_imprecise_dtypes=True)
            nc.gpsimd.iota(part_id[:], [[0, 1]], base=0, channel_multiplier=1,
                           allow_small_or_imprecise_dtypes=True)
            nc.gpsimd.memset(ones[:], 1.0)
            nc.gpsimd.memset(mean_m[:], 1.0 / D)
            nc.gpsimd.memset(eps_col[:], EPS)
            nc.gpsimd.memset(one_col[:], 1.0)
            nc.gpsimd.memset(ones_bf[:], 1.0)

    early = ExitStack()

    def eb(name, shape, dt=F32):
        return early.enter_context(nc.sbuf_tensor(name, shape, dt))

    adj = eb("adj", [P, NT, AW], BF16)

    end_phase()
    with ExitStack() as stack:
        def bb(name, shape, dt=F32):
            return stack.enter_context(nc.sbuf_tensor(name, shape, dt))

        src_i = bb("src_i", [P, CH], I32)
        dst_i = bb("dst_i", [P, CH], I32)
        base_i = bb("base_i", [P, QUADS], I32)
        lo_f = bb("lo_f", [P, CH + 4])
        hi_f = bb("adj_hi", [P, CH], BF16)
        valid = bb("valid", [P, CH], BF16)
        place = bb("place", [P, CH])
        key = bb("key", [P, CH + 4])
        q_base = bb("q_base", [1, QUADS], I32)
        q_last = bb("q_last", [1, QUADS], I32)
        span = bb("span", [1, QUADS])
        steps = bb("steps", [1, N // WIN])
        passes_f = bb("passes_f", [1, 1])
        passes_i = bb("passes_i", [1, 1], I32)
        iota_key = bb("iota_key", [P, KEYS], F16)
        lo_off = bb("adj_lo_off", [P, 2, 4 * P], BF16)
        lo_hot = bb("adj_lo_hot", [P, 2, 4 * P], BF16)
        key_hot = bb("adj_key_hot", [P, 8, KEYS], BF16)

        loaded = sem("adj_loaded")
        iotas = sem("adj_iotas")
        ready = sem("adj_ready")
        pass_ready = sem("adj_pass_ready")
        keys_made = sem("adj_keys_made")
        lo_off_made = sem("adj_lo_off_made")
        lo_made = sem("adj_lo_made")
        counted = sem("adj_counted")
        added = sem("adj_added")
        ch = sem("adj_chain")

        with nc.Block() as block:

            @block.sync
            def _(sp):
                for to, of in ((src_i[:], t["src_cl"]), (dst_i[:], t["dst_cl"]),
                               (base_i[:], t["quad_base"].partition_broadcast(P)),
                               (q_base[:], t["quad_base"].rearrange("(a n) -> a n", a=1)),
                               (q_last[:], t["quad_last"].rearrange("(a n) -> a n", a=1))):
                    sp.dma_start(to, of).then_inc(loaded, 16)

            @block.gpsimd
            def _(pool):
                nc.gpsimd.iota(iota_key[:], [[1, KEYS]], base=0, channel_multiplier=0,
                               allow_small_or_imprecise_dtypes=True).then_inc(iotas, 1)
                nc.gpsimd.iota(steps[:], [[WIN, N // WIN]], base=WIN, channel_multiplier=0,
                               allow_small_or_imprecise_dtypes=True).then_inc(iotas, 1)
                nc.gpsimd.memset(adj[:, 0:NT // 2, :].rearrange("p h n -> p (h n)").bitcast(I32), 0
                                 ).then_inc(iotas, 1)

            @block.vector
            def _(dve):
                chain = Chain(dve, ch)
                half = NT // 2
                nc.vector.memset(adj[:, half:NT, :].rearrange("p h n -> p (h n)").bitcast(I32), 0)
                nc.vector.memset(key[:, CH:CH + 4], -1.0)
                nc.vector.memset(lo_f[:, CH:CH + 4], 0.0)
                dve.wait_ge(loaded, 16 * 5)
                chain.link(nc.vector.tensor_tensor(
                    place[:].rearrange("p (q k) -> p q k", k=4), dst_i[:].rearrange("p (q k) -> p q k", k=4),
                    base_i[:, :, None].to_broadcast([P, QUADS, 4]), ALU.subtract))
                chain.link(nc.vector.tensor_single_scalar(dst_i[:], src_i[:], P - 1, ALU.bitwise_and))
                chain.link(nc.vector.tensor_scalar(lo_f[:, 0:CH], dst_i[:], -1.0, None, ALU.mult))
                chain.link(nc.vector.tensor_single_scalar(dst_i[:], src_i[:], 7, ALU.arith_shift_right))
                chain.link(nc.vector.tensor_copy(hi_f[:], dst_i[:]))
                chain.link(nc.vector.tensor_scalar(span[:], q_last[:], float(N - 1), None, ALU.min))
                chain.link(nc.vector.tensor_tensor(span[:], span[:], q_base[:], ALU.subtract))
                chain.link(nc.vector.tensor_reduce(passes_f[:], span[:], AX, ALU.max))
                dve.wait_ge(iotas, 3)
                chain.link(nc.vector.tensor_scalar(steps[:], steps[:], passes_f[:], None, ALU.is_le))
                chain.link(nc.vector.tensor_reduce(passes_f[:], steps[:], AX, ALU.add))
                chain.link(nc.vector.tensor_scalar(passes_i[:], passes_f[:], 1.0, None, ALU.add))
                dve.sem_inc(ready, 1)
                passes = dve.value_load(passes_i[0:1, 0:1], min_val=1, max_val=N // WIN + 1)

                def key_hot_of(c, k):
                    nc.vector.tensor_scalar(key_hot[:, k % 8, :], iota_key[:], key[:, bass.ds(c, 1)], None,
                                            ALU.is_equal).then_inc(keys_made, 1)

                def lo_hot_of(j, place):
                    dve.wait_ge(lo_off_made, s * (4 * QUADS + 4) + j * 4 + 4)
                    nc.vector.tensor_scalar(lo_hot[:, place, :], lo_off[:, place, :], 0.0, None,
                                            ALU.is_equal).then_inc(lo_made, 1)

                dve.sem_inc(lo_made, 2)
                dve.sem_inc(added, RING)
                dve.sem_inc(pass_ready, 1)
                with dve.Fori(0, passes) as s:
                    def after(ins, n):
                        ins.then_inc(pass_ready, 1)
                        dve.wait_ge(pass_ready, s * 7 + (n + 2))
                    after(nc.vector.tensor_scalar(valid[:], place[:], 0.0, None, ALU.is_ge), 0)
                    after(nc.vector.scalar_tensor_tensor(valid[:], place[:], float(WIN), valid[:],
                                                         ALU.is_lt, ALU.mult), 1)
                    after(nc.vector.scalar_tensor_tensor(key[:, 0:CH], hi_f[:], float(WIN), place[:],
                                                         ALU.mult, ALU.add), 2)
                    after(nc.vector.scalar_tensor_tensor(key[:, 0:CH], key[:, 0:CH], 1.0, valid[:],
                                                         ALU.add, ALU.mult), 3)
                    after(nc.vector.tensor_scalar(key[:, 0:CH], key[:, 0:CH], -1.0, None, ALU.add), 4)
                    for c in range(4):
                        key_hot_of(c, c)
                    lo_hot_of(0, 0)
                    with dve.Fori(0, ITERS) as i:
                        _, bases = nc.values_load_multi_w_load_instructions(
                            q_base[0:1, bass.ds(i * RING, RING)], engines=(mybir.EngineType.DVE,),
                            min_val=0, max_val=AW - WIN)
                        for q in range(RING):
                            lo_hot_of(i * RING + (q + 1), (q + 1) % 2)
                            for k in range(4):
                                key_hot_of(i * BODY + (4 * q + k + 4), 4 * q + k + 4)
                            dve.wait_ge(counted, s * QUADS + i * RING + (q + 1 + RING))
                            dve.wait_ge(added, s * QUADS + i * RING + (q + RING))
                            window = adj[:, :, bass.ds(bases[q], WIN)]
                            nc.vector.tensor_tensor(window, window, psum[:, q, 0:KEYS].rearrange(
                                "p (h w) -> p h w", w=WIN), ALU.add).then_inc(added, 1)
                    after(nc.vector.tensor_scalar(place[:], place[:], -float(WIN), None, ALU.add), 5)
                    after(nc.vector.tensor_scalar(q_base[:], q_base[:], float(WIN), float(AW - WIN),
                                                  ALU.add, ALU.min), 6)

            @block.scalar
            def _(act):
                act.wait_ge(ready, 1)
                passes = act.value_load(passes_i[0:1, 0:1], min_val=1, max_val=N // WIN + 1)

                def offsets(c, place):
                    for k in range(4):
                        nc.scalar.activation(lo_off[:, place, k * P:(k + 1) * P], iota_key[:, 0:P], ACT.Abs,
                                             bias=lo_f[:, bass.ds(c + k, 1)]).then_inc(lo_off_made, 1)

                with act.Fori(0, passes) as s:
                    act.wait_ge(lo_made, s * (QUADS + 1) + 2)
                    offsets(0, 0)
                    with act.Fori(0, ITERS) as i:
                        for q in range(RING):
                            act.wait_ge(lo_made, s * (QUADS + 1) + i * RING + (q + 2))
                            offsets(i * BODY + (4 * q + 4), (q + 1) % 2)

            @block.tensor
            def _(pe):
                pe.wait_ge(ready, 1)
                passes = pe.value_load(passes_i[0:1, 0:1], min_val=1, max_val=N // WIN + 1)
                pe.sem_inc(counted, RING)
                with pe.Fori(0, passes) as s:
                    with pe.Fori(0, ITERS) as i:
                        for q in range(RING):
                            pe.wait_ge(lo_made, s * (QUADS + 1) + i * RING + (q + 3))
                            pe.wait_ge(added, s * QUADS + i * RING + (q + 1))
                            for k in range(4):
                                pe.wait_ge(keys_made, s * (CH + 4) + i * BODY + (4 * q + k + 1))
                                last = nc.tensor.matmul(psum[:, q, 0:KEYS], lhsT=lo_hot[:, q % 2, k * P:(k + 1) * P],
                                                        rhs=key_hot[:, (4 * q + k) % 8, :],
                                                        start=k == 0, stop=k == 3)
                            last.then_inc(counted, 1)

    end_phase()
    mm, dv, ch = sem("first_mm"), sem("first_dv"), sem("first_chain")
    with ExitStack() as stack, nc.Block() as block:
        deg_row = stack.enter_context(nc.sbuf_tensor("deg_row", [1, NP], F32))
        first_row = stack.enter_context(nc.sbuf_tensor("first_row", [1, NP], F32))
        dump = stack.enter_context(nc.sbuf_tensor("dump", [1, P], F32))
        dumped = sem("dumped")
        rooted = sem("rooted")

        @block.gpsimd
        def _(pool):
            nc.gpsimd.iota(dump[:], [[1, P]], base=EP, channel_multiplier=0,
                           allow_small_or_imprecise_dtypes=True).then_inc(dumped, 1)

        @block.tensor
        def _(pe):
            for b, (lo, n) in enumerate(ADJ_BLOCKS):
                for h in range(NT):
                    last = nc.tensor.matmul(psum[0:1, b, 0:n], lhsT=ones_bf[:, 0:1],
                                            rhs=adj[:, h, lo:lo + n], start=h == 0, stop=h == NT - 1)
                last.then_inc(mm, 1)
            pe.wait_ge(dv, NB + 1)
            for k in range(NT):
                nc.tensor.matmul(psum[:, 7, k:k + 1], lhsT=deg_row[0:1, k * P:(k + 1) * P],
                                 rhs=one_col[0:1, :], start=True, stop=True)
                last = nc.tensor.matmul(psum[:, 7, NT + k:NT + k + 1], lhsT=first_row[0:1, k * P:(k + 1) * P],
                                        rhs=one_col[0:1, :], start=True, stop=True)
            last.then_inc(mm, 1)

        @block.vector
        def _(dve):
            chain = Chain(dve, ch)
            chain.link(nc.vector.memset(deg_row[:, ADJ_END:NP], 0.0))
            chain.link(nc.vector.memset(first_row[:], 1.0))
            for b, (lo, n) in enumerate(ADJ_BLOCKS):
                dve.wait_ge(mm, b + 1)
                nc.vector.tensor_copy(deg_row[:, lo:lo + n], psum[0:1, b, 0:n]).then_inc(dv, 1)
            dve.wait_ge(dv, NB)
            chain.link(nc.vector.tensor_tensor_scan(first_row[:], first_row[:], deg_row[:], 0.0,
                                                    ALU.mult, ALU.add))
            chain.link(nc.vector.tensor_tensor(first_row[:], first_row[:], deg_row[:], ALU.subtract))
            dve.wait_ge(dumped, 1)
            nc.vector.tensor_copy(first_row[:, N:NP], dump[:, 0:NP - N]).then_inc(dv, 1)
            dve.wait_ge(mm, NB + 1)
            nc.vector.tensor_copy(first_pos[:], psum[:, 7, NT:2 * NT])
            chain.link(nc.vector.tensor_scalar_max(rdeg[:], psum[:, 7, 0:NT], 1.0))
            chain.link(nc.vector.reciprocal(rdeg[:], rdeg[:]))
            nc.vector.tensor_scalar(dinv[:], psum[:, 7, 0:NT], 1.0, None, ALU.add).then_inc(dv, 1)
            dve.wait_ge(rooted, 1)
            nc.vector.reciprocal(dinv[:], dinv[:]).then_inc(dv, 1)

        @block.scalar
        def _(act):
            act.wait_ge(dv, NB + 2)
            nc.scalar.activation(dinv[:], dinv[:], ACT.Sqrt).then_inc(rooted, 1)

    ew = {k: eb("sb_" + k, list(t[k].shape)) for k in t
          if k.startswith(("w_", "b_")) and not k.startswith(GAT_WEIGHTS)}
    gate_b = eb("gate_b", [P, 3])
    parts = eb("parts", [P, 3, NT, D], BF16)
    temp = eb("temp", [P, 5, 512])
    diag = eb("adj_diag", [P, 4, P])
    SLICES = 6
    products = [(h, s) for h in range(NT) for s in range(3)]

    def neighbour_slice(b, k):
        lo, n = ADJ_BLOCKS[b]
        size = -(-len(products) // SLICES)
        for j, (h, s) in list(enumerate(products))[k * size:(k + 1) * size]:
            last = nc.tensor.matmul(psum[:, b % 2, 0:n], lhsT=parts[:, s, h, :], rhs=adj[:, h, lo:lo + n],
                                    start=j == 0, stop=j == len(products) - 1)
        return last

    def spread(b):
        lo, n = ADJ_BLOCKS[b]
        for k in range(0, n, P):
            m = min(P, n - k)
            last = nc.tensor.matmul(psum[:, 2, k:k + m], lhsT=ones[:], rhs=diag[:, k // P, 0:m],
                                    start=True, stop=True)
        return last

    def diagonals(b, value):
        lo, n = ADJ_BLOCKS[b]
        for k in range(0, n, P):
            last = nc.vector.tensor_scalar(diag[:, k // P, :], ident[:],
                                           value[:, lo // P + k // P:lo // P + k // P + 1], None, ALU.mult)
        return last

    def split_dve(dve, b, source, spare, chain):
        lo, n = BLOCKS[b]
        s = slice(lo // P, (lo + n) // P)
        first, second, third = (parts[:, k, s, :].rearrange("p t d -> p (t d)") for k in range(3))
        chain.link(nc.vector.tensor_tensor(spare, source, first, ALU.subtract))
        chain.link(nc.vector.tensor_copy(second, spare))
        return nc.vector.tensor_tensor(third, spare, second, ALU.subtract)

    def norm(name, after):
        end_phase()
        mean_done, var_done, node_done = sem(name + "_mean"), sem(name + "_var"), sem(name + "_node")
        centred, normed, split = sem(name + "_centred"), sem(name + "_normed"), sem(name + "_split")
        squared, rooted, first_part, ch = (sem(f"{name}_{k}") for k in ("squared", "rooted", "first", "chain"))
        with nc.Block() as block:

            @block.tensor
            def _(pe):
                for b, (lo, n) in enumerate(BLOCKS):
                    nc.tensor.matmul(psum[:, b, 0:n], lhsT=mean_m[:], rhs=xT[:, lo:lo + n],
                                     start=True, stop=True).then_inc(mean_done, 1)
                for b, (lo, n) in enumerate(BLOCKS):
                    pe.wait_ge(squared, b + 1)
                    nc.tensor.matmul(psum[:, b, 0:n], lhsT=mean_m[:], rhs=temp[:, b % 2, 0:n],
                                     start=True, stop=True).then_inc(var_done, 1)
                for b, (lo, n) in enumerate(BLOCKS):
                    if after is None:
                        break
                    pe.wait_ge(normed, b + 1)
                    for k in range(n // P):
                        to, of = psum[:, b, k * P:(k + 1) * P], xT[:, lo + k * P:lo + (k + 1) * P]
                        if after == "transpose":
                            last = nc.tensor.transpose(to, of, ident[:])
                        else:
                            last = nc.tensor.matmul(to, lhsT=of, rhs=ew["w_gcn"][:], start=True, stop=True)
                    last.then_inc(node_done, 1)

            @block.gpsimd
            def _(pool):
                for h in range(NT if after == "project" else 0):
                    own = adj[:, h, h * P:min(h * P + P, N)]
                    nc.gpsimd.tensor_tensor(own, own, ident_bf[:, 0:own.shape[-1]], ALU.add)

            @block.scalar
            def _(act):
                for b, (lo, n) in enumerate(BLOCKS):
                    act.wait_ge(centred, b + 1)
                    if b >= 2:
                        act.wait_ge(var_done, b - 1)
                    nc.scalar.activation(temp[:, b % 2, 0:n], xT[:, lo:lo + n], ACT.Square).then_inc(squared, 1)
                for b, (lo, n) in enumerate(BLOCKS):
                    act.wait_ge(var_done, b + 1)
                    if b >= 2:
                        act.wait_ge(normed, b - 1)
                    nc.scalar.activation(temp[:, 2 + b % 2, 0:n], psum[:, b, 0:n], ACT.Sqrt,
                                         bias=eps_col[:]).then_inc(rooted, 1)
                for b, (lo, n) in enumerate(BLOCKS):
                    if after is None:
                        break
                    act.wait_ge(node_done, b + 1)
                    if after == "project":
                        if b >= 2:
                            act.wait_ge(split, b - 1)
                        for k in range(n // P):
                            last = nc.scalar.activation(temp[:, b % 2, k * P:(k + 1) * P],
                                                        psum[:, b, k * P:(k + 1) * P], ACT.Copy,
                                                        scale=dinv[:, lo // P + k:lo // P + k + 1])
                        last.then_inc(squared, 1)
                        act.wait_ge(squared, NB + b + 1)
                        source = temp[:, b % 2, 0:n]
                    else:
                        source = psum[:, b, 0:n]
                    nc.scalar.copy(parts[:, 0, lo // P:(lo + n) // P, :].rearrange("p t d -> p (t d)"),
                                   source).then_inc(first_part, 1)

            @block.vector
            def _(dve):
                chain = Chain(dve, ch)
                for b, (lo, n) in enumerate(BLOCKS):
                    dve.wait_ge(mean_done, b + 1)
                    nc.vector.tensor_tensor(xT[:, lo:lo + n], xT[:, lo:lo + n], psum[:, b, 0:n], ALU.subtract
                                            ).then_inc(centred, 1)
                for b, (lo, n) in enumerate(BLOCKS):
                    std = temp[:, 2 + b % 2, 0:n]
                    dve.wait_ge(rooted, b + 1)
                    chain.link(nc.vector.reciprocal(std, std))
                    nc.vector.tensor_tensor(xT[:, lo:lo + n], xT[:, lo:lo + n], std, ALU.mult
                                            ).then_inc(normed, 1)
                for b, (lo, n) in enumerate(BLOCKS):
                    if after is None:
                        break
                    dve.wait_ge(first_part, b + 1)
                    source = psum[:, b, 0:n] if after == "transpose" else temp[:, b % 2, 0:n]
                    split_dve(dve, b, source, temp[:, 4, 0:n], chain).then_inc(split, 1)
                    dve.wait_ge(split, b + 1)

    end_phase()
    landed, weights_landed = sem("x_zeroed"), sem("weights_landed")
    first_part, split, ch = sem("x_first"), sem("x_split"), sem("x_chain")
    x_rows = [sem(f"x_rows{k}") for k in range(2)]
    with nc.Block() as block:
        full = N // P

        @block.sync
        def _(sp):
            for b, (lo, n) in enumerate(BLOCKS):
                if b >= 2:
                    sp.wait_ge(split, b - 1)
                to = temp[:, b % 2, 0:n].rearrange("p (t d) -> p t d", d=D)
                if b < NB - 1:
                    sp.dma_start(to, t["x"][lo:lo + n, :].rearrange("(t p) d -> p t d", p=P)
                                 ).then_inc(x_rows[b % 2], 16)
                else:
                    sp.wait_ge(landed, 1)
                    sp.dma_start(to[0:N - lo, 0, :], t["x"][lo:N, :]).then_inc(x_rows[b % 2], 16)

        @block.scalar
        def _(act):
            for k, w in ew.items():
                act.dma_start(w[:], t[k]).then_inc(weights_landed, 16)
            act.dma_start(xT[:, 0:N], t["xT"]).then_inc(weights_landed, 16)
            for b, (lo, n) in enumerate(BLOCKS):
                act.wait_ge(x_rows[b % 2], 16 * (b // 2 + 1))
                nc.scalar.copy(parts[:, 0, lo // P:(lo + n) // P, :].rearrange("p t d -> p (t d)"),
                               temp[:, b % 2, 0:n]).then_inc(first_part, 1)
            act.wait_ge(weights_landed, 16 * (len(ew) + 1))

        @block.gpsimd
        def _(pool):
            nc.gpsimd.memset(xT[:, N:NP], 0.0)

        @block.vector
        def _(dve):
            chain = Chain(dve, ch)
            for b, (lo, n) in enumerate(BLOCKS):
                if b == NB - 1:
                    dve.wait_ge(split, b - 1)
                    nc.vector.memset(temp[:, b % 2, 0:n], 0.0).then_inc(landed, 1)
                dve.wait_ge(first_part, b + 1)
                split_dve(dve, b, temp[:, b % 2, 0:n], temp[:, 4, 0:n], chain).then_inc(split, 1)
                dve.wait_ge(split, b + 1)

    class Layer:

        def __init__(self, name, pe, dve, act):
            self.pe, self.dve, self.act = pe, dve, act
            self.sums, self.spread, self.diags, self.chain = (
                sem(f"{name}_{k}") for k in ("sums", "spread", "diagonals", "chain"))
            self.pe_done, self.dve_done, self.act_done = (sem(f"{name}_{k}_done") for k in ("pe", "dve", "act"))

    def blocks_pe(pe, y, step):
        pe.wait_ge(y.diags, 1)
        spread(0).then_inc(y.spread, 1)
        for k in range(SLICES):
            last = neighbour_slice(0, k)
        last.then_inc(y.sums, 1)
        for b in range(NB):
            more = b + 1 < NB
            if more:
                pe.wait_ge(y.diags, b + 2)
                pe.wait_ge(y.act_done, b * y.act + 1)
                spread(b + 1).then_inc(y.spread, 1)
                if b >= 1:
                    pe.wait_ge(y.dve_done, (b - 1) * y.dve + 1)
            for k in range(SLICES):
                if k < y.pe:
                    step(b, k).then_inc(y.pe_done, 1)
                if more:
                    last = neighbour_slice(b + 1, k)
            if more:
                last.then_inc(y.sums, 1)

    def spread_act(act, y, b, behind):
        lo, n = ADJ_BLOCKS[b]
        act.wait_ge(y.spread, b + 1)
        if b >= 1:
            act.wait_ge(y.dve_done, (b - 1) * y.dve + behind + 1)
        nc.scalar.copy(temp[:, 4, 0:n], psum[:, 2, 0:n]).then_inc(y.act_done, 1)

    def scaled_dve(dve, y, b, value):
        lo, n = ADJ_BLOCKS[b]
        dve.wait_ge(y.sums, b + 1)
        dve.wait_ge(y.act_done, b * y.act + 1)
        if b >= 1:
            dve.wait_ge(y.dve_done, b * y.dve)
        nc.vector.tensor_tensor(temp[:, 0, 0:n], psum[:, b % 2, 0:n], temp[:, 4, 0:n], ALU.mult
                                ).then_inc(y.dve_done, 1)
        if b + 1 < NB:
            diagonals(b + 1, value).then_inc(y.diags, 1)

    end_phase()
    y = Layer("sage", 2, 2, 2)
    with nc.Block() as block:

        @block.tensor
        def _(pe):
            def step(b, k):
                lo, n = ADJ_BLOCKS[b]
                if k == 0:
                    pe.wait_ge(y.dve_done, b * y.dve + 1)
                    return nc.tensor.matmul(psum[:, 3, 0:n], lhsT=ew["w_src"][:], rhs=temp[:, 0, 0:n],
                                            start=True, stop=True)
                if b >= 1:
                    pe.wait_ge(y.dve_done, b * y.dve)
                pe.wait_ge(y.act_done, b * y.act + 2)
                nc.tensor.matmul(psum[:, 4, 0:n], lhsT=ew["w_fc"][:, 0:D], rhs=xT[:, lo:lo + n],
                                 start=True, stop=False)
                return nc.tensor.matmul(psum[:, 4, 0:n], lhsT=ew["w_fc"][:, D:2 * D], rhs=temp[:, 1, 0:n],
                                        start=False, stop=True)

            blocks_pe(pe, y, step)

        @block.scalar
        def _(act):
            for b, (lo, n) in enumerate(ADJ_BLOCKS):
                spread_act(act, y, b, 0)
                act.wait_ge(y.pe_done, b * y.pe + 1)
                nc.scalar.activation(temp[:, 1, 0:n], psum[:, 3, 0:n], ACT.Identity, bias=ew["b_src"][:]
                                     ).then_inc(y.act_done, 1)

        @block.vector
        def _(dve):
            diagonals(0, rdeg).then_inc(y.diags, 1)
            for b, (lo, n) in enumerate(ADJ_BLOCKS):
                scaled_dve(dve, y, b, rdeg)
                dve.wait_ge(y.pe_done, b * y.pe + 2)
                nc.vector.scalar_tensor_tensor(xT[:, lo:lo + n], psum[:, 4, 0:n], ew["b_fc"][:],
                                               xT[:, lo:lo + n], ALU.add, ALU.add).then_inc(y.dve_done, 1)

    norm("norm0", "transpose")

    end_phase()
    y = Layer("gru", 6, 4, 6)
    with nc.Block() as block:

        @block.tensor
        def _(pe):
            def step(b, k):
                lo, n = ADJ_BLOCKS[b]
                x_b, t0, t1, t2 = xT[:, lo:lo + n], temp[:, 0, 0:n], temp[:, 1, 0:n], temp[:, 2, 0:n]
                wi, wh = ew["w_ih"], ew["w_hh"]
                if k == 0:
                    pe.wait_ge(y.dve_done, b * y.dve + 1)
                if k < 2:
                    w = ew["w_in"] if k == 0 else ew["w_out"]
                    return nc.tensor.matmul(psum[:, 3 + k, 0:n], lhsT=w[:], rhs=t0, start=True, stop=True)
                if k == 2:
                    pe.wait_ge(y.act_done, b * y.act + 3)
                gate = {2: 0, 3: 1, 4: 2, 5: 2}[k]
                g = slice(gate * D, (gate + 1) * D)
                bank = {2: 5, 3: 6, 4: 7, 5: 3}[k]
                if k != 4:
                    nc.tensor.matmul(psum[:, bank, 0:n], lhsT=wi[:, 0, g], rhs=t1, start=True, stop=False)
                    last = nc.tensor.matmul(psum[:, bank, 0:n], lhsT=wi[:, 1, g], rhs=t2,
                                            start=False, stop=k == 5)
                if k != 5:
                    last = nc.tensor.matmul(psum[:, bank, 0:n], lhsT=wh[:, g], rhs=x_b,
                                            start=k == 4, stop=True)
                return last

            blocks_pe(pe, y, step)

        @block.scalar
        def _(act):
            act.wait_ge(y.chain, 1)
            for b, (lo, n) in enumerate(ADJ_BLOCKS):
                spread_act(act, y, b, 3)
                for k, bias in enumerate(("b_in", "b_out")):
                    act.wait_ge(y.pe_done, b * y.pe + k + 1)
                    nc.scalar.activation(temp[:, 1 + k, 0:n], psum[:, 3 + k, 0:n], ACT.Identity,
                                         bias=ew[bias][:]).then_inc(y.act_done, 1)
                for k in range(2):
                    act.wait_ge(y.pe_done, b * y.pe + 3 + k)
                    nc.scalar.activation(temp[:, 3 + k, 0:n], psum[:, 5 + k, 0:n], ACT.Sigmoid,
                                         bias=gate_b[:, k:k + 1]).then_inc(y.act_done, 1)
                act.wait_ge(y.dve_done, b * y.dve + 3)
                nc.scalar.activation(temp[:, 3, 0:n], temp[:, 3, 0:n], ACT.Tanh).then_inc(y.act_done, 1)

        @block.vector
        def _(dve):
            chain = Chain(dve, y.chain)
            chain.link(nc.vector.tensor_tensor(gate_b[:], ew["b_ih"][:], ew["b_hh"][:], ALU.add))
            diagonals(0, rdeg).then_inc(y.diags, 1)
            for b, (lo, n) in enumerate(ADJ_BLOCKS):
                t0, t3, t4, x_b = temp[:, 0, 0:n], temp[:, 3, 0:n], temp[:, 4, 0:n], xT[:, lo:lo + n]
                scaled_dve(dve, y, b, rdeg)
                dve.wait_ge(y.pe_done, b * y.pe + 5)
                dve.wait_ge(y.act_done, b * y.act + 5)
                nc.vector.scalar_tensor_tensor(t3, psum[:, 7, 0:n], ew["b_hh"][:, 2:3], t3,
                                               ALU.add, ALU.mult).then_inc(y.dve_done, 1)
                dve.wait_ge(y.pe_done, b * y.pe + 6)
                dve.wait_ge(y.dve_done, b * y.dve + 2)
                nc.vector.scalar_tensor_tensor(t3, psum[:, 3, 0:n], ew["b_ih"][:, 2:3], t3,
                                               ALU.add, ALU.add).then_inc(y.dve_done, 1)
                dve.wait_ge(y.act_done, b * y.act + 6)
                chain.link(nc.vector.tensor_tensor(t0, x_b, t3, ALU.subtract))
                chain.link(nc.vector.tensor_tensor(t0, t0, t4, ALU.mult))
                chain.link(nc.vector.tensor_tensor(t0, t0, t3, ALU.add))
                nc.vector.tensor_tensor(x_b, x_b, t0, ALU.add).then_inc(y.dve_done, 1)

    norm("norm1", "project")

    end_phase()
    y = Layer("gcn", 0, 2, 1)
    with nc.Block() as block:

        @block.tensor
        def _(pe):
            blocks_pe(pe, y, None)

        @block.scalar
        def _(act):
            for b in range(NB):
                spread_act(act, y, b, 0)

        @block.vector
        def _(dve):
            chain = Chain(dve, y.chain)
            diagonals(0, dinv).then_inc(y.diags, 1)
            for b, (lo, n) in enumerate(ADJ_BLOCKS):
                t0, x_b = temp[:, 0, 0:n], xT[:, lo:lo + n]
                scaled_dve(dve, y, b, dinv)
                dve.wait_ge(y.dve_done, b * y.dve + 1)
                chain.link(nc.vector.tensor_scalar(t0, t0, ew["b_gcn"][:], 0.0, ALU.add, ALU.max))
                nc.vector.tensor_tensor(x_b, x_b, t0, ALU.add).then_inc(y.dve_done, 1)

    norm("norm2", None)
    early.close()

    nodes = sb("nodes", [P, NT, D])
    weights = {k: sb("sb_" + k, list(t[k].shape)) for k in t if k.startswith(GAT_WEIGHTS)}
    src_cl = sb("src_cl", [P, CH + SLOTS // TURNS], I32)
    dloc = sb("dloc", [P, CH + LEAD])
    scale = sb("scale", [P, CH + LEAD])
    wxx = [sb(f"wxx{l}", [din, WIDE + 2]) for l, (din, dout) in enumerate(LAYERS)]
    ae = [sb(f"ae{l}", [P, CH]) for l in range(len(LAYERS))]
    ae_mean = sb("ae_mean", [P, len(LAYERS)])
    base_row = sb("base_row", [1, CH], I32)
    ring = sb("ring", [P, SLOTS, WIDE])
    idx = sb("idx", [P, SLOTS], I32)
    hot = sb("hot", [P, BANKS * GROUP, P])

    rows_landed = [sem(f"rows_landed{k}", True) for k in range(SLOTS // GROUP)]
    idx_copied = sem("idx_copied", True)
    idx_seen = sem("idx_seen", True)
    hot_ready = sem("hot_ready", True)
    sum_ready = sem("sum_ready", True)
    sum_added = sem("sum_added", True)

    def gather(l, slot, index):
        nc.gpsimd.indirect_dma_start(
            out=ring[:, slot, :], out_offset=None, in_=h_tab[l],
            in_offset=bass.IndirectOffsetOnAxis(ap=index, axis=0)).then_inc(rows_landed[slot // GROUP], 16)

    def gather_ahead(l, first, last):
        for c in range(first, last):
            gather(l, c, src_cl[:, c:c + 1])

    def neighbour_sums(l, acc):
        groups = SLOTS // GROUP
        turn = SLOTS // TURNS
        rounds = CH // SLOTS
        landed_before = l * rounds * 16 * GROUP
        copied_before = l * ((rounds - 1) * TURNS + 1)
        sums_before = l * (CH // GROUP)
        hots_before = l * (CH + LEAD)
        added_before = l * (CH + BANKS * GROUP)

        with nc.Block() as block:

            @block.gpsimd
            def _(pool):
                gather_ahead(l, AHEAD_SOFT, SLOTS)

                def take_index(i, k):
                    pool.wait_ge(sum_ready, i * groups + (sums_before + (k + 1) * turn // GROUP))
                    nc.gpsimd.tensor_copy(
                        idx[:, k % TURNS * turn:(k % TURNS + 1) * turn],
                        src_cl[:, bass.ds(i * SLOTS + (SLOTS + k * turn), turn)]).then_inc(idx_copied, 1)

                take_index(0, 0)
                with pool.Fori(0, rounds - 1) as i:
                    for k in range(TURNS):
                        take_index(i, k + 1)
                        pool.wait_ge(idx_copied, i * TURNS + (copied_before + k + 1))
                        pool.sem_inc(idx_seen, 1)
                        for c in range(k * turn, (k + 1) * turn):
                            gather(l, c, idx[:, c:c + 1])

            @block.tensor
            def _(pe):
                with pe.Fori(0, rounds) as i:
                    for g in range(groups):
                        pe.wait_ge(rows_landed[g], i * (16 * GROUP) + (landed_before + 16 * GROUP))
                        pe.wait_ge(hot_ready, i * SLOTS + (hots_before + (g + 1) * GROUP))
                        pe.wait_ge(sum_added, i * SLOTS + (added_before + (g + 1) * GROUP))
                        for k in range(GROUP):
                            c = g * GROUP + k
                            last = nc.tensor.matmul(psum[0:WIDE, g % BANKS, k * P:(k + 1) * P],
                                                    lhsT=ring[:, c, :],
                                                    rhs=hot[:, g % BANKS * GROUP + k, :], start=True, stop=True)
                        last.then_inc(sum_ready, 1)

            @block.vector
            def _(dve):
                dve.sem_inc(sum_added, BANKS * GROUP)

                def one_hot(c, place):
                    nc.vector.tensor_scalar(hot[:, place, :], iota_row[:], dloc[:, bass.ds(c, 1)],
                                            scale[:, bass.ds(c, 1)], ALU.is_equal, ALU.mult
                                            ).then_inc(hot_ready, 1)

                for c in range(LEAD):
                    one_hot(c, c)
                with dve.Fori(0, CH // (BANKS * GROUP)) as i:
                    for g in range(BANKS):
                        c = i * (BANKS * GROUP) + g * GROUP
                        _, bases = nc.values_load_multi_w_load_instructions(
                            base_row[0:1, bass.ds(c, GROUP)], engines=(mybir.EngineType.DVE,),
                            min_val=0, max_val=N)
                        for k, base in enumerate(bases):
                            one_hot(c + (LEAD + k), (g * GROUP + LEAD + k) % (BANKS * GROUP))
                            if k == 0:
                                dve.wait_ge(sum_ready, i * BANKS + (sums_before + g + 1))
                            dve.wait_ge(sum_added, c + (added_before + BANKS * GROUP + k))
                            window = acc[0:WIDE, 0, bass.ds(base, P)]
                            nc.vector.tensor_tensor(window, window, psum[0:WIDE, g, k * P:(k + 1) * P],
                                                    ALU.add).then_inc(sum_added, 1)

    end_phase()
    loaded = sem("gat_loaded")
    v0 = sem("v0")
    with ExitStack() as stack:
        dst_cl = stack.enter_context(nc.sbuf_tensor("gat_dst_cl", [P, CH], I32))
        base_cl = stack.enter_context(nc.sbuf_tensor("base_cl", [P, CH], I32))
        src_sl = stack.enter_context(nc.sbuf_tensor("gat_src_sl", [P, CH], I32))
        lo_sl = stack.enter_context(nc.sbuf_tensor("lo_sl", [P, CH], I32))
        lo_bf = stack.enter_context(nc.sbuf_tensor("lo_bf", [P, CH], BF16))
        with nc.Block() as block:
            loads = len(weights) + 5
            lo_ready = sem("lo_ready")
            lo_stored = sem("lo_stored")

            @block.sync
            def _(sp):
                for dst, src in ((src_cl[:, 0:CH], t["src_cl"]), (dst_cl[:], t["dst_cl"]),
                                 (base_cl[:], t["base"].partition_broadcast(P)),
                                 (src_sl[:], t["src_sl"]), (base_row[:], t["base"].rearrange("(a n) -> a n", a=1))):
                    sp.dma_start(dst, src).then_inc(loaded, 16)
                for k, w in weights.items():
                    sp.dma_start(w[:], t[k]).then_inc(loaded, 16)
                sp.wait_ge(lo_ready, 1)
                sp.dma_start(e_lo.rearrange("(p n) -> p n", p=P), lo_bf[:]).then_inc(lo_stored, 16)
                sp.wait_ge(lo_stored, 16)

            @block.vector
            def _(dve):
                nc.vector.memset(scale[:], 1.0)
                nc.vector.memset(src_cl[:, CH:], 0)
                nc.vector.memset(dloc[:, CH:CH + LEAD], -1.0)
                dve.wait_ge(loaded, 16 * loads)
                nc.vector.tensor_tensor(dloc[:, 0:CH], dst_cl[:], base_cl[:], ALU.subtract)
                chain = Chain(dve, v0)
                chain.link(nc.vector.tensor_single_scalar(lo_sl[:], src_sl[:], P - 1, ALU.bitwise_and))
                nc.vector.tensor_copy(lo_bf[:], lo_sl[:]).then_inc(lo_ready, 1)


    end_phase()
    mm, dv, ch = sem("edge_mm"), sem("edge_dv"), sem("edge_chain")
    GR = P // EDIM
    COLS = CH // GR
    PART = COLS // 6
    with ExitStack() as stack:
        attr = stack.enter_context(nc.sbuf_tensor("attr", [P, 2, PART, P], F32))
        we_rep = stack.enter_context(nc.sbuf_tensor("we_rep", [P, len(LAYERS), GR, EDIM], F32))
        own = stack.enter_context(nc.sbuf_tensor("own", [P, GR], F32))
        we_ae = stack.enter_context(nc.sbuf_tensor("we_ae", [P, len(LAYERS), GR], F32))
        sums = stack.enter_context(nc.sbuf_tensor("sums", [P, len(LAYERS)], F32))
        with nc.Block() as block:
            attr_landed = [sem(f"attr_landed{k}") for k in range(2)]
            masked = sem("attr_masked")

            @block.sync
            def _(sp):
                for j in range(6):
                    if j >= 2:
                        sp.wait_ge(mm, len(LAYERS) + j - 1)
                    sp.dma_start(attr[:, j % 2, :, :], t["attr"][:, j * PART:(j + 1) * PART, :]
                                 ).then_inc(attr_landed[j % 2], 16)

            @block.gpsimd
            def _(pool):
                nc.gpsimd.memset(own[:], 1.0).then_inc(masked, 1)
                pool.wait_ge(masked, 1)
                nc.gpsimd.affine_select(out=own[:], in_=own[:], compare_op=ALU.is_ge, fill=0.0, base=0,
                                        pattern=[[-EDIM, GR]], channel_multiplier=1).then_inc(masked, 1)
                pool.wait_ge(masked, 2)
                nc.gpsimd.affine_select(out=own[:], in_=own[:], compare_op=ALU.is_ge, fill=0.0, base=EDIM - 1,
                                        pattern=[[EDIM, GR]], channel_multiplier=-1).then_inc(masked, 1)

            @block.tensor
            def _(pe):
                pe.wait_ge(dv, 1)
                for l, (din, dout) in enumerate(LAYERS):
                    nc.tensor.matmul(psum[0:din, l, 0:2], lhsT=weights[f"w_gatT{l}"][:],
                                     rhs=weights[f"w_a{l}"][:], start=True, stop=True)
                    nc.tensor.matmul(psum[:, 3 + l, 0:1],
                                     lhsT=we_rep[0:dout, l, :, :].rearrange("p g d -> p (g d)"),
                                     rhs=weights[f"w_ae{l}"][:], start=True, stop=True).then_inc(mm, 1)
                pe.wait_ge(dv, 2)
                for j in range(6):
                    pe.wait_ge(attr_landed[j % 2], 16 * (j // 2 + 1))
                    for c in range(PART):
                        last = nc.tensor.matmul(
                            psum[:, j, c * len(LAYERS) * GR:(c + 1) * len(LAYERS) * GR], lhsT=attr[:, j % 2, c, :],
                            rhs=we_ae[:].rearrange("p l g -> p (l g)"), start=True, stop=True)
                    last.then_inc(mm, 1)
                pe.wait_ge(dv, 3)
                nc.tensor.matmul(psum[:, 7, 0:len(LAYERS)], lhsT=ones[:], rhs=sums[:], start=True, stop=True
                                 ).then_inc(mm, 1)

            @block.vector
            def _(dve):
                chain = Chain(dve, ch)
                for l, (din, dout) in enumerate(LAYERS):
                    last = nc.vector.tensor_copy(
                        we_rep[0:dout, l, :, :], weights[f"w_eT{l}"][:, None, :].to_broadcast([dout, GR, EDIM]))
                last.then_inc(dv, 1)
                dve.wait_ge(masked, 3)
                for l, (din, dout) in enumerate(LAYERS):
                    dve.wait_ge(mm, l + 1)
                    nc.vector.tensor_copy(wxx[l][:, 0:WIDE], weights[f"w_gat{l}"][:] if dout == WIDE
                                          else ident[0:WIDE, 0:WIDE])
                    nc.vector.tensor_copy(wxx[l][:, WIDE:WIDE + 2], psum[0:din, l, 0:2])
                    chain.link(nc.vector.tensor_scalar(we_ae[:, l, :], own[:], psum[:, 3 + l, 0:1], None, ALU.mult))
                nc.vector.sem_inc(dv, 1)
                for j in range(6):
                    dve.wait_ge(mm, len(LAYERS) + j + 1)
                    for l in range(len(LAYERS)):
                        chain.link(nc.vector.tensor_copy(
                            ae[l][:, j * PART * GR:(j + 1) * PART * GR].rearrange("p (c g) -> p c g", g=GR),
                            psum[:, j, 0:PART * len(LAYERS) * GR].rearrange(
                                "p (c l g) -> p l c g", l=len(LAYERS), g=GR)[:, l]))
                for l in range(len(LAYERS)):
                    chain.link(nc.vector.tensor_reduce(sums[:, l:l + 1], ae[l][:], AX, ALU.add))
                nc.vector.sem_inc(dv, 1)
                dve.wait_ge(mm, len(LAYERS) + 7)
                nc.vector.tensor_scalar(ae_mean[:], psum[:, 7, 0:len(LAYERS)], 1.0 / E, None,
                                        ALU.mult).then_inc(dv, 1)

    def norm_pe(pe, mm, dv, ac, m, d, w2, w3):
        for b, (lo, n) in enumerate(BLOCKS):
            pe.wait_ge(dv, ev(d, b))
            nc.tensor.matmul(psum[:, b, 0:n], lhsT=mean_m[:], rhs=w2[:, lo:lo + n],
                             start=True, stop=True).then_inc(mm, 1)
        for b, (lo, n) in enumerate(BLOCKS):
            pe.wait_ge(ac["sq"], b + 1)
            nc.tensor.matmul(psum[:, b, 0:n], lhsT=mean_m[:], rhs=w3[:, lo:lo + n],
                             start=True, stop=True).then_inc(mm, 1)
        for b, (lo, n) in enumerate(BLOCKS):
            pe.wait_ge(dv, ev(d + 2, b))
            for k in range(n // P):
                last = nc.tensor.transpose(psum[:, b, k * P:(k + 1) * P], xT[:, lo + k * P:lo + (k + 1) * P],
                                           ident[:])
            last.then_inc(mm, 1)

    def norm_dve(dve, mm, dv, ac, m, chain, w2, w3):
        for b, (lo, n) in enumerate(BLOCKS):
            s = slice(lo, lo + n)
            dve.wait_ge(mm, ev(m, b))
            nc.vector.tensor_tensor(w1[:, s], w2[:, s], psum[:, b, 0:n], ALU.subtract).then_inc(dv, 1)
        for b, (lo, n) in enumerate(BLOCKS):
            s = slice(lo, lo + n)
            dve.wait_ge(ac["std"], b + 1)
            chain.link(nc.vector.reciprocal(w3[:, s], w3[:, s]))
            nc.vector.tensor_tensor(xT[:, s], w1[:, s], w3[:, s], ALU.mult).then_inc(dv, 1)

    def norm_act(act, mm, dv, ac, m, d, w3):
        for b, (lo, n) in enumerate(BLOCKS):
            act.wait_ge(dv, ev(d + 1, b))
            nc.scalar.activation(w3[:, lo:lo + n], w1[:, lo:lo + n], ACT.Square).then_inc(ac["sq"], 1)
        for b, (lo, n) in enumerate(BLOCKS):
            act.wait_ge(mm, ev(m + 1, b))
            nc.scalar.activation(w3[:, lo:lo + n], psum[:, b, 0:n], ACT.Sqrt,
                                 bias=eps_col[:]).then_inc(ac["std"], 1)
        take_nodes(act, mm, ac, m + 2)

    def take_nodes(act, mm, ac, m):
        for b, (lo, n) in enumerate(BLOCKS):
            act.wait_ge(mm, ev(m, b))
            nc.scalar.copy(nodes[:, lo // P:(lo + n) // P, :].rearrange("p t d -> p (t d)"),
                           psum[:, b, 0:n]).then_inc(ac["nodes"], 1)

    def phase_sems(name):
        return (sem(name + "_mm"), sem(name + "_dv"), sem(name + "_chain"), sem(name + "_stored"),
                {k: sem(f"{name}_{k}") for k in ("gate", "sq", "std", "nodes")})

    GROUPS = [(g, min(P, CH - g)) for g in range(0, CH, P)]

    def prefix_pe(pe, s, number):
        col, crow = s["col"], s["crow"]
        pe.wait_ge(s["state"], number + 1)
        nc.tensor.matmul(psum[0:1, 7, 0:P], lhsT=col[:], rhs=ident[:], start=True, stop=True
                         ).then_inc(s["row"], 1)
        pe.wait_ge(s["starts_row"], number + 1)
        at = s["at"][number]
        nc.tensor.matmul(psum[:, 7, P:P + 1], lhsT=crow[0:1, at:at + P], rhs=one_col[0:1, :],
                         start=True, stop=True).then_inc(s["starts"], 1)

    def prefix_dve(dve, s, number, chain, out_, link, data, back=False, largest=False):
        op0, op1 = (ALU.add, ALU.max) if largest else (ALU.mult, ALU.add)
        first = -BIG if largest else 0.0
        links_row = {(False, False): 0, (False, True): 1, (True, False): 2, (True, True): 3}[back, largest]
        crow, link_rows, col, start_col = s["crow"], s["link_rows"], s["col"], s["start_col"]
        turn = slice(None, None, -1) if back else slice(None)
        chain.link(nc.vector.tensor_tensor_scan(out_[:, turn], link[:, turn], data[:, turn], first, op0, op1))
        end = 0 if back else CH - 1
        chain.link(nc.vector.memset(crow[:], first))
        nc.vector.tensor_copy(col[:], out_[:, end:end + 1]).then_inc(s["state"], 1)
        dve.wait_ge(s["row"], number + 1)
        nc.vector.tensor_tensor_scan(crow[0:1, 1:P + 1][:, turn], link_rows[0:1, links_row, :][:, turn],
                                     psum[0:1, 7, 0:P][:, turn], first, op0, op1).then_inc(s["starts_row"], 1)
        dve.wait_ge(s["starts"], number + 1)
        chain.link(nc.vector.tensor_copy(start_col[:], psum[:, 7, P:P + 1]))
        chain.link(nc.vector.tensor_tensor_scan(out_[:, turn], link[:, turn], data[:, turn],
                                                start_col[:], op0, op1))

    acc = sb("gat_acc", [P, 1, ACCW])
    gat = ExitStack()

    def gb(name, shape, dt=F32):
        return gat.enter_context(nc.sbuf_tensor(name, shape, dt))

    same = gb("same", [P, CH], BF16)
    same_next = gb("same_next", [P, CH], BF16)
    pen = gb("pen", [P, CH], BF16)
    pen_next = gb("pen_next", [P, CH], BF16)
    last_of = gb("last_of", [P, CH], BF16)
    hi_hot = gb("hi_hot", [P, CH, NT], U8)
    link_rows = gb("link_rows", [1, 4, P])
    crow = gb("crow", [1, P + 2])
    col = gb("col", [P, 1])
    start_col = gb("start_col", [P, 1])
    ends = gb("ends", [P, 4])
    scan_sems = {k: sem("prefix_" + k, True) for k in ("state", "row", "starts_row", "starts")}
    scan_sems |= {"crow": crow, "link_rows": link_rows, "col": col, "start_col": start_col}
    scan_sems["at"] = [0, 0, 0, 2, 0, 2] * len(LAYERS)

    end_phase()
    mm, dv, ch, stored, ac = phase_sems("gat_setup")
    with ExitStack() as stack, nc.Block() as block:
        dst_sl = stack.enter_context(nc.sbuf_tensor("dst_sl", [P, CH], I32))
        before_sl = stack.enter_context(nc.sbuf_tensor("before_sl", [P, CH], I32))
        after_sl = stack.enter_context(nc.sbuf_tensor("after_sl", [P, CH], I32))
        hi_cl = stack.enter_context(nc.sbuf_tensor("hi_cl", [P, CH], I32))
        hi_f = stack.enter_context(nc.sbuf_tensor("hi_f", [P, CH], F32))
        zero2 = stack.enter_context(nc.sbuf_tensor("zero2", [P, 2 * (CH + 1)], F32))
        landed = sem("gat_edges_landed")
        zeroed = sem("gat_zeroed")
        cleared = sem("gat_cleared")

        @block.sync
        def _(sp):
            for to, of in ((dst_sl, "dst_sl"), (before_sl, "dst_before"), (after_sl, "dst_after")):
                sp.dma_start(to[:], t[of]).then_inc(landed, 16)
            sp.wait_ge(zeroed, 1)
            sp.dma_start(e_first.rearrange("(p n) two -> p (n two)", p=P), zero2[:]).then_inc(cleared, 16)
            sp.dma_start(e_self.rearrange("(p n) one -> p (n one)", p=P), zero2[:, 0:CH + 1]).then_inc(cleared, 16)
            sp.wait_ge(cleared, 32)

        @block.vector
        def _(dve):
            chain = Chain(dve, ch)
            nc.vector.memset(zero2[:], 0.0).then_inc(zeroed, 1)
            dve.wait_ge(landed, 48)
            for links, pens, other in ((same, pen, before_sl), (same_next, pen_next, after_sl)):
                chain.link(nc.vector.tensor_tensor(links[:], dst_sl[:], other[:], ALU.is_equal))
                chain.link(nc.vector.tensor_scalar(pens[:], links[:], -1.0, BIG, ALU.add, ALU.mult))
            chain.link(nc.vector.tensor_scalar(last_of[:], same_next[:], -1.0, -1.0, ALU.add, ALU.mult))
            for n, links in enumerate((same, pen, same_next, pen_next)):
                chain.link(nc.vector.tensor_reduce(ends[:, n:n + 1], links[:], AX, ALU.min))
            nc.vector.tensor_copy(col[:], ends[:, 0:1]).then_inc(dv, 1)
            for n in range(4):
                dve.wait_ge(mm, n + 1)
                chain.link(nc.vector.tensor_copy(link_rows[0:1, n, :], psum[0:1, n + 1, 0:P]))
            chain.link(nc.vector.tensor_single_scalar(hi_cl[:], src_cl[:, 0:CH], 7, ALU.arith_shift_right))
            chain.link(nc.vector.tensor_copy(hi_f[:], hi_cl[:]))
            nc.vector.tensor_tensor(hi_hot[:], iota_row[:, None, 0:NT].to_broadcast([P, CH, NT]),
                                    hi_f[:, :, None].to_broadcast([P, CH, NT]), ALU.is_equal).then_inc(dv, 1)

        @block.tensor
        def _(pe):
            pe.wait_ge(dv, 1)
            for n in range(4):
                nc.tensor.matmul(psum[0:1, n + 1, 0:P], lhsT=ends[:, n:n + 1], rhs=ident[:],
                                 start=True, stop=True).then_inc(mm, 1)

    as_cl = gb("as_cl", [P, CH])
    score = gb("score", [P, CH])
    self_e = gb("self_e", [P, CH])
    top = gb("top", [P, CH])
    den = gb("den", [P, CH])
    asad = gb("asad", [P, NT, 2])
    node_vals = gb("node_vals", [P, NT, 2])
    self_n = gb("self_n", [P, NT])
    as_parts = gb("as_parts", [P, 3, NT], BF16)
    as_rest = gb("as_rest", [P, NT])

    for l, (din, _) in enumerate(LAYERS):
        inp = xT if l == 0 else acc[:, 0, :]
        b_l = weights[f"b_gat{l}"]

        end_phase()
        mm, dv, ch, stored, ac = phase_sems(f"gat{l}_rows")
        with nc.Block() as block:

            @block.tensor
            def _(pe):
                for k in range(NT):
                    if k >= 7:
                        pe.wait_ge(ac["nodes"], k - 6)
                        pe.wait_ge(dv, k - 6)
                    nc.tensor.matmul(psum[:, k % 7, 0:WIDE + 2], lhsT=inp[0:din, k * P:(k + 1) * P],
                                     rhs=wxx[l][:], start=True, stop=True).then_inc(mm, 1)

            @block.scalar
            def _(act):
                for k in range(NT):
                    act.wait_ge(dv, k + 1)
                    nc.scalar.copy(nodes[:, k, 0:WIDE], psum[:, k % 7, 0:WIDE]).then_inc(ac["nodes"], 1)

            @block.vector
            def _(dve):
                chain = Chain(dve, ch)
                for k in range(NT):
                    dve.wait_ge(mm, k + 1)
                    nc.vector.tensor_copy(asad[:, k, :], psum[:, k % 7, WIDE:WIDE + 2]).then_inc(dv, 1)
                dve.wait_ge(dv, NT)
                chain.link(nc.vector.tensor_copy(node_vals[:, :, 0], asad[:, :, 1]))
                chain.link(nc.vector.scalar_tensor_tensor(self_n[:], asad[:, :, 0], ae_mean[:, l:l + 1],
                                                          asad[:, :, 1], ALU.add, ALU.add))
                nc.vector.scalar_tensor_tensor(node_vals[:, :, 1], self_n[:], SLOPE, self_n[:],
                                               ALU.mult, ALU.max).then_inc(dv, 1)
                chain.link(nc.vector.tensor_copy(as_parts[:, 0, :], asad[:, :, 0]))
                chain.link(nc.vector.tensor_tensor(as_rest[:], asad[:, :, 0], as_parts[:, 0, :], ALU.subtract))
                chain.link(nc.vector.tensor_copy(as_parts[:, 1, :], as_rest[:]))
                chain.link(nc.vector.tensor_tensor(as_parts[:, 2, :], as_rest[:], as_parts[:, 1, :], ALU.subtract))

            @block.sync
            def _(sp):
                sp.wait_ge(ac["nodes"], NT)
                sp.dma_start(h_tab[l].rearrange("(t p) d -> p t d", p=P), nodes[:, :, 0:WIDE]
                             ).then_inc(stored, 16)
                sp.wait_ge(stored, 16)

        end_phase()
        with ExitStack() as stack, nc.Block() as block:
            lo_rep = stack.enter_context(nc.sbuf_tensor(f"lo_rep{l}", [P, 4, HALF * P], BF16))
            lo_hot = stack.enter_context(nc.sbuf_tensor(f"lo_hot{l}", [P, 2, HALF * P], BF16))
            picked = top[:, 0:HALF * NT].rearrange("p (c h) -> p c h", c=HALF)
            lo_landed = [sem(f"gat{l}_lo_landed{k}") for k in range(4)]
            lo_used = sem(f"gat{l}_lo_used")
            table_rows = sem(f"gat{l}_table_rows")
            rows_used = sem(f"gat{l}_rows_used")
            summed = sem(f"gat{l}_summed")
            scattered = sem(f"gat{l}_scattered")
            TIMES = CH // (4 * HALF)

            @block.sync
            def _(sp):
                with sp.Fori(0, TIMES) as i:
                    for k in range(4):
                        sp.wait_ge(lo_used, i * 4 + (k + 1))
                        sp.dma_start(lo_rep[:, k, :], e_lo[bass.ds(i * (4 * HALF * P) + k * HALF * P, HALF * P)]
                                     .partition_broadcast(P)).then_inc(lo_landed[k], 16)

            @block.gpsimd
            def _(pool):
                for k in range(NT):
                    nc.gpsimd.indirect_dma_start(
                        out=e_first, out_offset=bass.IndirectOffsetOnAxis(ap=first_pos[:, k:k + 1], axis=0),
                        in_=node_vals[:, k, :], in_offset=None).then_inc(scattered, 16)
                gather_ahead(l, 0, AHEAD_PICK)
                pool.wait_ge(scattered, 16 * NT)

            @block.vector
            def _(dve):
                dve.sem_inc(lo_used, 4)
                dve.sem_inc(summed, 1)

                def one_hot(k):
                    nc.vector.tensor_scalar(lo_hot[:, k % 2, :], lo_rep[:, k % 4, :], part_id[:], None,
                                            ALU.is_equal).then_inc(lo_used, 1)

                def pick(n, k):
                    dve.wait_ge(table_rows, n * 4 + (k + 1))
                    dve.wait_ge(summed, n * 4 + (k + 1))
                    c = n * (4 * HALF) + k * HALF
                    nc.vector.tensor_tensor(
                        picked, psum[:, k % 2, 0:HALF * NT].rearrange("p (c h) -> p c h", c=HALF),
                        hi_hot[:, bass.ds(c, HALF), :], ALU.mult).then_inc(rows_used, 1)
                    dve.wait_ge(rows_used, n * 4 + (k + 3))
                    nc.vector.tensor_reduce(as_cl[:, bass.ds(c, HALF)], picked, AX, ALU.add
                                            ).then_inc(summed, 1)

                dve.wait_ge(lo_landed[0], 16)
                one_hot(0)
                with dve.Fori(0, TIMES - 1) as i:
                    for k in range(4):
                        dve.wait_ge(lo_landed[(k + 1) % 4], i * 16 + (32 if k == 3 else 16))
                        one_hot(k + 1)
                        pick(i, k)
                for k in range(4):
                    if k < 3:
                        dve.wait_ge(lo_landed[k + 1], 16 * TIMES)
                        one_hot(k + 1)
                    pick(TIMES - 1, k)

            @block.tensor
            def _(pe):
                pe.sem_inc(rows_used, 2)
                with pe.Fori(0, TIMES) as i:
                    for k in range(4):
                        pe.wait_ge(lo_used, i * 4 + (k + 5))
                        pe.wait_ge(rows_used, i * 4 + (k + 1))
                        for c in range(HALF):
                            for part in range(3):
                                last = nc.tensor.matmul(psum[:, k % 2, c * NT:(c + 1) * NT],
                                                        lhsT=lo_hot[:, k % 2, c * P:(c + 1) * P],
                                                        rhs=as_parts[:, part, :],
                                                        start=part == 0, stop=part == 2)
                        last.then_inc(table_rows, 1)

        end_phase()
        mm, dv, ch, stored, ac = phase_sems(f"gat{l}_soft")
        with ExitStack() as stack, nc.Block() as block:
            efirst = stack.enter_context(nc.sbuf_tensor(f"efirst{l}", [P, CH, 2], F32))
            by_chunk = stack.enter_context(nc.sbuf_tensor(f"by_chunk{l}", [P, len(GROUPS), P], F32))
            diag = stack.enter_context(nc.sbuf_tensor(f"diag{l}", [P, 4, P], F32))
            as_landed = sem(f"gat{l}_as_landed")
            first_landed = sem(f"gat{l}_first_landed")
            coef_landed = sem(f"gat{l}_coef_landed")
            exped = sem(f"gat{l}_exped")
            self_got = sem(f"gat{l}_self_got")

            def chunk_rows(array):
                return [(g // P, n, array[g * P:(g + n) * P].rearrange("(c e) -> c e", e=P))
                        for g, n in GROUPS]

            @block.tensor
            def _(pe):
                for g, n in GROUPS:
                    nc.tensor.transpose(psum[0:n, g // P, 0:P], as_cl[:, g:g + n], ident[:]).then_inc(mm, 1)
                for s in range(6):
                    prefix_pe(pe, scan_sems, 6 * l + s)
                pe.wait_ge(coef_landed, 16 * len(GROUPS))
                for g, n in GROUPS:
                    nc.tensor.transpose(psum[:, g // P, 0:n], by_chunk[0:n, g // P, :], ident[0:n, 0:n]
                                        ).then_inc(mm, 1)
                for k in range(NT):
                    pe.wait_ge(dv, 4 + 2 * len(GROUPS) + k)
                    nc.tensor.matmul(psum[0:WIDE, k % 4, 0:P], lhsT=nodes[:, k, 0:WIDE], rhs=diag[:, k % 4, :],
                                     start=True, stop=True).then_inc(ac["gate"], 1)

            @block.sync
            def _(sp):
                sp.dma_start(efirst[:].rearrange("p n two -> p (n two)"),
                             e_first[0:EP, :].rearrange("(p n) two -> p (n two)", p=P)
                             ).then_inc(first_landed, 16)
                sp.wait_ge(dv, len(GROUPS))
                for g, n, rows_ in chunk_rows(e_as):
                    sp.dma_start(rows_, by_chunk[0:n, g, :]).then_inc(stored, 16)
                sp.wait_ge(stored, 16 * len(GROUPS))
                sp.dma_start(score[:], e_as.rearrange("(p n) -> p n", p=P)).then_inc(as_landed, 16)
                sp.wait_ge(dv, len(GROUPS) + 2)
                sp.dma_start(e_coef.rearrange("(p n) -> p n", p=P), score[:]).then_inc(stored, 16)
                sp.wait_ge(dv, len(GROUPS) + 3)
                sp.dma_start(e_self[0:EP, :].rearrange("(p n) one -> p (n one)", p=P), self_e[:]
                             ).then_inc(stored, 16)
                sp.wait_ge(stored, 16 * (len(GROUPS) + 2))
                for g, n, rows_ in chunk_rows(e_coef):
                    sp.dma_start(by_chunk[0:n, g, :], rows_).then_inc(coef_landed, 16)

            @block.gpsimd
            def _(pool):
                gather_ahead(l, AHEAD_PICK, AHEAD_SOFT)
                pool.wait_ge(stored, 16 * (len(GROUPS) + 2))
                for k in range(NT):
                    nc.gpsimd.indirect_dma_start(
                        out=self_n[:, k:k + 1], out_offset=None, in_=e_self,
                        in_offset=bass.IndirectOffsetOnAxis(ap=first_pos[:, k:k + 1], axis=0)
                    ).then_inc(self_got, 16)

            @block.scalar
            def _(act):
                act.wait_ge(dv, len(GROUPS) + 1)
                nc.scalar.activation(score[:], score[:], ACT.Exp).then_inc(exped, 1)
                nc.scalar.activation(self_e[:], self_e[:], ACT.Exp).then_inc(exped, 1)

            @block.vector
            def _(dve):
                chain = Chain(dve, ch)
                for g, n in GROUPS:
                    dve.wait_ge(mm, g // P + 1)
                    nc.vector.tensor_copy(by_chunk[0:n, g // P, :], psum[0:n, g // P, 0:P]).then_inc(dv, 1)
                dve.wait_ge(first_landed, 16)
                prefix_dve(dve, scan_sems, 6 * l, chain, den, same, efirst[:, :, 0])
                prefix_dve(dve, scan_sems, 6 * l + 1, chain, self_e, same, efirst[:, :, 1])
                dve.wait_ge(as_landed, 16)
                chain.link(nc.vector.tensor_tensor(den[:], den[:], ae[l][:], ALU.add))
                chain.link(nc.vector.tensor_tensor(score[:], score[:], den[:], ALU.add))
                chain.link(nc.vector.scalar_tensor_tensor(score[:], score[:], SLOPE, score[:],
                                                          ALU.mult, ALU.max))
                chain.link(nc.vector.tensor_tensor(den[:], score[:], self_e[:], ALU.max))
                prefix_dve(dve, scan_sems, 6 * l + 2, chain, top, pen, den, largest=True)
                prefix_dve(dve, scan_sems, 6 * l + 3, chain, den, pen_next, top, back=True, largest=True)
                chain.link(nc.vector.tensor_tensor(score[:], score[:], den[:], ALU.subtract))
                nc.vector.tensor_tensor(self_e[:], self_e[:], den[:], ALU.subtract).then_inc(dv, 1)
                dve.wait_ge(exped, 2)
                prefix_dve(dve, scan_sems, 6 * l + 4, chain, top, same, score)
                chain.link(nc.vector.tensor_tensor(top[:], top[:], last_of[:], ALU.mult))
                prefix_dve(dve, scan_sems, 6 * l + 5, chain, den, same_next, top, back=True)
                chain.link(nc.vector.tensor_tensor(den[:], den[:], self_e[:], ALU.add))
                chain.link(nc.vector.reciprocal(den[:], den[:]))
                nc.vector.tensor_tensor(score[:], score[:], den[:], ALU.mult).then_inc(dv, 1)
                nc.vector.tensor_tensor(self_e[:], self_e[:], den[:], ALU.mult).then_inc(dv, 1)
                for g, n in GROUPS:
                    dve.wait_ge(mm, len(GROUPS) + g // P + 1)
                    nc.vector.tensor_copy(scale[:, g:g + n], psum[:, g // P, 0:n]).then_inc(dv, 1)
                dve.wait_ge(self_got, 16 * NT)
                nc.vector.memset(acc[:, 0, NP:ACCW], 0.0)
                for k in range(NT + 2):
                    if k < NT:
                        nc.vector.tensor_scalar(diag[:, k % 4, :], ident[:], self_n[:, k:k + 1], None,
                                                ALU.mult).then_inc(dv, 1)
                    if k >= 2:
                        dve.wait_ge(ac["gate"], k - 1)
                        nc.vector.tensor_copy(acc[0:WIDE, 0, (k - 2) * P:(k - 1) * P],
                                              psum[0:WIDE, (k - 2) % 4, 0:P]).then_inc(ch, 1)

        neighbour_sums(l, acc)

        if l < len(LAYERS) - 1:
            relu_done = sem(f"gat{l}_relu")
            with nc.Block() as block:

                @block.vector
                def _(dve):
                    nc.vector.tensor_scalar(acc[0:WIDE, 0, 0:NP], acc[0:WIDE, 0, 0:NP], b_l[:], 0.0,
                                            ALU.add, ALU.max).then_inc(relu_done, 1)


    gat.close()
    w1, w2, w3 = (sb(f"last_w{k}", [P, NP]) for k in (1, 2, 3))
    end_phase()
    mm, dv, ch, stored, ac = phase_sems("last")
    with nc.Block() as block:

        @block.tensor
        def _(pe):
            for b, (lo, n) in enumerate(BLOCKS):
                nc.tensor.matmul(psum[:, b, 0:n], lhsT=weights["w_gat2"][:], rhs=acc[0:WIDE, 0, lo:lo + n],
                                 start=True, stop=True).then_inc(mm, 1)
            norm_pe(pe, mm, dv, ac, 1, 0, w2, w3)

        @block.vector
        def _(dve):
            chain = Chain(dve, ch)
            for b, (lo, n) in enumerate(BLOCKS):
                s = slice(lo, lo + n)
                dve.wait_ge(mm, ev(0, b))
                chain.link(nc.vector.scalar_tensor_tensor(w2[:, s], psum[:, b, 0:n], b_l[:], xT[:, s],
                                                          ALU.add, ALU.add))
                nc.vector.tensor_tensor(w2[:, s], w2[:, s], xT[:, s], ALU.add).then_inc(dv, 1)
            norm_dve(dve, mm, dv, ac, 1, chain, w2, w3)

        @block.scalar
        def _(act):
            norm_act(act, mm, dv, ac, 1, 0, w3)

        @block.sync
        def _(sp):
            sp.wait_ge(ac["nodes"], NB)
            full = N // P
            sp.dma_start(out[0:full * P, :].rearrange("(t p) d -> p t d", p=P), nodes[:, 0:full, :]
                         ).then_inc(stored, 16)
            sp.dma_start(out[full * P:N, :], nodes[0:N - full * P, full, :]).then_inc(stored, 16)
            sp.wait_ge(stored, 32)


def kernel(**inputs):
    import numpy as np
    import concourse.bacc as bacc
    from concourse.bass_utils import run_bass_kernel_spmd

    i = {k: np.asarray(v) for k, v in inputs.items()}
    src = np.concatenate([i["src"], np.zeros(EP - E, np.int32)])
    pad = np.full(EP - E, N, np.int32)
    dst = np.concatenate([i["dst"], pad])
    arrays = {
        "x": i["x"], "xT": i["x"].T,
        "src_cl": src.reshape(CH, P).T, "dst_cl": dst.reshape(CH, P).T, "base": dst[::P], "quad_base": dst[::4 * P], "quad_last": dst[4 * P - 1::4 * P],
        "src_sl": src.reshape(P, CH), "dst_sl": dst.reshape(P, CH),
        "dst_before": np.concatenate([np.full(1, -1, np.int32), dst[:-1]]).reshape(P, CH),
        "dst_after": np.concatenate([dst[1:], np.full(1, -1, np.int32)]).reshape(P, CH),
        "attr": np.concatenate([i["edge_attr_16"], np.zeros((EP - E, EDIM), np.float32)]).reshape(
            P, CH * EDIM // P, P).transpose(2, 1, 0),
        "w_src": i["L0_gnn_W_src"].T, "b_src": i["L0_gnn_b_src"][:, None],
        "w_fc": i["L0_gnn_W_fc"].T.reshape(2, D, D).transpose(1, 0, 2).reshape(D, 2 * D),
        "b_fc": i["L0_gnn_b_fc"][:, None],
        "w_in": i["L1_gnn_W_in"].T, "b_in": i["L1_gnn_b_in"][:, None],
        "w_out": i["L1_gnn_W_out"].T, "b_out": i["L1_gnn_b_out"][:, None],
        "w_ih": i["L1_gnn_w_ih"].T.reshape(2, D, 3 * D).transpose(1, 0, 2),
        "w_hh": i["L1_gnn_w_hh"].T,
        "b_ih": i["L1_gnn_b_ih"].reshape(3, D).T, "b_hh": i["L1_gnn_b_hh"].reshape(3, D).T,
        "w_gcn": i["L2_gnn_weight"], "b_gcn": i["L2_gnn_bias"][:, None],
    }
    for l in range(len(LAYERS)):
        arrays[f"w_gat{l}"] = i[f"L3_gnn_W{l + 1}"]
        arrays[f"w_gatT{l}"] = i[f"L3_gnn_W{l + 1}"].T
        arrays[f"w_a{l}"] = np.stack([i[f"L3_gnn_as{l + 1}"], i[f"L3_gnn_ad{l + 1}"]], 1)
        arrays[f"w_eT{l}"] = i[f"L3_gnn_We{l + 1}"].T
        arrays[f"w_ae{l}"] = i[f"L3_gnn_ae{l + 1}"][:, None]
        arrays[f"b_gat{l}"] = i[f"L3_gnn_b{l + 1}"][:, None]
    arrays = {k: np.ascontiguousarray(v) for k, v in arrays.items()}

    nc = bacc.Bacc("TRN2", target_bir_lowering=False, num_devices=1)
    aps = {k: nc.dram_tensor("in_" + k, v.shape, mybir.dt.from_np(v.dtype), kind="ExternalInput").ap()
           for k, v in arrays.items()}
    out = nc.dram_tensor("out", (N, D), F32, kind="ExternalOutput").ap()
    gnn_kernel(nc, aps, out)
    r = run_bass_kernel_spmd(nc, [{"in_" + k: v for k, v in arrays.items()}], core_ids=[0])
    return r.results[0]["out"]
```

```python
from contextlib import ExitStack

import concourse.bass as bass
from concourse import mybir

P = 128
N = 3125
NT = -(-N // P)
NP = NT * P
E = 103125
HALF = 12
BODY = 2 * HALF
CH = -(-E // (P * BODY)) * BODY
EP = CH * P
ITERS = CH // BODY
ACCW = NP + P
BLOCKS = [(b, min(512, NP - b)) for b in range(0, NP, 512)]
NB = len(BLOCKS)
D = 128
EDIM = 16
LAYERS = [(128, 80), (80, 80), (80, 128)]
WIDE = 80
SLOPE = 0.2
EPS = 1e-5
QUADS = CH // 4
RING = BODY // 4
WIN = 20
KEYS = NT * WIN
AW = N + WIN + 1
ADJ_BLOCKS = [(b, min(n, 64)) if b + 512 > NP else (b, n) for b, n in BLOCKS]
ADJ_END = sum(ADJ_BLOCKS[-1])
GAT_WEIGHTS = ("w_gat", "b_gat", "w_a", "w_eT")
BIG = 1e30
LEAD = 8
GROUP = 4
TURNS = 17
SLOTS = 204
BANKS = 3
AHEAD_PICK = 84
AHEAD_SOFT = 150
assert KEYS <= 512 and N <= ADJ_END <= AW and RING % 2 == 0
assert CH == ITERS * BODY
assert CH % SLOTS == 0 and SLOTS % (GROUP * TURNS) == 0 and SLOTS // GROUP % BANKS == 0

F32 = mybir.dt.float32
I32 = mybir.dt.int32
BF16 = mybir.dt.bfloat16
U8 = mybir.dt.uint8
F16 = mybir.dt.float16
ALU = mybir.AluOpType
ACT = mybir.ActivationFunctionType
AX = mybir.AxisListType.X


def ev(step, block):
    return NB * step + block + 1


class Chain:

    def __init__(self, engine, sem):
        self.engine, self.sem, self.n = engine, sem, 0

    def link(self, ins):
        self.n += 1
        ins.then_inc(self.sem, 1)
        self.engine.wait_ge(self.sem, self.n)


def gnn_kernel(nc, t, out):
    def sb(name, shape, dt=F32):
        return nc.alloc_sbuf_tensor(name, shape, dt)

    phase_own = []

    def sem(name, kept=False):
        made = nc.alloc_semaphore(name)
        if not kept:
            phase_own.append(made)
        return made

    def end_phase():
        nc.clear_and_free_semaphores(list(phase_own))
        phase_own.clear()
        nc.all_engine_barrier()

    def dram(name, shape, dt=F32):
        return nc.dram_tensor(name, shape, dt, kind="Internal").ap()

    h_tab = [dram(f"h_tab{l}", [NP, WIDE]) for l in range(len(LAYERS))]
    e_first = dram("e_first", [EP + P, 2])
    e_as = dram("e_as", [EP])
    e_coef = dram("e_coef", [EP])
    e_lo = dram("e_lo", [EP], BF16)

    xT = sb("xT", [P, NP])
    ident = sb("ident", [P, P])
    ident_bf = sb("ident_bf", [P, P], BF16)
    iota_row = sb("iota_row", [P, P])
    part_id = sb("part_id", [P, 1])
    ones = sb("ones", [P, P])
    ones_bf = sb("ones_bf", [P, 1], BF16)
    mean_m = sb("mean_m", [P, P])
    eps_col = sb("eps_col", [P, 1])
    one_col = sb("one_col", [P, 1])
    first_pos = sb("first_pos", [P, NT], I32)
    rdeg = sb("rdeg", [P, NT])
    dinv = sb("dinv", [P, NT])
    psum = nc.alloc_psum_tensor("psum", [P, 8, 512], F32)

    consts = sem("consts")
    with nc.Block() as block:

        @block.gpsimd
        def _(pool):
            nc.gpsimd.memset(ident[:], 0.0).then_inc(consts, 1)
            pool.wait_ge(consts, 1)
            nc.gpsimd.affine_select(out=ident[:], in_=ident[:], compare_op=ALU.not_equal, fill=1.0,
                                    base=0, pattern=[[-1, P]], channel_multiplier=1)
            nc.gpsimd.memset(ident_bf[:], 0.0).then_inc(consts, 1)
            pool.wait_ge(consts, 2)
            nc.gpsimd.affine_select(out=ident_bf[:], in_=ident_bf[:], compare_op=ALU.not_equal, fill=1.0,
                                    base=0, pattern=[[-1, P]], channel_multiplier=1)
            nc.gpsimd.iota(iota_row[:], [[1, P]], base=0, channel_multiplier=0,
                           allow_small_or_imprecise_dtypes=True)
            nc.gpsimd.iota(part_id[:], [[0, 1]], base=0, channel_multiplier=1,
                           allow_small_or_imprecise_dtypes=True)
            nc.gpsimd.memset(ones[:], 1.0)
            nc.gpsimd.memset(mean_m[:], 1.0 / D)
            nc.gpsimd.memset(eps_col[:], EPS)
            nc.gpsimd.memset(one_col[:], 1.0)
            nc.gpsimd.memset(ones_bf[:], 1.0)

    early = ExitStack()

    def eb(name, shape, dt=F32):
        return early.enter_context(nc.sbuf_tensor(name, shape, dt))

    adj = eb("adj", [P, NT, AW], BF16)

    end_phase()
    with ExitStack() as stack:
        def bb(name, shape, dt=F32):
            return stack.enter_context(nc.sbuf_tensor(name, shape, dt))

        base_i = bb("base_i", [P, QUADS], I32)
        lo_f = bb("lo_f", [P, CH + 8])
        hi_f = bb("adj_hi", [P, CH], BF16)
        valid = bb("valid", [P, CH], BF16)
        place = bb("place", [P, CH])
        key = bb("key", [P, CH + 8])
        dst_i, src_i, whole = place[:].bitcast(I32), key[:, 0:CH].bitcast(I32), lo_f[:, 0:CH].bitcast(I32)
        q_base = bb("q_base", [1, QUADS], I32)
        q_last = bb("q_last", [1, QUADS], I32)
        span = bb("span", [1, QUADS])
        steps = bb("steps", [1, N // WIN])
        passes_f = bb("passes_f", [1, 1])
        passes_i = bb("passes_i", [1, 1], I32)
        iota_key = bb("iota_key", [P, KEYS], F16)
        lo_off = bb("adj_lo_off", [P, 3, 4 * P], BF16)
        lo_hot = bb("adj_lo_hot", [P, 3, 4 * P], BF16)
        key_hot = bb("adj_key_hot", [P, 12, KEYS], BF16)
        counts = bb("adj_counts", [P, 2, KEYS], BF16)

        loaded = sem("adj_loaded")
        iotas = sem("adj_iotas")
        ready = sem("adj_ready")
        pass_ready = sem("adj_pass_ready")
        keys_made = sem("adj_keys_made")
        lo_off_made = sem("adj_lo_off_made")
        lo_made = sem("adj_lo_made")
        counted = sem("adj_counted")
        copied = sem("adj_copied")
        added = sem("adj_added")
        ch = sem("adj_chain")

        with nc.Block() as block:

            @block.sync
            def _(sp):
                for to, of in ((src_i, t["src_cl"]), (dst_i, t["dst_cl"]),
                               (base_i[:], t["quad_base"].partition_broadcast(P)),
                               (q_base[:], t["quad_base"].rearrange("(a n) -> a n", a=1)),
                               (q_last[:], t["quad_last"].rearrange("(a n) -> a n", a=1))):
                    sp.dma_start(to, of).then_inc(loaded, 16)

            @block.gpsimd
            def _(pool):
                nc.gpsimd.iota(iota_key[:], [[1, KEYS]], base=0, channel_multiplier=0,
                               allow_small_or_imprecise_dtypes=True).then_inc(iotas, 1)
                nc.gpsimd.iota(steps[:], [[WIN, N // WIN]], base=WIN, channel_multiplier=0,
                               allow_small_or_imprecise_dtypes=True).then_inc(iotas, 1)
                nc.gpsimd.memset(adj[:, 0:NT // 2, :].rearrange("p h n -> p (h n)").bitcast(I32), 0
                                 ).then_inc(iotas, 1)

            @block.vector
            def _(dve):
                chain = Chain(dve, ch)
                half = NT // 2
                nc.vector.memset(adj[:, half:NT, :].rearrange("p h n -> p (h n)").bitcast(I32), 0)
                nc.vector.memset(key[:, CH:], -1.0)
                nc.vector.memset(lo_f[:, CH:], 0.0)
                dve.wait_ge(loaded, 16 * 5)
                chain.link(nc.vector.tensor_tensor(
                    place[:].rearrange("p (q k) -> p q k", k=4), dst_i.rearrange("p (q k) -> p q k", k=4),
                    base_i[:, :, None].to_broadcast([P, QUADS, 4]), ALU.subtract))
                chain.link(nc.vector.tensor_single_scalar(whole, src_i, 7, ALU.arith_shift_right))
                chain.link(nc.vector.tensor_copy(hi_f[:], whole))
                chain.link(nc.vector.tensor_single_scalar(whole, src_i, P - 1, ALU.bitwise_and))
                chain.link(nc.vector.tensor_scalar(lo_f[:, 0:CH], whole, -1.0, None, ALU.mult))
                chain.link(nc.vector.tensor_scalar(span[:], q_last[:], float(N - 1), None, ALU.min))
                chain.link(nc.vector.tensor_tensor(span[:], span[:], q_base[:], ALU.subtract))
                chain.link(nc.vector.tensor_reduce(passes_f[:], span[:], AX, ALU.max))
                dve.wait_ge(iotas, 3)
                chain.link(nc.vector.tensor_scalar(steps[:], steps[:], passes_f[:], None, ALU.is_le))
                chain.link(nc.vector.tensor_reduce(passes_f[:], steps[:], AX, ALU.add))
                chain.link(nc.vector.tensor_scalar(passes_i[:], passes_f[:], 1.0, None, ALU.add))
                dve.sem_inc(ready, 1)
                passes = dve.value_load(passes_i[0:1, 0:1], min_val=1, max_val=N // WIN + 1)

                def key_hot_of(c, k):
                    nc.vector.tensor_scalar(key_hot[:, k % 12, :], iota_key[:], key[:, bass.ds(c, 1)], None,
                                            ALU.is_equal).then_inc(keys_made, 1)

                def lo_hot_of(j, place):
                    dve.wait_ge(lo_off_made, s * (4 * QUADS + 8) + j * 4 + 4)
                    nc.vector.tensor_scalar(lo_hot[:, place, :], lo_off[:, place, :], 0.0, None,
                                            ALU.is_equal).then_inc(lo_made, 1)

                dve.sem_inc(lo_made, 3)
                dve.sem_inc(added, 2)
                dve.sem_inc(pass_ready, 1)
                with dve.Fori(0, passes) as s:
                    def after(ins, n):
                        ins.then_inc(pass_ready, 1)
                        dve.wait_ge(pass_ready, s * 7 + (n + 2))
                    after(nc.vector.tensor_scalar(valid[:], place[:], 0.0, None, ALU.is_ge), 0)
                    after(nc.vector.scalar_tensor_tensor(valid[:], place[:], float(WIN), valid[:],
                                                         ALU.is_lt, ALU.mult), 1)
                    after(nc.vector.scalar_tensor_tensor(key[:, 0:CH], hi_f[:], float(WIN), place[:],
                                                         ALU.mult, ALU.add), 2)
                    after(nc.vector.scalar_tensor_tensor(key[:, 0:CH], key[:, 0:CH], 1.0, valid[:],
                                                         ALU.add, ALU.mult), 3)
                    after(nc.vector.tensor_scalar(key[:, 0:CH], key[:, 0:CH], -1.0, None, ALU.add), 4)
                    for q in range(2):
                        lo_hot_of(q, q)
                        for c in range(4 * q, 4 * q + 4):
                            key_hot_of(c, c)
                    with dve.Fori(0, ITERS) as i:
                        _, bases = nc.values_load_multi_w_load_instructions(
                            q_base[0:1, bass.ds(i * RING, RING)], engines=(mybir.EngineType.DVE,),
                            min_val=0, max_val=AW - WIN)
                        for q in range(RING):
                            lo_hot_of(i * RING + (q + 2), (q + 2) % 3)
                            for k in range(8, 12):
                                key_hot_of(i * BODY + (4 * q + k), 4 * q + k)
                            dve.wait_ge(copied, s * QUADS + i * RING + (q + 1 + RING))
                            dve.wait_ge(added, s * QUADS + i * RING + (q + 2))
                            window = adj[:, :, bass.ds(bases[q], WIN)]
                            nc.vector.tensor_tensor(window, window, counts[:, q % 2, :].rearrange(
                                "p (h w) -> p h w", w=WIN), ALU.add).then_inc(added, 1)
                    after(nc.vector.tensor_scalar(place[:], place[:], -float(WIN), None, ALU.add), 5)
                    after(nc.vector.tensor_scalar(q_base[:], q_base[:], float(WIN), float(AW - WIN),
                                                  ALU.add, ALU.min), 6)

            @block.scalar
            def _(act):
                act.wait_ge(ready, 1)
                act.sem_inc(copied, RING)
                passes = act.value_load(passes_i[0:1, 0:1], min_val=1, max_val=N // WIN + 1)

                def offsets(c, place):
                    for k in range(4):
                        nc.scalar.activation(lo_off[:, place, k * P:(k + 1) * P], iota_key[:, 0:P], ACT.Abs,
                                             bias=lo_f[:, bass.ds(c + k, 1)]).then_inc(lo_off_made, 1)

                with act.Fori(0, passes) as s:
                    act.wait_ge(lo_made, s * (QUADS + 2) + 3)
                    for q in range(2):
                        offsets(4 * q, q)
                    with act.Fori(0, ITERS) as i:
                        for q in range(RING):
                            act.wait_ge(lo_made, s * (QUADS + 2) + i * RING + (q + 3))
                            offsets(i * BODY + (4 * q + 8), (q + 2) % 3)
                            act.wait_ge(counted, s * QUADS + i * RING + (q + 1))
                            act.wait_ge(added, s * QUADS + i * RING + (q + 1))
                            nc.scalar.copy(counts[:, q % 2, :], psum[:, q, 0:KEYS]).then_inc(copied, 1)

            @block.tensor
            def _(pe):
                pe.wait_ge(ready, 1)
                passes = pe.value_load(passes_i[0:1, 0:1], min_val=1, max_val=N // WIN + 1)
                with pe.Fori(0, passes) as s:
                    with pe.Fori(0, ITERS) as i:
                        for q in range(RING):
                            pe.wait_ge(lo_made, s * (QUADS + 2) + i * RING + (q + 4))
                            pe.wait_ge(copied, s * QUADS + i * RING + (q + 1))
                            for k in range(4):
                                pe.wait_ge(keys_made, s * (CH + 8) + i * BODY + (4 * q + k + 1))
                                last = nc.tensor.matmul(psum[:, q, 0:KEYS], lhsT=lo_hot[:, q % 3, k * P:(k + 1) * P],
                                                        rhs=key_hot[:, (4 * q + k) % 12, :],
                                                        start=k == 0, stop=k == 3)
                            last.then_inc(counted, 1)

    end_phase()
    mm, dv, ch = sem("first_mm"), sem("first_dv"), sem("first_chain")
    with ExitStack() as stack, nc.Block() as block:
        deg_row = stack.enter_context(nc.sbuf_tensor("deg_row", [1, NP], F32))
        first_row = stack.enter_context(nc.sbuf_tensor("first_row", [1, NP], F32))
        dump = stack.enter_context(nc.sbuf_tensor("dump", [1, P], F32))
        dumped = sem("dumped")
        rooted = sem("rooted")

        @block.gpsimd
        def _(pool):
            nc.gpsimd.iota(dump[:], [[1, P]], base=EP, channel_multiplier=0,
                           allow_small_or_imprecise_dtypes=True).then_inc(dumped, 1)

        @block.tensor
        def _(pe):
            for b, (lo, n) in enumerate(ADJ_BLOCKS):
                for h in range(NT):
                    last = nc.tensor.matmul(psum[0:1, b, 0:n], lhsT=ones_bf[:, 0:1],
                                            rhs=adj[:, h, lo:lo + n], start=h == 0, stop=h == NT - 1)
                last.then_inc(mm, 1)
            pe.wait_ge(dv, NB + 1)
            for k in range(NT):
                nc.tensor.matmul(psum[:, 7, k:k + 1], lhsT=deg_row[0:1, k * P:(k + 1) * P],
                                 rhs=one_col[0:1, :], start=True, stop=True)
                last = nc.tensor.matmul(psum[:, 7, NT + k:NT + k + 1], lhsT=first_row[0:1, k * P:(k + 1) * P],
                                        rhs=one_col[0:1, :], start=True, stop=True)
            last.then_inc(mm, 1)

        @block.vector
        def _(dve):
            chain = Chain(dve, ch)
            chain.link(nc.vector.memset(deg_row[:, ADJ_END:NP], 0.0))
            chain.link(nc.vector.memset(first_row[:], 1.0))
            for b, (lo, n) in enumerate(ADJ_BLOCKS):
                dve.wait_ge(mm, b + 1)
                nc.vector.tensor_copy(deg_row[:, lo:lo + n], psum[0:1, b, 0:n]).then_inc(dv, 1)
            dve.wait_ge(dv, NB)
            chain.link(nc.vector.tensor_tensor_scan(first_row[:], first_row[:], deg_row[:], 0.0,
                                                    ALU.mult, ALU.add))
            chain.link(nc.vector.tensor_tensor(first_row[:], first_row[:], deg_row[:], ALU.subtract))
            dve.wait_ge(dumped, 1)
            nc.vector.tensor_copy(first_row[:, N:NP], dump[:, 0:NP - N]).then_inc(dv, 1)
            dve.wait_ge(mm, NB + 1)
            nc.vector.tensor_copy(first_pos[:], psum[:, 7, NT:2 * NT])
            chain.link(nc.vector.tensor_scalar_max(rdeg[:], psum[:, 7, 0:NT], 1.0))
            chain.link(nc.vector.reciprocal(rdeg[:], rdeg[:]))
            nc.vector.tensor_scalar(dinv[:], psum[:, 7, 0:NT], 1.0, None, ALU.add).then_inc(dv, 1)
            dve.wait_ge(rooted, 1)
            nc.vector.reciprocal(dinv[:], dinv[:]).then_inc(dv, 1)

        @block.scalar
        def _(act):
            act.wait_ge(dv, NB + 2)
            nc.scalar.activation(dinv[:], dinv[:], ACT.Sqrt).then_inc(rooted, 1)

    ew = {k: eb("sb_" + k, list(t[k].shape)) for k in t
          if k.startswith(("w_", "b_")) and not k.startswith(GAT_WEIGHTS)}
    gate_b = eb("gate_b", [P, 3])
    parts = eb("parts", [P, 3, NT, D], BF16)
    temp = eb("temp", [P, 5, 512])
    diag = eb("adj_diag", [P, 4, P])
    SLICES = 6
    products = [(h, s) for h in range(NT) for s in range(3)]

    def neighbour_slice(b, k):
        lo, n = ADJ_BLOCKS[b]
        size = -(-len(products) // SLICES)
        for j, (h, s) in list(enumerate(products))[k * size:(k + 1) * size]:
            last = nc.tensor.matmul(psum[:, b % 2, 0:n], lhsT=parts[:, s, h, :], rhs=adj[:, h, lo:lo + n],
                                    start=j == 0, stop=j == len(products) - 1)
        return last

    def spread(b):
        lo, n = ADJ_BLOCKS[b]
        for k in range(0, n, P):
            m = min(P, n - k)
            last = nc.tensor.matmul(psum[:, 2, k:k + m], lhsT=ones[:], rhs=diag[:, k // P, 0:m],
                                    start=True, stop=True)
        return last

    def diagonals(b, value):
        lo, n = ADJ_BLOCKS[b]
        for k in range(0, n, P):
            last = nc.vector.tensor_scalar(diag[:, k // P, :], ident[:],
                                           value[:, lo // P + k // P:lo // P + k // P + 1], None, ALU.mult)
        return last

    def split_dve(dve, b, source, spare, chain):
        lo, n = BLOCKS[b]
        s = slice(lo // P, (lo + n) // P)
        first, second, third = (parts[:, k, s, :].rearrange("p t d -> p (t d)") for k in range(3))
        chain.link(nc.vector.tensor_tensor(spare, source, first, ALU.subtract))
        chain.link(nc.vector.tensor_copy(second, spare))
        return nc.vector.tensor_tensor(third, spare, second, ALU.subtract)

    def norm(name, after):
        end_phase()
        mean_done, var_done, node_done = sem(name + "_mean"), sem(name + "_var"), sem(name + "_node")
        centred, normed, split = sem(name + "_centred"), sem(name + "_normed"), sem(name + "_split")
        squared, rooted, first_part, ch = (sem(f"{name}_{k}") for k in ("squared", "rooted", "first", "chain"))
        with nc.Block() as block:

            @block.tensor
            def _(pe):
                for b, (lo, n) in enumerate(BLOCKS):
                    nc.tensor.matmul(psum[:, b, 0:n], lhsT=mean_m[:], rhs=xT[:, lo:lo + n],
                                     start=True, stop=True).then_inc(mean_done, 1)
                for b, (lo, n) in enumerate(BLOCKS):
                    pe.wait_ge(squared, b + 1)
                    nc.tensor.matmul(psum[:, b, 0:n], lhsT=mean_m[:], rhs=temp[:, b % 2, 0:n],
                                     start=True, stop=True).then_inc(var_done, 1)
                for b, (lo, n) in enumerate(BLOCKS):
                    if after is None:
                        break
                    pe.wait_ge(normed, b + 1)
                    for k in range(n // P):
                        to, of = psum[:, b, k * P:(k + 1) * P], xT[:, lo + k * P:lo + (k + 1) * P]
                        if after == "transpose":
                            last = nc.tensor.transpose(to, of, ident[:])
                        else:
                            last = nc.tensor.matmul(to, lhsT=of, rhs=ew["w_gcn"][:], start=True, stop=True)
                    last.then_inc(node_done, 1)

            @block.gpsimd
            def _(pool):
                for h in range(NT if after == "project" else 0):
                    own = adj[:, h, h * P:min(h * P + P, N)]
                    nc.gpsimd.tensor_tensor(own, own, ident_bf[:, 0:own.shape[-1]], ALU.add)

            @block.scalar
            def _(act):
                for b, (lo, n) in enumerate(BLOCKS):
                    act.wait_ge(centred, b + 1)
                    if b >= 2:
                        act.wait_ge(var_done, b - 1)
                    nc.scalar.activation(temp[:, b % 2, 0:n], xT[:, lo:lo + n], ACT.Square).then_inc(squared, 1)
                for b, (lo, n) in enumerate(BLOCKS):
                    act.wait_ge(var_done, b + 1)
                    if b >= 2:
                        act.wait_ge(normed, b - 1)
                    nc.scalar.activation(temp[:, 2 + b % 2, 0:n], psum[:, b, 0:n], ACT.Sqrt,
                                         bias=eps_col[:]).then_inc(rooted, 1)
                for b, (lo, n) in enumerate(BLOCKS):
                    if after is None:
                        break
                    act.wait_ge(node_done, b + 1)
                    if after == "project":
                        if b >= 2:
                            act.wait_ge(split, b - 1)
                        for k in range(n // P):
                            last = nc.scalar.activation(temp[:, b % 2, k * P:(k + 1) * P],
                                                        psum[:, b, k * P:(k + 1) * P], ACT.Copy,
                                                        scale=dinv[:, lo // P + k:lo // P + k + 1])
                        last.then_inc(squared, 1)
                        act.wait_ge(squared, NB + b + 1)
                        source = temp[:, b % 2, 0:n]
                    else:
                        source = psum[:, b, 0:n]
                    nc.scalar.copy(parts[:, 0, lo // P:(lo + n) // P, :].rearrange("p t d -> p (t d)"),
                                   source).then_inc(first_part, 1)

            @block.vector
            def _(dve):
                chain = Chain(dve, ch)
                for b, (lo, n) in enumerate(BLOCKS):
                    dve.wait_ge(mean_done, b + 1)
                    nc.vector.tensor_tensor(xT[:, lo:lo + n], xT[:, lo:lo + n], psum[:, b, 0:n], ALU.subtract
                                            ).then_inc(centred, 1)
                for b, (lo, n) in enumerate(BLOCKS):
                    std = temp[:, 2 + b % 2, 0:n]
                    dve.wait_ge(rooted, b + 1)
                    chain.link(nc.vector.reciprocal(std, std))
                    nc.vector.tensor_tensor(xT[:, lo:lo + n], xT[:, lo:lo + n], std, ALU.mult
                                            ).then_inc(normed, 1)
                for b, (lo, n) in enumerate(BLOCKS):
                    if after is None:
                        break
                    dve.wait_ge(first_part, b + 1)
                    source = psum[:, b, 0:n] if after == "transpose" else temp[:, b % 2, 0:n]
                    split_dve(dve, b, source, temp[:, 4, 0:n], chain).then_inc(split, 1)
                    dve.wait_ge(split, b + 1)

    end_phase()
    landed, weights_landed = sem("x_zeroed"), sem("weights_landed")
    first_part, split, ch = sem("x_first"), sem("x_split"), sem("x_chain")
    x_rows = [sem(f"x_rows{k}") for k in range(2)]
    with nc.Block() as block:
        full = N // P

        @block.sync
        def _(sp):
            for b, (lo, n) in enumerate(BLOCKS):
                if b >= 2:
                    sp.wait_ge(split, b - 1)
                to = temp[:, b % 2, 0:n].rearrange("p (t d) -> p t d", d=D)
                if b < NB - 1:
                    sp.dma_start(to, t["x"][lo:lo + n, :].rearrange("(t p) d -> p t d", p=P)
                                 ).then_inc(x_rows[b % 2], 16)
                else:
                    sp.wait_ge(landed, 1)
                    sp.dma_start(to[0:N - lo, 0, :], t["x"][lo:N, :]).then_inc(x_rows[b % 2], 16)

        @block.scalar
        def _(act):
            for k, w in ew.items():
                act.dma_start(w[:], t[k]).then_inc(weights_landed, 16)
            act.dma_start(xT[:, 0:N], t["xT"]).then_inc(weights_landed, 16)
            for b, (lo, n) in enumerate(BLOCKS):
                act.wait_ge(x_rows[b % 2], 16 * (b // 2 + 1))
                nc.scalar.copy(parts[:, 0, lo // P:(lo + n) // P, :].rearrange("p t d -> p (t d)"),
                               temp[:, b % 2, 0:n]).then_inc(first_part, 1)
            act.wait_ge(weights_landed, 16 * (len(ew) + 1))

        @block.gpsimd
        def _(pool):
            nc.gpsimd.memset(xT[:, N:NP], 0.0)

        @block.vector
        def _(dve):
            chain = Chain(dve, ch)
            for b, (lo, n) in enumerate(BLOCKS):
                if b == NB - 1:
                    dve.wait_ge(split, b - 1)
                    nc.vector.memset(temp[:, b % 2, 0:n], 0.0).then_inc(landed, 1)
                dve.wait_ge(first_part, b + 1)
                split_dve(dve, b, temp[:, b % 2, 0:n], temp[:, 4, 0:n], chain).then_inc(split, 1)
                dve.wait_ge(split, b + 1)

    class Layer:

        def __init__(self, name, pe, dve, act):
            self.pe, self.dve, self.act = pe, dve, act
            self.sums, self.spread, self.diags, self.chain = (
                sem(f"{name}_{k}") for k in ("sums", "spread", "diagonals", "chain"))
            self.pe_done, self.dve_done, self.act_done = (sem(f"{name}_{k}_done") for k in ("pe", "dve", "act"))

    def blocks_pe(pe, y, step):
        pe.wait_ge(y.diags, 1)
        spread(0).then_inc(y.spread, 1)
        for k in range(SLICES):
            last = neighbour_slice(0, k)
        last.then_inc(y.sums, 1)
        for b in range(NB):
            more = b + 1 < NB
            if more:
                pe.wait_ge(y.diags, b + 2)
                pe.wait_ge(y.act_done, b * y.act + 1)
                spread(b + 1).then_inc(y.spread, 1)
                if b >= 1:
                    pe.wait_ge(y.dve_done, (b - 1) * y.dve + 1)
            for k in range(SLICES):
                if k < y.pe:
                    step(b, k).then_inc(y.pe_done, 1)
                if more:
                    last = neighbour_slice(b + 1, k)
            if more:
                last.then_inc(y.sums, 1)

    def spread_act(act, y, b, behind):
        lo, n = ADJ_BLOCKS[b]
        act.wait_ge(y.spread, b + 1)
        if b >= 1:
            act.wait_ge(y.dve_done, (b - 1) * y.dve + behind + 1)
        nc.scalar.copy(temp[:, 4, 0:n], psum[:, 2, 0:n]).then_inc(y.act_done, 1)

    def scaled_dve(dve, y, b, value):
        lo, n = ADJ_BLOCKS[b]
        dve.wait_ge(y.sums, b + 1)
        dve.wait_ge(y.act_done, b * y.act + 1)
        if b >= 1:
            dve.wait_ge(y.dve_done, b * y.dve)
        nc.vector.tensor_tensor(temp[:, 0, 0:n], psum[:, b % 2, 0:n], temp[:, 4, 0:n], ALU.mult
                                ).then_inc(y.dve_done, 1)
        if b + 1 < NB:
            diagonals(b + 1, value).then_inc(y.diags, 1)

    end_phase()
    y = Layer("sage", 2, 2, 2)
    with nc.Block() as block:

        @block.tensor
        def _(pe):
            def step(b, k):
                lo, n = ADJ_BLOCKS[b]
                if k == 0:
                    pe.wait_ge(y.dve_done, b * y.dve + 1)
                    return nc.tensor.matmul(psum[:, 3, 0:n], lhsT=ew["w_src"][:], rhs=temp[:, 0, 0:n],
                                            start=True, stop=True)
                if b >= 1:
                    pe.wait_ge(y.dve_done, b * y.dve)
                pe.wait_ge(y.act_done, b * y.act + 2)
                nc.tensor.matmul(psum[:, 4, 0:n], lhsT=ew["w_fc"][:, 0:D], rhs=xT[:, lo:lo + n],
                                 start=True, stop=False)
                return nc.tensor.matmul(psum[:, 4, 0:n], lhsT=ew["w_fc"][:, D:2 * D], rhs=temp[:, 1, 0:n],
                                        start=False, stop=True)

            blocks_pe(pe, y, step)

        @block.scalar
        def _(act):
            for b, (lo, n) in enumerate(ADJ_BLOCKS):
                spread_act(act, y, b, 0)
                act.wait_ge(y.pe_done, b * y.pe + 1)
                nc.scalar.activation(temp[:, 1, 0:n], psum[:, 3, 0:n], ACT.Identity, bias=ew["b_src"][:]
                                     ).then_inc(y.act_done, 1)

        @block.vector
        def _(dve):
            diagonals(0, rdeg).then_inc(y.diags, 1)
            for b, (lo, n) in enumerate(ADJ_BLOCKS):
                scaled_dve(dve, y, b, rdeg)
                dve.wait_ge(y.pe_done, b * y.pe + 2)
                nc.vector.scalar_tensor_tensor(xT[:, lo:lo + n], psum[:, 4, 0:n], ew["b_fc"][:],
                                               xT[:, lo:lo + n], ALU.add, ALU.add).then_inc(y.dve_done, 1)

    norm("norm0", "transpose")

    end_phase()
    y = Layer("gru", 6, 4, 6)
    with nc.Block() as block:

        @block.tensor
        def _(pe):
            def step(b, k):
                lo, n = ADJ_BLOCKS[b]
                x_b, t0, t1, t2 = xT[:, lo:lo + n], temp[:, 0, 0:n], temp[:, 1, 0:n], temp[:, 2, 0:n]
                wi, wh = ew["w_ih"], ew["w_hh"]
                if k == 0:
                    pe.wait_ge(y.dve_done, b * y.dve + 1)
                if k < 2:
                    w = ew["w_in"] if k == 0 else ew["w_out"]
                    return nc.tensor.matmul(psum[:, 3 + k, 0:n], lhsT=w[:], rhs=t0, start=True, stop=True)
                if k == 2:
                    pe.wait_ge(y.act_done, b * y.act + 3)
                gate = {2: 0, 3: 1, 4: 2, 5: 2}[k]
                g = slice(gate * D, (gate + 1) * D)
                bank = {2: 5, 3: 6, 4: 7, 5: 3}[k]
                if k != 4:
                    nc.tensor.matmul(psum[:, bank, 0:n], lhsT=wi[:, 0, g], rhs=t1, start=True, stop=False)
                    last = nc.tensor.matmul(psum[:, bank, 0:n], lhsT=wi[:, 1, g], rhs=t2,
                                            start=False, stop=k == 5)
                if k != 5:
                    last = nc.tensor.matmul(psum[:, bank, 0:n], lhsT=wh[:, g], rhs=x_b,
                                            start=k == 4, stop=True)
                return last

            blocks_pe(pe, y, step)

        @block.scalar
        def _(act):
            act.wait_ge(y.chain, 1)
            for b, (lo, n) in enumerate(ADJ_BLOCKS):
                spread_act(act, y, b, 3)
                for k, bias in enumerate(("b_in", "b_out")):
                    act.wait_ge(y.pe_done, b * y.pe + k + 1)
                    nc.scalar.activation(temp[:, 1 + k, 0:n], psum[:, 3 + k, 0:n], ACT.Identity,
                                         bias=ew[bias][:]).then_inc(y.act_done, 1)
                for k in range(2):
                    act.wait_ge(y.pe_done, b * y.pe + 3 + k)
                    nc.scalar.activation(temp[:, 3 + k, 0:n], psum[:, 5 + k, 0:n], ACT.Sigmoid,
                                         bias=gate_b[:, k:k + 1]).then_inc(y.act_done, 1)
                act.wait_ge(y.dve_done, b * y.dve + 3)
                nc.scalar.activation(temp[:, 3, 0:n], temp[:, 3, 0:n], ACT.Tanh).then_inc(y.act_done, 1)

        @block.vector
        def _(dve):
            chain = Chain(dve, y.chain)
            chain.link(nc.vector.tensor_tensor(gate_b[:], ew["b_ih"][:], ew["b_hh"][:], ALU.add))
            diagonals(0, rdeg).then_inc(y.diags, 1)
            for b, (lo, n) in enumerate(ADJ_BLOCKS):
                t0, t3, t4, x_b = temp[:, 0, 0:n], temp[:, 3, 0:n], temp[:, 4, 0:n], xT[:, lo:lo + n]
                scaled_dve(dve, y, b, rdeg)
                dve.wait_ge(y.pe_done, b * y.pe + 5)
                dve.wait_ge(y.act_done, b * y.act + 5)
                nc.vector.scalar_tensor_tensor(t3, psum[:, 7, 0:n], ew["b_hh"][:, 2:3], t3,
                                               ALU.add, ALU.mult).then_inc(y.dve_done, 1)
                dve.wait_ge(y.pe_done, b * y.pe + 6)
                dve.wait_ge(y.dve_done, b * y.dve + 2)
                nc.vector.scalar_tensor_tensor(t3, psum[:, 3, 0:n], ew["b_ih"][:, 2:3], t3,
                                               ALU.add, ALU.add).then_inc(y.dve_done, 1)
                dve.wait_ge(y.act_done, b * y.act + 6)
                chain.link(nc.vector.tensor_tensor(t0, x_b, t3, ALU.subtract))
                chain.link(nc.vector.tensor_tensor(t0, t0, t4, ALU.mult))
                chain.link(nc.vector.tensor_tensor(t0, t0, t3, ALU.add))
                nc.vector.tensor_tensor(x_b, x_b, t0, ALU.add).then_inc(y.dve_done, 1)

    norm("norm1", "project")

    end_phase()
    y = Layer("gcn", 0, 2, 1)
    with nc.Block() as block:

        @block.tensor
        def _(pe):
            blocks_pe(pe, y, None)

        @block.scalar
        def _(act):
            for b in range(NB):
                spread_act(act, y, b, 0)

        @block.vector
        def _(dve):
            chain = Chain(dve, y.chain)
            diagonals(0, dinv).then_inc(y.diags, 1)
            for b, (lo, n) in enumerate(ADJ_BLOCKS):
                t0, x_b = temp[:, 0, 0:n], xT[:, lo:lo + n]
                scaled_dve(dve, y, b, dinv)
                dve.wait_ge(y.dve_done, b * y.dve + 1)
                chain.link(nc.vector.tensor_scalar(t0, t0, ew["b_gcn"][:], 0.0, ALU.add, ALU.max))
                nc.vector.tensor_tensor(x_b, x_b, t0, ALU.add).then_inc(y.dve_done, 1)

    norm("norm2", None)
    early.close()

    nodes = sb("nodes", [P, NT, D])
    weights = {k: sb("sb_" + k, list(t[k].shape)) for k in t if k.startswith(GAT_WEIGHTS)}
    src_cl = sb("src_cl", [P, CH], I32)
    dloc = sb("dloc", [P, CH + LEAD])
    scale = sb("scale", [P, CH + LEAD])
    wxx = [sb(f"wxx{l}", [din, WIDE + 2]) for l, (din, dout) in enumerate(LAYERS)]
    ae = [sb(f"ae{l}", [P, CH]) for l in range(len(LAYERS))]
    ae_mean = sb("ae_mean", [P, len(LAYERS)])
    base_row = sb("base_row", [1, CH], I32)
    ring = sb("ring", [P, SLOTS, WIDE])
    idx = sb("idx", [P, SLOTS], I32)
    hot = sb("hot", [P, BANKS * GROUP, P])

    rows_landed = [sem(f"rows_landed{k}", True) for k in range(SLOTS // GROUP)]
    idx_copied = sem("idx_copied", True)
    idx_seen = sem("idx_seen", True)
    hot_ready = sem("hot_ready", True)
    sum_ready = sem("sum_ready", True)
    sum_added = sem("sum_added", True)

    def gather(l, slot, index):
        nc.gpsimd.indirect_dma_start(
            out=ring[:, slot, :], out_offset=None, in_=h_tab[l],
            in_offset=bass.IndirectOffsetOnAxis(ap=index, axis=0)).then_inc(rows_landed[slot // GROUP], 16)

    def gather_ahead(l, first, last):
        for c in range(first, last):
            gather(l, c, src_cl[:, c:c + 1])

    def neighbour_sums(l, acc):
        groups = SLOTS // GROUP
        turn = SLOTS // TURNS
        rounds = CH // SLOTS
        filled = -(-(E - (rounds - 1) * SLOTS * P) // (P * GROUP))
        copied_before = l * ((rounds - 2) * TURNS + 1)
        sums_before = l * (CH // GROUP)
        hots_before = l * (CH + LEAD)
        added_before = l * (CH + BANKS * GROUP)

        with nc.Block() as block:

            @block.gpsimd
            def _(pool):
                gather_ahead(l, AHEAD_SOFT, SLOTS)

                def take_index(i, k):
                    pool.wait_ge(sum_ready, i * groups + (sums_before + (k + 1) * turn // GROUP))
                    nc.gpsimd.tensor_copy(
                        idx[:, k % TURNS * turn:(k % TURNS + 1) * turn],
                        src_cl[:, bass.ds(i * SLOTS + (SLOTS + k * turn), turn)]).then_inc(idx_copied, 1)

                take_index(0, 0)
                with pool.Fori(0, rounds - 2) as i:
                    for k in range(TURNS):
                        take_index(i, k + 1)
                        pool.wait_ge(idx_copied, i * TURNS + (copied_before + k + 1))
                        pool.sem_inc(idx_seen, 1)
                        for c in range(k * turn, (k + 1) * turn):
                            gather(l, c, idx[:, c:c + 1])
                for k in range(TURNS):
                    pool.wait_ge(sum_ready, (rounds - 2) * groups + sums_before + (k + 1) * turn // GROUP)
                    for slot in range(k * turn, min((k + 1) * turn, filled * GROUP)):
                        c = (rounds - 1) * SLOTS + slot
                        gather(l, slot, src_cl[:, c:c + 1])

            @block.tensor
            def _(pe):
                def sum_group(g, first, landed):
                    if landed is not None:
                        pe.wait_ge(rows_landed[g], landed)
                    pe.wait_ge(hot_ready, first + (hots_before + (g + 1) * GROUP))
                    pe.wait_ge(sum_added, first + (added_before + (g + 1) * GROUP))
                    for k in range(GROUP):
                        c = g * GROUP + k
                        last = nc.tensor.matmul(psum[0:WIDE, g % BANKS, k * P:(k + 1) * P], lhsT=ring[:, c, :],
                                                rhs=hot[:, g % BANKS * GROUP + k, :], start=True, stop=True)
                    last.then_inc(sum_ready, 1)

                def landed_before(g):
                    return l * (rounds if g < filled else rounds - 1) * 16 * GROUP

                with pe.Fori(0, rounds - 1) as i:
                    for g in range(groups):
                        sum_group(g, i * SLOTS, i * (16 * GROUP) + (landed_before(g) + 16 * GROUP))
                for g in range(groups):
                    sum_group(g, (rounds - 1) * SLOTS,
                              landed_before(g) + rounds * 16 * GROUP if g < filled else None)

            @block.vector
            def _(dve):
                dve.sem_inc(sum_added, BANKS * GROUP)

                def one_hot(c, place):
                    nc.vector.tensor_scalar(hot[:, place, :], iota_row[:], dloc[:, bass.ds(c, 1)],
                                            scale[:, bass.ds(c, 1)], ALU.is_equal, ALU.mult
                                            ).then_inc(hot_ready, 1)

                for c in range(LEAD):
                    one_hot(c, c)
                with dve.Fori(0, CH // (BANKS * GROUP)) as i:
                    _, bases = nc.values_load_multi_w_load_instructions(
                        base_row[0:1, bass.ds(i * (BANKS * GROUP), BANKS * GROUP)],
                        engines=(mybir.EngineType.DVE,), min_val=0, max_val=N)
                    for g in range(BANKS):
                        c = i * (BANKS * GROUP) + g * GROUP
                        for k, base in enumerate(bases[g * GROUP:(g + 1) * GROUP]):
                            one_hot(c + (LEAD + k), (g * GROUP + LEAD + k) % (BANKS * GROUP))
                            if k == 0:
                                dve.wait_ge(sum_ready, i * BANKS + (sums_before + g + 1))
                            dve.wait_ge(sum_added, c + (added_before + BANKS * GROUP + k))
                            window = acc[0:WIDE, 0, bass.ds(base, P)]
                            nc.vector.tensor_tensor(window, window, psum[0:WIDE, g, k * P:(k + 1) * P],
                                                    ALU.add).then_inc(sum_added, 1)

    end_phase()
    loaded = sem("gat_loaded")
    v0 = sem("v0")
    with ExitStack() as stack:
        dst_cl = stack.enter_context(nc.sbuf_tensor("gat_dst_cl", [P, CH], I32))
        base_cl = stack.enter_context(nc.sbuf_tensor("base_cl", [P, CH], I32))
        src_sl = stack.enter_context(nc.sbuf_tensor("gat_src_sl", [P, CH], I32))
        lo_sl = stack.enter_context(nc.sbuf_tensor("lo_sl", [P, CH], I32))
        lo_bf = stack.enter_context(nc.sbuf_tensor("lo_bf", [P, CH], BF16))
        with nc.Block() as block:
            loads = len(weights) + 5
            lo_ready = sem("lo_ready")
            lo_stored = sem("lo_stored")

            @block.sync
            def _(sp):
                for dst, src in ((src_cl[:], t["src_cl"]), (dst_cl[:], t["dst_cl"]),
                                 (base_cl[:], t["base"].partition_broadcast(P)),
                                 (src_sl[:], t["src_sl"]), (base_row[:], t["base"].rearrange("(a n) -> a n", a=1))):
                    sp.dma_start(dst, src).then_inc(loaded, 16)
                for k, w in weights.items():
                    sp.dma_start(w[:], t[k]).then_inc(loaded, 16)
                sp.wait_ge(lo_ready, 1)
                sp.dma_start(e_lo.rearrange("(p n) -> p n", p=P), lo_bf[:]).then_inc(lo_stored, 16)
                sp.wait_ge(lo_stored, 16)

            @block.vector
            def _(dve):
                nc.vector.memset(scale[:, CH:], 1.0)
                nc.vector.memset(dloc[:, CH:CH + LEAD], -1.0)
                dve.wait_ge(loaded, 16 * loads)
                nc.vector.tensor_tensor(dloc[:, 0:CH], dst_cl[:], base_cl[:], ALU.subtract)
                chain = Chain(dve, v0)
                chain.link(nc.vector.tensor_single_scalar(lo_sl[:], src_sl[:], P - 1, ALU.bitwise_and))
                nc.vector.tensor_copy(lo_bf[:], lo_sl[:]).then_inc(lo_ready, 1)


    def norm_pe(pe, mm, dv, ac, m, d, w2, w3):
        for b, (lo, n) in enumerate(BLOCKS):
            pe.wait_ge(dv, ev(d, b))
            nc.tensor.matmul(psum[:, b, 0:n], lhsT=mean_m[:], rhs=w2[:, lo:lo + n],
                             start=True, stop=True).then_inc(mm, 1)
        for b, (lo, n) in enumerate(BLOCKS):
            pe.wait_ge(ac["sq"], b + 1)
            nc.tensor.matmul(psum[:, b, 0:n], lhsT=mean_m[:], rhs=w3[:, lo:lo + n],
                             start=True, stop=True).then_inc(mm, 1)
        for b, (lo, n) in enumerate(BLOCKS):
            pe.wait_ge(dv, ev(d + 2, b))
            for k in range(n // P):
                last = nc.tensor.transpose(psum[:, b, k * P:(k + 1) * P], xT[:, lo + k * P:lo + (k + 1) * P],
                                           ident[:])
            last.then_inc(mm, 1)

    def norm_dve(dve, mm, dv, ac, m, chain, w2, w3):
        for b, (lo, n) in enumerate(BLOCKS):
            s = slice(lo, lo + n)
            dve.wait_ge(mm, ev(m, b))
            nc.vector.tensor_tensor(w1[:, s], w2[:, s], psum[:, b, 0:n], ALU.subtract).then_inc(dv, 1)
        for b, (lo, n) in enumerate(BLOCKS):
            s = slice(lo, lo + n)
            dve.wait_ge(ac["std"], b + 1)
            chain.link(nc.vector.reciprocal(w3[:, s], w3[:, s]))
            nc.vector.tensor_tensor(xT[:, s], w1[:, s], w3[:, s], ALU.mult).then_inc(dv, 1)

    def norm_act(act, mm, dv, ac, m, d, w3):
        for b, (lo, n) in enumerate(BLOCKS):
            act.wait_ge(dv, ev(d + 1, b))
            nc.scalar.activation(w3[:, lo:lo + n], w1[:, lo:lo + n], ACT.Square).then_inc(ac["sq"], 1)
        for b, (lo, n) in enumerate(BLOCKS):
            act.wait_ge(mm, ev(m + 1, b))
            nc.scalar.activation(w3[:, lo:lo + n], psum[:, b, 0:n], ACT.Sqrt,
                                 bias=eps_col[:]).then_inc(ac["std"], 1)
        take_nodes(act, mm, ac, m + 2)

    def take_nodes(act, mm, ac, m):
        for b, (lo, n) in enumerate(BLOCKS):
            act.wait_ge(mm, ev(m, b))
            nc.scalar.copy(nodes[:, lo // P:(lo + n) // P, :].rearrange("p t d -> p (t d)"),
                           psum[:, b, 0:n]).then_inc(ac["nodes"], 1)

    def phase_sems(name):
        return (sem(name + "_mm"), sem(name + "_dv"), sem(name + "_chain"), sem(name + "_stored"),
                {k: sem(f"{name}_{k}") for k in ("sq", "std", "nodes")})

    GROUPS = [(g, min(P, CH - g)) for g in range(0, CH, P)]

    def prefix_pe(pe, s, number):
        col, crow = s["col"], s["crow"]
        pe.wait_ge(s["state"], number + 1)
        nc.tensor.matmul(psum[0:1, 7, 0:P], lhsT=col[:], rhs=ident[:], start=True, stop=True
                         ).then_inc(s["row"], 1)
        pe.wait_ge(s["starts_row"], number + 1)
        at = s["at"][number]
        nc.tensor.matmul(psum[:, 7, P:P + 1], lhsT=crow[0:1, at:at + P], rhs=one_col[0:1, :],
                         start=True, stop=True).then_inc(s["starts"], 1)

    def prefix_dve(dve, s, number, chain, out_, link, data, back=False, largest=False):
        op0, op1 = (ALU.add, ALU.max) if largest else (ALU.mult, ALU.add)
        first = -BIG if largest else 0.0
        links_row = {(False, False): 0, (False, True): 1, (True, False): 2, (True, True): 3}[back, largest]
        crow, link_rows, col, start_col = s["crow"], s["link_rows"], s["col"], s["start_col"]
        turn = slice(None, None, -1) if back else slice(None)
        chain.link(nc.vector.tensor_tensor_scan(out_[:, turn], link[:, turn], data[:, turn], first, op0, op1))
        end = 0 if back else CH - 1
        chain.link(nc.vector.memset(crow[:], first))
        nc.vector.tensor_copy(col[:], out_[:, end:end + 1]).then_inc(s["state"], 1)
        dve.wait_ge(s["row"], number + 1)
        nc.vector.tensor_tensor_scan(crow[0:1, 1:P + 1][:, turn], link_rows[0:1, links_row, :][:, turn],
                                     psum[0:1, 7, 0:P][:, turn], first, op0, op1).then_inc(s["starts_row"], 1)
        dve.wait_ge(s["starts"], number + 1)
        chain.link(nc.vector.tensor_copy(start_col[:], psum[:, 7, P:P + 1]))
        chain.link(nc.vector.tensor_tensor_scan(out_[:, turn], link[:, turn], data[:, turn],
                                                start_col[:], op0, op1))

    acc = sb("gat_acc", [P, 1, ACCW])
    gat = ExitStack()

    def gb(name, shape, dt=F32):
        return gat.enter_context(nc.sbuf_tensor(name, shape, dt))

    same = gb("same", [P, CH], BF16)
    same_next = gb("same_next", [P, CH], BF16)
    pen = gb("pen", [P, CH], BF16)
    pen_next = gb("pen_next", [P, CH], BF16)
    last_of = gb("last_of", [P, CH], BF16)
    loop_share = gb("loop_share", [P, CH])
    hi_hot = gb("hi_hot", [P, CH, NT], U8)
    link_rows = gb("link_rows", [1, 4, P])
    crow = gb("crow", [1, P + 2])
    col = gb("col", [P, 1])
    start_col = gb("start_col", [P, 1])
    ends = gb("ends", [P, 4])
    scan_sems = {k: sem("prefix_" + k, True) for k in ("state", "row", "starts_row", "starts")}
    scan_sems |= {"crow": crow, "link_rows": link_rows, "col": col, "start_col": start_col}
    scan_sems["at"] = [0, 2] + [0, 0, 0, 2, 0, 2] * len(LAYERS)

    end_phase()
    mm, dv, ch, stored, ac = phase_sems("gat_setup")
    edge_mm, edge_dv = sem("edge_mm"), sem("edge_dv")
    attr_landed = [sem(f"attr_landed{k}") for k in range(2)]
    masked = sem("attr_masked")
    GR = P // EDIM
    COLS = CH // GR
    PART = COLS // 6
    with ExitStack() as stack, nc.Block() as block:
        attr = stack.enter_context(nc.sbuf_tensor("attr", [P, 2, PART, P], F32))
        we_rep = stack.enter_context(nc.sbuf_tensor("we_rep", [P, len(LAYERS), GR, EDIM], F32))
        own = stack.enter_context(nc.sbuf_tensor("own", [P, GR], F32))
        we_ae = stack.enter_context(nc.sbuf_tensor("we_ae", [P, len(LAYERS), GR], F32))
        sums = stack.enter_context(nc.sbuf_tensor("sums", [P, len(LAYERS)], F32))
        dst_sl = stack.enter_context(nc.sbuf_tensor("dst_sl", [P, CH], I32))
        before_sl = stack.enter_context(nc.sbuf_tensor("before_sl", [P, CH], I32))
        after_sl = stack.enter_context(nc.sbuf_tensor("after_sl", [P, CH], I32))
        hi_f = scale[:, 0:CH]
        own_sl = stack.enter_context(nc.sbuf_tensor("own_sl", [P, CH], I32))
        loops = stack.enter_context(nc.sbuf_tensor("loops", [P, CH], F32))
        zeros = acc[:, 0, 0:2 * (CH + 1)]
        landed = sem("gat_edges_landed")
        zeroed = sem("gat_zeroed")
        cleared = sem("gat_cleared")

        @block.sync
        def _(sp):
            for to, of in ((dst_sl, "dst_sl"), (before_sl, "dst_before"), (after_sl, "dst_after"),
                           (own_sl, "src_sl")):
                sp.dma_start(to[:], t[of]).then_inc(landed, 16)
            sp.wait_ge(zeroed, 1)
            sp.dma_start(e_first.rearrange("(p n) two -> p (n two)", p=P), zeros).then_inc(cleared, 16)
            sp.wait_ge(cleared, 16)

        @block.vector
        def _(dve):
            chain = Chain(dve, ch)
            for l, (din, dout) in enumerate(LAYERS):
                last = nc.vector.tensor_copy(
                    we_rep[0:dout, l, :, :], weights[f"w_eT{l}"][:, None, :].to_broadcast([dout, GR, EDIM]))
            last.then_inc(edge_dv, 1)
            dve.wait_ge(masked, 3)
            for l, (din, dout) in enumerate(LAYERS):
                dve.wait_ge(edge_mm, l + 1)
                nc.vector.tensor_copy(wxx[l][:, 0:WIDE], weights[f"w_gat{l}"][:] if dout == WIDE
                                      else ident[0:WIDE, 0:WIDE])
                nc.vector.tensor_copy(wxx[l][:, WIDE:WIDE + 2], psum[0:din, l, 0:2])
                chain.link(nc.vector.tensor_scalar(we_ae[:, l, :], own[:], psum[:, 3 + l, 0:1], None, ALU.mult))
            nc.vector.sem_inc(edge_dv, 1)
            nc.vector.memset(zeros, 0.0).then_inc(zeroed, 1)
            dve.wait_ge(landed, 64)
            for links, pens, other in ((same, pen, before_sl), (same_next, pen_next, after_sl)):
                chain.link(nc.vector.tensor_tensor(links[:], dst_sl[:], other[:], ALU.is_equal))
                chain.link(nc.vector.tensor_scalar(pens[:], links[:], -1.0, BIG, ALU.add, ALU.mult))
            chain.link(nc.vector.tensor_scalar(last_of[:], same_next[:], -1.0, -1.0, ALU.add, ALU.mult))
            for n, links in enumerate((same, pen, same_next, pen_next)):
                chain.link(nc.vector.tensor_reduce(ends[:, n:n + 1], links[:], AX, ALU.min))
            nc.vector.tensor_copy(col[:], ends[:, 0:1]).then_inc(dv, 1)
            for n in range(4):
                dve.wait_ge(mm, n + 1)
                chain.link(nc.vector.tensor_copy(link_rows[0:1, n, :], psum[0:1, n + 1, 0:P]))
            chain.link(nc.vector.tensor_tensor(loop_share[:], own_sl[:], dst_sl[:], ALU.is_equal))
            prefix_dve(dve, scan_sems, 0, chain, hi_f, same, loop_share)
            chain.link(nc.vector.tensor_tensor(hi_f[:], hi_f[:], last_of[:], ALU.mult))
            prefix_dve(dve, scan_sems, 1, chain, loops, same_next, hi_f, back=True)
            chain.link(nc.vector.tensor_scalar_max(loops[:], loops[:], 1.0))
            chain.link(nc.vector.reciprocal(loops[:], loops[:]))
            chain.link(nc.vector.tensor_tensor(loop_share[:], loop_share[:], loops[:], ALU.mult))
            chain.link(nc.vector.tensor_single_scalar(own_sl[:], src_cl[:], 7, ALU.arith_shift_right))
            chain.link(nc.vector.tensor_copy(hi_f[:], own_sl[:]))
            nc.vector.tensor_tensor(hi_hot[:], iota_row[:, None, 0:NT].to_broadcast([P, CH, NT]),
                                    hi_f[:, :, None].to_broadcast([P, CH, NT]), ALU.is_equal).then_inc(dv, 1)
            for j in range(6):
                dve.wait_ge(edge_mm, len(LAYERS) + j + 1)
                for l in range(len(LAYERS)):
                    chain.link(nc.vector.tensor_copy(
                        ae[l][:, j * PART * GR:(j + 1) * PART * GR].rearrange("p (c g) -> p c g", g=GR),
                        psum[:, j, 0:PART * len(LAYERS) * GR].rearrange(
                            "p (c l g) -> p l c g", l=len(LAYERS), g=GR)[:, l]))
            for l in range(len(LAYERS)):
                chain.link(nc.vector.tensor_reduce(sums[:, l:l + 1], ae[l][:], AX, ALU.add))
            nc.vector.sem_inc(edge_dv, 1)
            dve.wait_ge(edge_mm, len(LAYERS) + 7)
            nc.vector.tensor_scalar(ae_mean[:], psum[:, 7, 0:len(LAYERS)], 1.0 / E, None,
                                    ALU.mult).then_inc(edge_dv, 1)

        @block.tensor
        def _(pe):
            pe.wait_ge(edge_dv, 1)
            for l, (din, dout) in enumerate(LAYERS):
                nc.tensor.matmul(psum[0:din, l, 0:2], lhsT=weights[f"w_gatT{l}"][:],
                                 rhs=weights[f"w_a{l}"][:], start=True, stop=True)
                nc.tensor.matmul(psum[:, 3 + l, 0:1],
                                 lhsT=we_rep[0:dout, l, :, :].rearrange("p g d -> p (g d)"),
                                 rhs=weights[f"w_ae{l}"][:], start=True, stop=True).then_inc(edge_mm, 1)
            pe.wait_ge(dv, 1)
            for n in range(4):
                nc.tensor.matmul(psum[0:1, n + 1, 0:P], lhsT=ends[:, n:n + 1], rhs=ident[:],
                                 start=True, stop=True).then_inc(mm, 1)
            for s in range(2):
                prefix_pe(pe, scan_sems, s)
            pe.wait_ge(edge_dv, 2)
            for j in range(6):
                pe.wait_ge(attr_landed[j % 2], 16 * (j // 2 + 1))
                for c in range(PART):
                    last = nc.tensor.matmul(
                        psum[:, j, c * len(LAYERS) * GR:(c + 1) * len(LAYERS) * GR], lhsT=attr[:, j % 2, c, :],
                        rhs=we_ae[:].rearrange("p l g -> p (l g)"), start=True, stop=True)
                last.then_inc(edge_mm, 1)
            pe.wait_ge(edge_dv, 3)
            nc.tensor.matmul(psum[:, 7, 0:len(LAYERS)], lhsT=ones[:], rhs=sums[:], start=True, stop=True
                             ).then_inc(edge_mm, 1)

        @block.gpsimd
        def _(pool):
            nc.gpsimd.memset(own[:], 1.0).then_inc(masked, 1)
            pool.wait_ge(masked, 1)
            nc.gpsimd.affine_select(out=own[:], in_=own[:], compare_op=ALU.is_ge, fill=0.0, base=0,
                                    pattern=[[-EDIM, GR]], channel_multiplier=1).then_inc(masked, 1)
            pool.wait_ge(masked, 2)
            nc.gpsimd.affine_select(out=own[:], in_=own[:], compare_op=ALU.is_ge, fill=0.0, base=EDIM - 1,
                                    pattern=[[EDIM, GR]], channel_multiplier=-1).then_inc(masked, 1)

        @block.scalar
        def _(act):
            for j in range(6):
                if j >= 2:
                    act.wait_ge(edge_mm, len(LAYERS) + j - 1)
                act.dma_start(attr[:, j % 2, :, :], t["attr"][:, j * PART:(j + 1) * PART, :]
                             ).then_inc(attr_landed[j % 2], 16)

    as_cl = gb("as_cl", [P, CH])
    score = gb("score", [P, CH])
    self_e = gb("self_e", [P, CH])
    top = gb("top", [P, CH])
    den = gb("den", [P, CH])
    asad = gb("asad", [P, NT, 2])
    node_vals = gb("node_vals", [P, NT, 2])
    self_n = gb("self_n", [P, NT])
    as_parts = gb("as_parts", [P, 3, NT], BF16)
    as_rest = gb("as_rest", [P, NT])

    for l, (din, _) in enumerate(LAYERS):
        inp = xT if l == 0 else acc[:, 0, :]
        b_l = weights[f"b_gat{l}"]

        end_phase()
        mm, dv, ch, stored, ac = phase_sems(f"gat{l}_rows")
        with nc.Block() as block:

            @block.tensor
            def _(pe):
                for k in range(NT):
                    if k >= 7:
                        pe.wait_ge(ac["nodes"], k - 6)
                        pe.wait_ge(dv, k - 6)
                    nc.tensor.matmul(psum[:, k % 7, 0:WIDE + 2], lhsT=inp[0:din, k * P:(k + 1) * P],
                                     rhs=wxx[l][:], start=True, stop=True).then_inc(mm, 1)

            @block.scalar
            def _(act):
                for k in range(NT):
                    act.wait_ge(dv, k + 1)
                    nc.scalar.copy(nodes[:, k, 0:WIDE], psum[:, k % 7, 0:WIDE]).then_inc(ac["nodes"], 1)

            @block.vector
            def _(dve):
                chain = Chain(dve, ch)
                for k in range(NT):
                    dve.wait_ge(mm, k + 1)
                    nc.vector.tensor_copy(asad[:, k, :], psum[:, k % 7, WIDE:WIDE + 2]).then_inc(dv, 1)
                dve.wait_ge(dv, NT)
                chain.link(nc.vector.tensor_copy(node_vals[:, :, 0], asad[:, :, 1]))
                chain.link(nc.vector.scalar_tensor_tensor(self_n[:], asad[:, :, 0], ae_mean[:, l:l + 1],
                                                          asad[:, :, 1], ALU.add, ALU.add))
                nc.vector.scalar_tensor_tensor(node_vals[:, :, 1], self_n[:], SLOPE, self_n[:],
                                               ALU.mult, ALU.max).then_inc(dv, 1)
                chain.link(nc.vector.tensor_copy(as_parts[:, 0, :], asad[:, :, 0]))
                chain.link(nc.vector.tensor_tensor(as_rest[:], asad[:, :, 0], as_parts[:, 0, :], ALU.subtract))
                chain.link(nc.vector.tensor_copy(as_parts[:, 1, :], as_rest[:]))
                chain.link(nc.vector.tensor_tensor(as_parts[:, 2, :], as_rest[:], as_parts[:, 1, :], ALU.subtract))

            @block.sync
            def _(sp):
                sp.wait_ge(ac["nodes"], NT)
                sp.dma_start(h_tab[l].rearrange("(t p) d -> p t d", p=P), nodes[:, :, 0:WIDE]
                             ).then_inc(stored, 16)
                sp.wait_ge(stored, 16)

        end_phase()
        with ExitStack() as stack, nc.Block() as block:
            lo_rep = stack.enter_context(nc.sbuf_tensor(f"lo_rep{l}", [P, 4, HALF * P], BF16))
            lo_hot = stack.enter_context(nc.sbuf_tensor(f"lo_hot{l}", [P, 2, HALF * P], BF16))
            picked = top[:, 0:HALF * NT].rearrange("p (c h) -> p c h", c=HALF)
            lo_landed = [sem(f"gat{l}_lo_landed{k}") for k in range(4)]
            lo_used = sem(f"gat{l}_lo_used")
            table_rows = sem(f"gat{l}_table_rows")
            rows_used = sem(f"gat{l}_rows_used")
            summed = sem(f"gat{l}_summed")
            scattered = sem(f"gat{l}_scattered")
            TIMES = CH // (4 * HALF)

            @block.sync
            def _(sp):
                with sp.Fori(0, TIMES) as i:
                    for k in range(4):
                        sp.wait_ge(lo_used, i * 4 + (k + 1))
                        sp.dma_start(lo_rep[:, k, :], e_lo[bass.ds(i * (4 * HALF * P) + k * HALF * P, HALF * P)]
                                     .partition_broadcast(P)).then_inc(lo_landed[k], 16)

            @block.gpsimd
            def _(pool):
                for k in range(NT):
                    nc.gpsimd.indirect_dma_start(
                        out=e_first, out_offset=bass.IndirectOffsetOnAxis(ap=first_pos[:, k:k + 1], axis=0),
                        in_=node_vals[:, k, :], in_offset=None).then_inc(scattered, 16)
                gather_ahead(l, 0, AHEAD_PICK)
                pool.wait_ge(scattered, 16 * NT)

            @block.vector
            def _(dve):
                dve.sem_inc(lo_used, 4)
                dve.sem_inc(summed, 1)

                def one_hot(k):
                    nc.vector.tensor_scalar(lo_hot[:, k % 2, :], lo_rep[:, k % 4, :], part_id[:], None,
                                            ALU.is_equal).then_inc(lo_used, 1)

                def pick(n, k):
                    dve.wait_ge(table_rows, n * 4 + (k + 1))
                    dve.wait_ge(summed, n * 4 + (k + 1))
                    c = n * (4 * HALF) + k * HALF
                    nc.vector.tensor_tensor(
                        picked, psum[:, k % 2, 0:HALF * NT].rearrange("p (c h) -> p c h", c=HALF),
                        hi_hot[:, bass.ds(c, HALF), :], ALU.mult).then_inc(rows_used, 1)
                    dve.wait_ge(rows_used, n * 4 + (k + 3))
                    nc.vector.tensor_reduce(as_cl[:, bass.ds(c, HALF)], picked, AX, ALU.add
                                            ).then_inc(summed, 1)

                dve.wait_ge(lo_landed[0], 16)
                one_hot(0)
                with dve.Fori(0, TIMES - 1) as i:
                    for k in range(4):
                        dve.wait_ge(lo_landed[(k + 1) % 4], i * 16 + (32 if k == 3 else 16))
                        one_hot(k + 1)
                        pick(i, k)
                for k in range(4):
                    if k < 3:
                        dve.wait_ge(lo_landed[k + 1], 16 * TIMES)
                        one_hot(k + 1)
                    pick(TIMES - 1, k)

            @block.tensor
            def _(pe):
                pe.sem_inc(rows_used, 2)
                with pe.Fori(0, TIMES) as i:
                    for k in range(4):
                        pe.wait_ge(lo_used, i * 4 + (k + 5))
                        pe.wait_ge(rows_used, i * 4 + (k + 1))
                        for c in range(HALF):
                            for part in range(3):
                                last = nc.tensor.matmul(psum[:, k % 2, c * NT:(c + 1) * NT],
                                                        lhsT=lo_hot[:, k % 2, c * P:(c + 1) * P],
                                                        rhs=as_parts[:, part, :],
                                                        start=part == 0, stop=part == 2)
                        last.then_inc(table_rows, 1)

        end_phase()
        mm, dv, ch, stored, ac = phase_sems(f"gat{l}_soft")
        with ExitStack() as stack, nc.Block() as block:
            efirst = stack.enter_context(nc.sbuf_tensor(f"efirst{l}", [P, CH, 2], F32))
            by_chunk = stack.enter_context(nc.sbuf_tensor(f"by_chunk{l}", [P, len(GROUPS), P], F32))
            as_landed = sem(f"gat{l}_as_landed")
            first_landed = sem(f"gat{l}_first_landed")
            coef_landed = sem(f"gat{l}_coef_landed")
            exped = sem(f"gat{l}_exped")

            def chunk_rows(array):
                return [(g // P, n, array[g * P:(g + n) * P].rearrange("(c e) -> c e", e=P))
                        for g, n in GROUPS]

            @block.tensor
            def _(pe):
                for g, n in GROUPS:
                    nc.tensor.transpose(psum[0:n, g // P, 0:P], as_cl[:, g:g + n], ident[:]).then_inc(mm, 1)
                for s in range(6):
                    prefix_pe(pe, scan_sems, 2 + 6 * l + s)
                pe.wait_ge(coef_landed, 16 * len(GROUPS))
                for g, n in GROUPS:
                    nc.tensor.transpose(psum[:, g // P, 0:n], by_chunk[0:n, g // P, :], ident[0:n, 0:n]
                                        ).then_inc(mm, 1)

            @block.sync
            def _(sp):
                sp.dma_start(efirst[:].rearrange("p n two -> p (n two)"),
                             e_first[0:EP, :].rearrange("(p n) two -> p (n two)", p=P)
                             ).then_inc(first_landed, 16)
                sp.wait_ge(dv, len(GROUPS))
                for g, n, rows_ in chunk_rows(e_as):
                    sp.dma_start(rows_, by_chunk[0:n, g, :]).then_inc(stored, 16)
                sp.wait_ge(stored, 16 * len(GROUPS))
                sp.dma_start(score[:], e_as.rearrange("(p n) -> p n", p=P)).then_inc(as_landed, 16)
                sp.wait_ge(dv, len(GROUPS) + 2)
                sp.dma_start(e_coef.rearrange("(p n) -> p n", p=P), score[:]).then_inc(stored, 16)
                sp.wait_ge(stored, 16 * (len(GROUPS) + 1))
                for g, n, rows_ in chunk_rows(e_coef):
                    sp.dma_start(by_chunk[0:n, g, :], rows_).then_inc(coef_landed, 16)

            @block.gpsimd
            def _(pool):
                gather_ahead(l, AHEAD_PICK, AHEAD_SOFT)

            @block.scalar
            def _(act):
                act.wait_ge(dv, len(GROUPS) + 1)
                nc.scalar.activation(score[:], score[:], ACT.Exp).then_inc(exped, 1)
                nc.scalar.activation(self_e[:], self_e[:], ACT.Exp).then_inc(exped, 1)

            @block.vector
            def _(dve):
                chain = Chain(dve, ch)
                for g, n in GROUPS:
                    dve.wait_ge(mm, g // P + 1)
                    nc.vector.tensor_copy(by_chunk[0:n, g // P, :], psum[0:n, g // P, 0:P]).then_inc(dv, 1)
                nc.vector.memset(acc[0:WIDE, 0, :], 0.0)
                dve.wait_ge(first_landed, 16)
                prefix_dve(dve, scan_sems, 6 * l + 2, chain, den, same, efirst[:, :, 0])
                prefix_dve(dve, scan_sems, 6 * l + 3, chain, self_e, same, efirst[:, :, 1])
                dve.wait_ge(as_landed, 16)
                chain.link(nc.vector.tensor_tensor(den[:], den[:], ae[l][:], ALU.add))
                chain.link(nc.vector.tensor_tensor(score[:], score[:], den[:], ALU.add))
                chain.link(nc.vector.scalar_tensor_tensor(score[:], score[:], SLOPE, score[:],
                                                          ALU.mult, ALU.max))
                chain.link(nc.vector.tensor_tensor(den[:], score[:], self_e[:], ALU.max))
                prefix_dve(dve, scan_sems, 6 * l + 4, chain, top, pen, den, largest=True)
                prefix_dve(dve, scan_sems, 6 * l + 5, chain, den, pen_next, top, back=True, largest=True)
                chain.link(nc.vector.tensor_tensor(score[:], score[:], den[:], ALU.subtract))
                nc.vector.tensor_tensor(self_e[:], self_e[:], den[:], ALU.subtract).then_inc(dv, 1)
                dve.wait_ge(exped, 2)
                prefix_dve(dve, scan_sems, 6 * l + 6, chain, top, same, score)
                chain.link(nc.vector.tensor_tensor(top[:], top[:], last_of[:], ALU.mult))
                prefix_dve(dve, scan_sems, 6 * l + 7, chain, den, same_next, top, back=True)
                chain.link(nc.vector.tensor_tensor(den[:], den[:], self_e[:], ALU.add))
                chain.link(nc.vector.reciprocal(den[:], den[:]))
                chain.link(nc.vector.tensor_tensor(self_e[:], self_e[:], loop_share[:], ALU.mult))
                chain.link(nc.vector.tensor_tensor(score[:], score[:], self_e[:], ALU.add))
                nc.vector.tensor_tensor(score[:], score[:], den[:], ALU.mult).then_inc(dv, 1)
                for g, n in GROUPS:
                    dve.wait_ge(mm, len(GROUPS) + g // P + 1)
                    nc.vector.tensor_copy(scale[:, g:g + n], psum[:, g // P, 0:n]).then_inc(dv, 1)

        neighbour_sums(l, acc)

        if l < len(LAYERS) - 1:
            relu_done = sem(f"gat{l}_relu")
            with nc.Block() as block:

                @block.vector
                def _(dve):
                    nc.vector.tensor_scalar(acc[0:WIDE, 0, 0:NP], acc[0:WIDE, 0, 0:NP], b_l[:], 0.0,
                                            ALU.add, ALU.max).then_inc(relu_done, 1)


    gat.close()
    w1, w2, w3 = (sb(f"last_w{k}", [P, NP]) for k in (1, 2, 3))
    end_phase()
    mm, dv, ch, stored, ac = phase_sems("last")
    with nc.Block() as block:

        @block.tensor
        def _(pe):
            for b, (lo, n) in enumerate(BLOCKS):
                nc.tensor.matmul(psum[:, b, 0:n], lhsT=weights["w_gat2"][:], rhs=acc[0:WIDE, 0, lo:lo + n],
                                 start=True, stop=True).then_inc(mm, 1)
            norm_pe(pe, mm, dv, ac, 1, 0, w2, w3)

        @block.vector
        def _(dve):
            chain = Chain(dve, ch)
            for b, (lo, n) in enumerate(BLOCKS):
                s = slice(lo, lo + n)
                dve.wait_ge(mm, ev(0, b))
                chain.link(nc.vector.scalar_tensor_tensor(w2[:, s], psum[:, b, 0:n], b_l[:], xT[:, s],
                                                          ALU.add, ALU.add))
                nc.vector.tensor_tensor(w2[:, s], w2[:, s], xT[:, s], ALU.add).then_inc(dv, 1)
            norm_dve(dve, mm, dv, ac, 1, chain, w2, w3)

        @block.scalar
        def _(act):
            norm_act(act, mm, dv, ac, 1, 0, w3)

        @block.sync
        def _(sp):
            sp.wait_ge(ac["nodes"], NB)
            full = N // P
            sp.dma_start(out[0:full * P, :].rearrange("(t p) d -> p t d", p=P), nodes[:, 0:full, :]
                         ).then_inc(stored, 16)
            sp.dma_start(out[full * P:N, :], nodes[0:N - full * P, full, :]).then_inc(stored, 16)
            sp.wait_ge(stored, 32)


def kernel(**inputs):
    import numpy as np
    import concourse.bacc as bacc
    from concourse.bass_utils import run_bass_kernel_spmd

    i = {k: np.asarray(v) for k, v in inputs.items()}
    src = np.concatenate([i["src"], np.zeros(EP - E, np.int32)])
    pad = np.full(EP - E, N, np.int32)
    dst = np.concatenate([i["dst"], pad])
    arrays = {
        "x": i["x"], "xT": i["x"].T,
        "src_cl": src.reshape(CH, P).T, "dst_cl": dst.reshape(CH, P).T,
        "base": dst[::P], "quad_base": dst[::4 * P], "quad_last": dst[4 * P - 1::4 * P],
        "src_sl": src.reshape(P, CH), "dst_sl": dst.reshape(P, CH),
        "dst_before": np.concatenate([np.full(1, -1, np.int32), dst[:-1]]).reshape(P, CH),
        "dst_after": np.concatenate([dst[1:], np.full(1, -1, np.int32)]).reshape(P, CH),
        "attr": np.concatenate([i["edge_attr_16"], np.zeros((EP - E, EDIM), np.float32)]).reshape(
            P, CH * EDIM // P, P).transpose(2, 1, 0),
        "w_src": i["L0_gnn_W_src"].T, "b_src": i["L0_gnn_b_src"][:, None],
        "w_fc": i["L0_gnn_W_fc"].T.reshape(2, D, D).transpose(1, 0, 2).reshape(D, 2 * D),
        "b_fc": i["L0_gnn_b_fc"][:, None],
        "w_in": i["L1_gnn_W_in"].T, "b_in": i["L1_gnn_b_in"][:, None],
        "w_out": i["L1_gnn_W_out"].T, "b_out": i["L1_gnn_b_out"][:, None],
        "w_ih": i["L1_gnn_w_ih"].T.reshape(2, D, 3 * D).transpose(1, 0, 2),
        "w_hh": i["L1_gnn_w_hh"].T,
        "b_ih": i["L1_gnn_b_ih"].reshape(3, D).T, "b_hh": i["L1_gnn_b_hh"].reshape(3, D).T,
        "w_gcn": i["L2_gnn_weight"], "b_gcn": i["L2_gnn_bias"][:, None],
    }
    for l in range(len(LAYERS)):
        arrays[f"w_gat{l}"] = i[f"L3_gnn_W{l + 1}"]
        arrays[f"w_gatT{l}"] = i[f"L3_gnn_W{l + 1}"].T
        arrays[f"w_a{l}"] = np.stack([i[f"L3_gnn_as{l + 1}"], i[f"L3_gnn_ad{l + 1}"]], 1)
        arrays[f"w_eT{l}"] = i[f"L3_gnn_We{l + 1}"].T
        arrays[f"w_ae{l}"] = i[f"L3_gnn_ae{l + 1}"][:, None]
        arrays[f"b_gat{l}"] = i[f"L3_gnn_b{l + 1}"][:, None]
    arrays = {k: np.ascontiguousarray(v) for k, v in arrays.items()}

    nc = bacc.Bacc("TRN2", target_bir_lowering=False, num_devices=1)
    aps = {k: nc.dram_tensor("in_" + k, v.shape, mybir.dt.from_np(v.dtype), kind="ExternalInput").ap()
           for k, v in arrays.items()}
    out = nc.dram_tensor("out", (N, D), F32, kind="ExternalOutput").ap()
    gnn_kernel(nc, aps, out)
    r = run_bass_kernel_spmd(nc, [{"in_" + k: v for k, v in arrays.items()}], core_ids=[0])
    return r.results[0]["out"]
```
